# Optimizing a Trainium2 kernel written in Bass

```python
import numpy as np
import jax
import jax.numpy as jnp

def _softmax(x, axis=-1):
    return jax.nn.softmax(x, axis=axis)

def _gelu(x):
    return jax.nn.gelu(x, approximate=True)

def _silu(x):
    return jax.nn.silu(x)

def _sigmoid(x):
    return jax.nn.sigmoid(x)

def _layernorm(x, axis=-1, eps=1e-05):
    m = jnp.mean(x, axis=axis, keepdims=True)
    v = jnp.var(x, axis=axis, keepdims=True)
    return (x - m) / jnp.sqrt(v + eps)

def _scatter_add(tgt, idx, src, axis=0):
    return tgt.at[idx].add(src)

def _segment_sum(src, seg, n):
    return jax.ops.segment_sum(src, seg, n)
kernel_name = 'mk_decoder_postln_d2_seqx_r8_aa3bfd'

def setup_inputs(seed: int=0):
    np.random.seed(seed)
    _w = jnp.asarray

    def _rec_inputs():
        import jax
        import jax.numpy as jnp
        _rk = jax.random.key(seed)
        x = -0.0003929 + 0.9999 * jax.random.normal(jax.random.fold_in(_rk, 1), (16, 64, 512), jnp.float32)
        _lenS = 64 - jax.random.randint(jax.random.fold_in(_rk, 7), (16,), 0, max(1, 64 // 4) + 1, jnp.int32)
        _lenS2 = 64 - jax.random.randint(jax.random.fold_in(_rk, 8), (16,), 0, max(1, 64 // 4) + 1, jnp.int32)
        _ctx_4096P = jax.random.normal(jax.random.fold_in(_rk, 11), (16, 16, 512), jnp.float32)
        _ctx_4096c = jax.random.dirichlet(jax.random.fold_in(_rk, 511), 0.3 * jnp.ones((16,), jnp.float32), (16, 64))
        _ctx_4096t = jnp.einsum('bsk,bkd->bsd', _ctx_4096c, _ctx_4096P)
        _ctx_4096t = _ctx_4096t * jax.lax.rsqrt(jnp.mean(jnp.square(_ctx_4096t)) + 1e-12) * 0.953939
        ctx_4096 = 2.81802e-05 + 1.00001 * (_ctx_4096t + 0.3 * jax.random.normal(jax.random.fold_in(_rk, 611), (16, 64, 512), jnp.float32))
        pos_BxS2 = jnp.broadcast_to(jnp.arange(64, dtype=jnp.int32), (16, 64))
        _validS = jnp.arange(64)[None, :] < _lenS[:, None]
        _validS2 = jnp.arange(64)[None, :] < _lenS2[:, None]
        _causal = jnp.tril(jnp.ones((64, 64), dtype=bool))
        mask_BxSxS2_ik0 = jnp.where(jnp.broadcast_to(_validS2[:, None, :], (16, 64, 64)), 0, 1).astype(jnp.int32)
        return (x, ctx_4096, pos_BxS2, mask_BxSxS2_ik0)
    x, ctx_4096, pos_BxS2, mask_BxSxS2_ik0 = _rec_inputs()

    def _L0_attn_setup():
        import jax, jax.numpy as jnp
        import numpy as np
        import math
        HIDDEN = 512
        NUM_HEADS = 32
        HEAD_DIM = HIDDEN // NUM_HEADS
        SCALE = 1.0 / HEAD_DIM

        def _alibi_slopes(n_heads: int) -> np.ndarray:
            cp2 = 2 ** math.floor(math.log2(n_heads))
            base = 2 ** (-2 ** (-(math.log2(cp2) - 3)))
            slopes = base ** np.arange(1, cp2 + 1, dtype=np.float32)
            if cp2 != n_heads:
                extra_base = 2 ** (-2 ** (-(math.log2(2 * cp2) - 3)))
                n_rem = min(cp2, n_heads - cp2)
                extra = extra_base ** np.arange(1, 1 + 2 * n_rem, 2, dtype=np.float32)
                slopes = np.concatenate([slopes, extra])
            return slopes.astype(np.float32)
        key = jax.random.key(seed)
        k1, k2, k3, k4, k5 = jax.random.split(key, 5)
        B, S = (2, 256)
        return {'hidden_states': jax.random.normal(k1, (B, S, HIDDEN), dtype=jnp.float32), 'w_attn': jax.random.normal(k2, (HIDDEN, 3 * HIDDEN), dtype=jnp.float32) * 0.02, 'b_attn': jnp.zeros((3 * HIDDEN,), dtype=jnp.float32), 'w_proj': jax.random.normal(k3, (HIDDEN, HIDDEN), dtype=jnp.float32) * 0.02, 'b_proj': jnp.zeros((HIDDEN,), dtype=jnp.float32)}
    _L0_attn_all = _L0_attn_setup()
    _L0_attn_in = {k: v for k, v in _L0_attn_all.items() if k in ('w_attn', 'b_attn', 'w_proj', 'b_proj')}
    del _L0_attn_all

    def _L0_xattn_setup():
        import jax, jax.numpy as jnp
        import numpy as np
        B, S, E = (2, 256, 512)
        H, KVH, D = (32, 8, 128)
        GROUPS = H // KVH
        MAX_POS = 512
        ROPE_THETA = 10000.0

        def _rope_tables(max_pos, dim, theta):
            inv_freq = 1.0 / theta ** (jnp.arange(0, dim, 2, dtype=jnp.float32) / dim)
            t = jnp.arange(max_pos, dtype=jnp.float32)
            freqs = jnp.einsum('i,j->ij', t, inv_freq)
            emb = jnp.concatenate([freqs, freqs], axis=-1)
            return (jnp.cos(emb), jnp.sin(emb))

        def _rotate_half(x):
            x1, x2 = (x[..., :x.shape[-1] // 2], x[..., x.shape[-1] // 2:])
            return jnp.concatenate([-x2, x1], axis=-1)
        key = jax.random.key(seed)
        ks = jax.random.split(key, 8)
        scale_w = 1.0 / np.sqrt(E)
        query = jax.random.normal(ks[0], (B, S, E), dtype=jnp.float32)
        k_in = jax.random.normal(ks[1], (B, S, E), dtype=jnp.float32)
        v_in = jax.random.normal(ks[2], (B, S, E), dtype=jnp.float32)
        position_ids = jnp.broadcast_to(jnp.arange(S, dtype=jnp.int64), (B, S))
        src_mask = jnp.tril(jnp.ones((S, S), dtype=jnp.int32))
        src_mask = jnp.broadcast_to(src_mask, (B, S, S))
        Wq = jax.random.normal(ks[3], (E, H * D), dtype=jnp.float32) * scale_w
        Wk = jax.random.normal(ks[4], (E, KVH * D), dtype=jnp.float32) * scale_w
        Wv = jax.random.normal(ks[5], (E, KVH * D), dtype=jnp.float32) * scale_w
        Wo = jax.random.normal(ks[6], (H * D, E), dtype=jnp.float32) * scale_w
        return {'query': query, 'key': k_in, 'value': v_in, 'position_ids': position_ids, 'src_mask': src_mask, 'Wq': Wq, 'Wk': Wk, 'Wv': Wv, 'Wo': Wo}
    _L0_xattn_all = _L0_xattn_setup()
    _L0_xattn_in = {k: v for k, v in _L0_xattn_all.items() if k in ('Wq', 'Wk', 'Wv', 'Wo')}
    del _L0_xattn_all

    def _L0_ffn_setup():
        import jax, jax.numpy as jnp
        import numpy as np
        R = 16
        ALPHA = 32
        SCALING = ALPHA / R
        E = 8
        TOP_K = 2
        key = jax.random.key(seed)
        ks = jax.random.split(key, 5)
        B, S, D = (4, 256, 512)
        x = jax.random.normal(ks[0], (B, S, D), dtype=jnp.float32)
        base_W = jax.random.normal(ks[1], (D, D), dtype=jnp.float32) * 0.02
        router_W = jax.random.normal(ks[2], (E, D), dtype=jnp.float32) * 0.02
        lora_A = jax.random.normal(ks[3], (E, D, R), dtype=jnp.float32) * 0.02
        lora_B = jax.random.normal(ks[4], (E, R, D), dtype=jnp.float32) * 0.02
        return {'x': x, 'base_W': base_W, 'router_W': router_W, 'lora_A': lora_A, 'lora_B': lora_B}
    _L0_ffn_all = _L0_ffn_setup()
    _L0_ffn_in = {k: v for k, v in _L0_ffn_all.items() if k in ('base_W', 'router_W', 'lora_A', 'lora_B')}
    del _L0_ffn_all

    def _L1_attn_setup():
        import jax, jax.numpy as jnp
        import numpy as np
        D_MODEL = 512
        N_Q = 32
        N_KV = 8
        HD = 128
        SLIDE = 64

        def _gqa_swa_attention(q, k, v, slide):
            B, Hq, N, D = q.shape
            Hkv = k.shape[1]
            G = Hq // Hkv
            qg = q.reshape(B, Hkv, G, N, D)
            scale = 1.0 / jnp.sqrt(jnp.asarray(D, q.dtype))
            s = jnp.einsum('bhgnd,bhmd->bhgnm', qg, k) * scale
            i = jnp.arange(N)[:, None]
            j = jnp.arange(N)[None, :]
            mask = j <= i
            if slide > 0:
                mask = mask & (i - j < slide)
            s = jnp.where(mask[None, None, None], s, jnp.asarray(-jnp.inf, s.dtype))
            p = jax.nn.softmax(s, axis=-1)
            o = jnp.einsum('bhgnm,bhmd->bhgnd', p, v)
            return o.reshape(B, Hq, N, D)
        key = jax.random.key(seed)
        ks = jax.random.split(key, 5)
        std = 0.01
        x = jax.random.normal(ks[0], (2, 256, D_MODEL), dtype=jnp.float32)
        wq = jax.random.normal(ks[1], (N_Q * HD, D_MODEL), dtype=jnp.float32) * std
        wk = jax.random.normal(ks[2], (N_KV * HD, D_MODEL), dtype=jnp.float32) * std
        wv = jax.random.normal(ks[3], (N_KV * HD, D_MODEL), dtype=jnp.float32) * std
        wo = jax.random.normal(ks[4], (D_MODEL, N_Q * HD), dtype=jnp.float32) * std
        return {'x': x, 'wq': wq, 'wk': wk, 'wv': wv, 'wo': wo}
    _L1_attn_all = _L1_attn_setup()
    _L1_attn_in = {k: v for k, v in _L1_attn_all.items() if k in ('wq', 'wk', 'wv', 'wo')}
    del _L1_attn_all

    def _L1_xattn_setup():
        import jax, jax.numpy as jnp
        import numpy as np
        TEXT_DIM = 512
        FEATURE_DIM = 512

        def _xavier_uniform(key, shape):
            fan_in, fan_out = (shape[1], shape[0])
            limit = float(np.sqrt(6.0 / (fan_in + fan_out)))
            return jax.random.uniform(key, shape, jnp.float32, -limit, limit)
        key = jax.random.key(seed)
        k1, k2, k3, k4 = jax.random.split(key, 4)
        text = jax.random.normal(k1, (8, 256, TEXT_DIM), jnp.float32)
        features = jax.random.normal(k2, (8, 72, FEATURE_DIM), jnp.float32)
        Wq = _xavier_uniform(k3, (FEATURE_DIM, TEXT_DIM))
        bq = jnp.zeros((FEATURE_DIM,), jnp.float32)
        Wk = _xavier_uniform(k4, (FEATURE_DIM, FEATURE_DIM))
        bk = jnp.zeros((FEATURE_DIM,), jnp.float32)
        return {'text': text, 'features': features, 'Wq': Wq, 'bq': bq, 'Wk': Wk, 'bk': bk}
    _L1_xattn_all = _L1_xattn_setup()
    _L1_xattn_in = {k: v for k, v in _L1_xattn_all.items() if k in ('Wq', 'bq', 'Wk', 'bk')}
    del _L1_xattn_all

    def _L1_ffn_setup():
        import jax, jax.numpy as jnp
        import numpy as np
        H = 512
        I = 1376
        R = 32
        NLEV = 16
        Q_ZERO = 7.5
        Q_STEP = 0.005
        LR_SCALE = 0.02

        def _qlinear(x, q, scale, A, Bm):
            w = (q.astype(jnp.float32) - Q_ZERO) * (scale * Q_STEP)[:, None]
            y = jnp.einsum('bsh,oh->bso', x, w)
            return y + LR_SCALE * (x @ A @ Bm)
        key = jax.random.key(seed)
        ks = jax.random.split(key, 13)
        B, S = (2, 256)
        inp = {'x': jax.random.normal(ks[0], (B, S, H), jnp.float32), 'gate_q': jax.random.randint(ks[1], (I, H), 0, NLEV, jnp.int32), 'gate_scale': jax.random.uniform(ks[2], (I,), jnp.float32), 'gate_A': jax.random.normal(ks[3], (H, R), jnp.float32), 'gate_B': jax.random.normal(ks[4], (R, I), jnp.float32), 'up_q': jax.random.randint(ks[5], (I, H), 0, NLEV, jnp.int32), 'up_scale': jax.random.uniform(ks[6], (I,), jnp.float32), 'up_A': jax.random.normal(ks[7], (H, R), jnp.float32), 'up_B': jax.random.normal(ks[8], (R, I), jnp.float32), 'down_q': jax.random.randint(ks[9], (H, I), 0, NLEV, jnp.int32), 'down_scale': jax.random.uniform(ks[10], (H,), jnp.float32), 'down_A': jax.random.normal(ks[11], (I, R), jnp.float32), 'down_B': jax.random.normal(ks[12], (R, H), jnp.float32)}
        return inp
    _L1_ffn_all = _L1_ffn_setup()
    _L1_ffn_in = {k: v for k, v in _L1_ffn_all.items() if k in ('gate_q', 'gate_scale', 'gate_A', 'gate_B', 'up_q', 'up_scale', 'up_A', 'up_B', 'down_q', 'down_scale', 'down_A', 'down_B')}
    del _L1_ffn_all
    return {'x': x, 'ctx_4096': ctx_4096, 'pos_BxS2': pos_BxS2, 'mask_BxSxS2_ik0': mask_BxSxS2_ik0, 'L0_attn_w_attn': _L0_attn_in['w_attn'], 'L0_attn_b_attn': _L0_attn_in['b_attn'], 'L0_attn_w_proj': _L0_attn_in['w_proj'], 'L0_attn_b_proj': _L0_attn_in['b_proj'], 'L0_xattn_Wq': _L0_xattn_in['Wq'], 'L0_xattn_Wk': _L0_xattn_in['Wk'], 'L0_xattn_Wv': _L0_xattn_in['Wv'], 'L0_xattn_Wo': _L0_xattn_in['Wo'], 'L0_ffn_base_W': _L0_ffn_in['base_W'], 'L0_ffn_router_W': _L0_ffn_in['router_W'], 'L0_ffn_lora_A': _L0_ffn_in['lora_A'], 'L0_ffn_lora_B': _L0_ffn_in['lora_B'], 'L1_attn_wq': _L1_attn_in['wq'], 'L1_attn_wk': _L1_attn_in['wk'], 'L1_attn_wv': _L1_attn_in['wv'], 'L1_attn_wo': _L1_attn_in['wo'], 'L1_xattn_Wq': _L1_xattn_in['Wq'], 'L1_xattn_bq': _L1_xattn_in['bq'], 'L1_xattn_Wk': _L1_xattn_in['Wk'], 'L1_xattn_bk': _L1_xattn_in['bk'], 'L1_ffn_gate_q': _L1_ffn_in['gate_q'], 'L1_ffn_gate_scale': _L1_ffn_in['gate_scale'], 'L1_ffn_gate_A': _L1_ffn_in['gate_A'], 'L1_ffn_gate_B': _L1_ffn_in['gate_B'], 'L1_ffn_up_q': _L1_ffn_in['up_q'], 'L1_ffn_up_scale': _L1_ffn_in['up_scale'], 'L1_ffn_up_A': _L1_ffn_in['up_A'], 'L1_ffn_up_B': _L1_ffn_in['up_B'], 'L1_ffn_down_q': _L1_ffn_in['down_q'], 'L1_ffn_down_scale': _L1_ffn_in['down_scale'], 'L1_ffn_down_A': _L1_ffn_in['down_A'], 'L1_ffn_down_B': _L1_ffn_in['down_B']}

def reference(x, ctx_4096, pos_BxS2, mask_BxSxS2_ik0, L0_attn_w_attn, L0_attn_b_attn, L0_attn_w_proj, L0_attn_b_proj, L0_xattn_Wq, L0_xattn_Wk, L0_xattn_Wv, L0_xattn_Wo, L0_ffn_base_W, L0_ffn_router_W, L0_ffn_lora_A, L0_ffn_lora_B, L1_attn_wq, L1_attn_wk, L1_attn_wv, L1_attn_wo, L1_xattn_Wq, L1_xattn_bq, L1_xattn_Wk, L1_xattn_bk, L1_ffn_gate_q, L1_ffn_gate_scale, L1_ffn_gate_A, L1_ffn_gate_B, L1_ffn_up_q, L1_ffn_up_scale, L1_ffn_up_A, L1_ffn_up_B, L1_ffn_down_q, L1_ffn_down_scale, L1_ffn_down_A, L1_ffn_down_B):
    import jax
    import jax.numpy as jnp

    def _L0_attn_ref(hidden_states, w_attn, b_attn, w_proj, b_proj):
        import jax, jax.numpy as jnp
        import numpy as np
        import math
        HIDDEN = 512
        NUM_HEADS = 32
        HEAD_DIM = HIDDEN // NUM_HEADS
        SCALE = 1.0 / HEAD_DIM

        def _alibi_slopes(n_heads: int) -> np.ndarray:
            cp2 = 2 ** math.floor(math.log2(n_heads))
            base = 2 ** (-2 ** (-(math.log2(cp2) - 3)))
            slopes = base ** np.arange(1, cp2 + 1, dtype=np.float32)
            if cp2 != n_heads:
                extra_base = 2 ** (-2 ** (-(math.log2(2 * cp2) - 3)))
                n_rem = min(cp2, n_heads - cp2)
                extra = extra_base ** np.arange(1, 1 + 2 * n_rem, 2, dtype=np.float32)
                slopes = np.concatenate([slopes, extra])
            return slopes.astype(np.float32)
        B, S, _ = hidden_states.shape
        H, D = (NUM_HEADS, HEAD_DIM)
        qkv = hidden_states @ w_attn + b_attn
        q, k, v = jnp.split(qkv, 3, axis=-1)
        q = q.reshape(B, S, H, D)
        k = k.reshape(B, S, H, D)
        v = v.reshape(B, S, H, D)
        scores = jnp.einsum('bqhd,bkhd->bhqk', q, k) * SCALE
        slopes = jnp.asarray(_alibi_slopes(H))
        pos = jnp.arange(S)
        rel = pos[None, :] - pos[:, None]
        bias = slopes[:, None, None] * rel[None, :, :]
        causal = rel <= 0
        scores = jnp.where(causal[None, None], scores + bias[None], -jnp.inf)
        attn = jax.nn.softmax(scores, axis=-1)
        out = jnp.einsum('bhqk,bkhd->bqhd', attn, v).reshape(B, S, HIDDEN)
        return out @ w_proj + b_proj

    def _L0_xattn_ref(query, key, value, position_ids, src_mask, Wq, Wk, Wv, Wo):
        import jax, jax.numpy as jnp
        import numpy as np
        B, S, E = (2, 256, 512)
        H, KVH, D = (32, 8, 128)
        GROUPS = H // KVH
        MAX_POS = 512
        ROPE_THETA = 10000.0

        def _rope_tables(max_pos, dim, theta):
            inv_freq = 1.0 / theta ** (jnp.arange(0, dim, 2, dtype=jnp.float32) / dim)
            t = jnp.arange(max_pos, dtype=jnp.float32)
            freqs = jnp.einsum('i,j->ij', t, inv_freq)
            emb = jnp.concatenate([freqs, freqs], axis=-1)
            return (jnp.cos(emb), jnp.sin(emb))

        def _rotate_half(x):
            x1, x2 = (x[..., :x.shape[-1] // 2], x[..., x.shape[-1] // 2:])
            return jnp.concatenate([-x2, x1], axis=-1)
        nb, q_len, _ = query.shape
        q = (query @ Wq).reshape(nb, q_len, H, D).transpose(0, 2, 1, 3)
        k = (key @ Wk).reshape(nb, q_len, KVH, D).transpose(0, 2, 1, 3)
        v = (value @ Wv).reshape(nb, q_len, KVH, D).transpose(0, 2, 1, 3)
        cos_t, sin_t = _rope_tables(MAX_POS, D, ROPE_THETA)
        cos = cos_t[position_ids][:, None]
        sin = sin_t[position_ids][:, None]
        q = q * cos + _rotate_half(q) * sin
        k = k * cos + _rotate_half(k) * sin
        k = jnp.repeat(k, GROUPS, axis=1)
        v = jnp.repeat(v, GROUPS, axis=1)
        scores = jnp.einsum('bhqd,bhkd->bhqk', q, k) / jnp.sqrt(jnp.float32(D))
        mask = src_mask[:, None]
        scores = jnp.where(mask == 0, jnp.float32(-1000000000.0), scores)
        attn = jax.nn.softmax(scores, axis=-1)
        x = jnp.einsum('bhqk,bhkd->bhqd', attn, v)
        x = x.transpose(0, 2, 1, 3).reshape(nb, q_len, H * D)
        return x @ Wo

    def _L0_ffn_ref(x, base_W, router_W, lora_A, lora_B):
        import jax, jax.numpy as jnp
        import numpy as np
        R = 16
        ALPHA = 32
        SCALING = ALPHA / R
        E = 8
        TOP_K = 2
        base = jnp.einsum('bsd,od->bso', x, base_W)
        logits = jnp.einsum('bsd,ed->bse', x, router_W)
        probs = jax.nn.softmax(logits.astype(jnp.float32), axis=-1)
        top_vals, top_idx = jax.lax.top_k(probs, TOP_K)
        rw = top_vals / jnp.sum(top_vals, axis=-1, keepdims=True)
        w_dense = jnp.sum(jax.nn.one_hot(top_idx, E, dtype=rw.dtype) * rw[..., None], axis=-2).astype(x.dtype)
        mid = jnp.einsum('bsd,edr->bser', x, lora_A)
        mid = mid * w_dense[..., None]
        inc = jnp.einsum('bser,erd->bsd', mid, lora_B)
        return base + inc * SCALING

    def _L1_attn_ref(x, wq, wk, wv, wo):
        import jax, jax.numpy as jnp
        import numpy as np
        D_MODEL = 512
        N_Q = 32
        N_KV = 8
        HD = 128
        SLIDE = 64

        def _gqa_swa_attention(q, k, v, slide):
            B, Hq, N, D = q.shape
            Hkv = k.shape[1]
            G = Hq // Hkv
            qg = q.reshape(B, Hkv, G, N, D)
            scale = 1.0 / jnp.sqrt(jnp.asarray(D, q.dtype))
            s = jnp.einsum('bhgnd,bhmd->bhgnm', qg, k) * scale
            i = jnp.arange(N)[:, None]
            j = jnp.arange(N)[None, :]
            mask = j <= i
            if slide > 0:
                mask = mask & (i - j < slide)
            s = jnp.where(mask[None, None, None], s, jnp.asarray(-jnp.inf, s.dtype))
            p = jax.nn.softmax(s, axis=-1)
            o = jnp.einsum('bhgnm,bhmd->bhgnd', p, v)
            return o.reshape(B, Hq, N, D)
        B, N, _ = x.shape
        q = (x @ wq.T).reshape(B, N, N_Q, HD).transpose(0, 2, 1, 3)
        k = (x @ wk.T).reshape(B, N, N_KV, HD).transpose(0, 2, 1, 3)
        v = (x @ wv.T).reshape(B, N, N_KV, HD).transpose(0, 2, 1, 3)
        o = _gqa_swa_attention(q, k, v, SLIDE)
        o = o.transpose(0, 2, 1, 3).reshape(B, N, N_Q * HD)
        return o @ wo.T

    def _L1_xattn_ref(text, features, Wq, bq, Wk, bk):
        import jax, jax.numpy as jnp
        import numpy as np
        TEXT_DIM = 512
        FEATURE_DIM = 512

        def _xavier_uniform(key, shape):
            fan_in, fan_out = (shape[1], shape[0])
            limit = float(np.sqrt(6.0 / (fan_in + fan_out)))
            return jax.random.uniform(key, shape, jnp.float32, -limit, limit)
        Q = jnp.einsum('btx,dx->btd', text, Wq) + bq
        K = jnp.einsum('bpx,dx->bpd', features, Wk) + bk
        scale = 1.0 / jnp.sqrt(jnp.asarray(K.shape[-1], K.dtype))
        scores = jnp.einsum('btd,bpd->btp', Q, K) * scale
        attn = jax.nn.softmax(scores, axis=-1)
        attended = jnp.einsum('btp,bpd->btd', attn, features)
        return attended

    def _L1_ffn_ref(x, gate_q, gate_scale, gate_A, gate_B, up_q, up_scale, up_A, up_B, down_q, down_scale, down_A, down_B):
        import jax, jax.numpy as jnp
        import numpy as np
        H = 512
        I = 1376
        R = 32
        NLEV = 16
        Q_ZERO = 7.5
        Q_STEP = 0.005
        LR_SCALE = 0.02

        def _qlinear(x, q, scale, A, Bm):
            w = (q.astype(jnp.float32) - Q_ZERO) * (scale * Q_STEP)[:, None]
            y = jnp.einsum('bsh,oh->bso', x, w)
            return y + LR_SCALE * (x @ A @ Bm)
        g = _qlinear(x, gate_q, gate_scale, gate_A, gate_B)
        u = _qlinear(x, up_q, up_scale, up_A, up_B)
        h = jax.nn.silu(g) * u
        return _qlinear(h, down_q, down_scale, down_A, down_B)
    x = _layernorm(x + _L0_attn_ref(x, L0_attn_w_attn, L0_attn_b_attn, L0_attn_w_proj, L0_attn_b_proj), axis=-1)
    x = _layernorm(x + _L0_xattn_ref(x, ctx_4096, ctx_4096, pos_BxS2, mask_BxSxS2_ik0, L0_xattn_Wq, L0_xattn_Wk, L0_xattn_Wv, L0_xattn_Wo), axis=-1)
    x = _layernorm(x + _L0_ffn_ref(x, L0_ffn_base_W, L0_ffn_router_W, L0_ffn_lora_A, L0_ffn_lora_B), axis=-1)
    x = _layernorm(x + _L1_attn_ref(x, L1_attn_wq, L1_attn_wk, L1_attn_wv, L1_attn_wo), axis=-1)
    x = _layernorm(x + _L1_xattn_ref(x, ctx_4096, L1_xattn_Wq, L1_xattn_bq, L1_xattn_Wk, L1_xattn_bk), axis=-1)
    x = _layernorm(x + _L1_ffn_ref(x, L1_ffn_gate_q, L1_ffn_gate_scale, L1_ffn_gate_A, L1_ffn_gate_B, L1_ffn_up_q, L1_ffn_up_scale, L1_ffn_up_A, L1_ffn_up_B, L1_ffn_down_q, L1_ffn_down_scale, L1_ffn_down_A, L1_ffn_down_B), axis=-1)
    return x

_drawn_inputs = setup_inputs


def setup_inputs(seed=0):
    import zlib

    import numpy as np

    out = dict(_drawn_inputs(seed))
    spreads = {'L0_attn_b_attn': (0.0, 0.1),
     'L0_attn_b_proj': (0.0, 0.1),
     'L1_xattn_bq': (0.0, 0.1),
     'L1_xattn_bk': (0.0, 0.8)}
    factors = {'L1_attn_wq': 8.0, 'L1_attn_wk': 8.0}
    for name, (base, spread) in spreads.items():
        noise = np.random.default_rng([zlib.crc32(name.encode()), seed]).standard_normal(out[name].shape)
        drawn = base * np.exp(spread * noise) if base else spread * noise
        out[name] = jnp.asarray(drawn.astype(out[name].dtype))
    for name, factor in factors.items():
        out[name] = (out[name] * factor).astype(out[name].dtype)
    return out
```

```python
import math
from contextlib import ExitStack

import concourse.bass as bass
import numpy as np
from concourse import mybir

F32 = mybir.dt.float32
F32R = mybir.dt.float32r
I32 = mybir.dt.int32
U32 = mybir.dt.uint32
ALU = mybir.AluOpType
ACT = mybir.ActivationFunctionType
AXX = mybir.AxisListType.X

P = 128
B, S, D = 16, 64, 512
TOK = B * S
NT = TOK // P
KC = D // P
HALF = TOK // 2
NH, HD = 32, 128
KVH = 8
GROUP = NH // KVH
NPAIR = KVH // 2
A_HD = D // NH
WINDOW = S + TOK + S
EXPERTS, RANK = 8, 16
INNER, LR_RANK = 1376, 32
NI = -(-INNER // P)
EPS = 1e-5
OFF = -3.0e38
ROPE_ROWS = 512
BLK = 1024
NRAW = 3


def f32(ap):
    return ap.bitcast(F32)


def build_program(nc, io, phases=9):
    ctx = ExitStack()

    def sb(stack, name, shape, dt=F32):
        return stack.enter_context(nc.sbuf_tensor("sb_" + name, shape, dt))

    def sem(name):
        return ctx.enter_context(nc.semaphore(name))

    xtok = sb(ctx, "xtok", [P, NT, D])
    xT = [sb(ctx, f"xT{i}", [P, KC, TOK], F32R) for i in range(2)]
    ident = sb(ctx, "ident", [P, P])
    zero = sb(ctx, "zero", [P, 1])
    bankA = [ctx.enter_context(nc.psum_tensor(f"bankA{i}", [P, 512], F32)) for i in range(2)]
    bankT = [ctx.enter_context(nc.psum_tensor(f"bankT{i}", [P, 512], F32)) for i in range(2)]
    bankY = [ctx.enter_context(nc.psum_tensor(f"bankY{i}", [P, 512], F32)) for i in range(2)]
    bankO = ctx.enter_context(nc.psum_tensor("bankO", [P, 2, 512], F32))

    def high_part(dst, src):
        return nc.gpsimd.tensor_tensor(dst, src, zero[0:src.shape[0]].to_broadcast([src.shape[0], src.shape[1]]), ALU.add)

    def product(out, pairs, start=True, stop=True):
        for i, (lhs, rhs) in enumerate(pairs):
            last = nc.tensor.matmul(out, lhs, rhs, start=start and i == 0, stop=stop and i == len(pairs) - 1)
        return last

    def three(lhs, rhs):
        return [(lhs[0], rhs[0]), (lhs[0], rhs[1]), (lhs[1], rhs[0])]

    def window(kt, b, *lead):
        at = S + b * S - (S if b % 2 == 0 else 0)
        return kt[(*lead, slice(at, at + P))]

    ln_stat = sem("ln_stat"); ln_mean = sem("ln_mean"); ln_sqrt = sem("ln_sqrt"); ln_rstd = sem("ln_rstd")
    ln_norm = sem("ln_norm"); ln_tr = sem("ln_tr"); ln_high = sem("ln_high"); ln_low = sem("ln_low"); out_done = sem("out_done")
    stats = sb(ctx, "ln_stats", [P, NT, 6])
    moments = sb(ctx, "ln_moments", [P, NT, 2])
    rstd = sb(ctx, "ln_rstd", [P, NT])
    epsilon = sb(ctx, "ln_epsilon", [P, 1])
    LG = NT // 2
    ln_banks = [bankT[0], bankT[1], bankY[0], bankY[1]]

    def ln_vector(dve, n, transposed=True):
        def statistics(g):
            for t in range(g * LG, g * LG + LG):
                nc.vector.bn_stats(stats[:, t, :], xtok[:, t, :]).then_inc(ln_stat, 1)
            for t in range(g * LG, g * LG + LG):
                dve.wait_ge(ln_stat, n * NT + t + 1)
                nc.vector.bn_aggr(moments[:, t, :], stats[:, t, :]).then_inc(ln_mean, 1)

        def normalise(g):
            part = rstd[:, g * LG:g * LG + LG]
            dve.wait_ge(ln_sqrt, 2 * n + g + 1)
            nc.vector.reciprocal(part, part).then_inc(ln_rstd, 1)
            dve.wait_ge(ln_rstd, 2 * n + g + 1)
            for t in range(g * LG, g * LG + LG):
                nc.vector.tensor_scalar(xtok[:, t, :], xtok[:, t, :], moments[:, t, 0:1], rstd[:, t:t + 1],
                                        ALU.subtract, ALU.mult).then_inc(ln_norm, 1)

        def low_parts(g):
            for t in range(g * LG, g * LG + LG):
                dve.wait_ge(ln_high, n * NT + t + 1)
                nc.vector.tensor_tensor(xT[1][:, :, t * P:(t + 1) * P], ln_banks[t % 4][:].rearrange("p (k c) -> p k c", k=KC),
                                        f32(xT[0][:, :, t * P:(t + 1) * P]), ALU.subtract).then_inc(ln_low, 1)

        statistics(0)
        normalise(0)
        statistics(1)
        if transposed:
            low_parts(0)
        normalise(1)
        if transposed:
            low_parts(1)

    def ln_scalar(act, n, transposed=True):
        for g in range(2):
            act.wait_ge(ln_mean, n * NT + g * LG + LG)
            nc.scalar.activation(rstd[:, g * LG:g * LG + LG], moments[:, g * LG:g * LG + LG, 1], ACT.Sqrt, bias=epsilon[:]).then_inc(ln_sqrt, 1)
            if transposed:
                for t in range(g * LG, g * LG + LG):
                    act.wait_ge(ln_tr, n * NT + t + 1)
                    nc.scalar.activation(xT[0][:, :, t * P:(t + 1) * P],
                                         ln_banks[t % 4][:].rearrange("p (k c) -> p k c", k=KC), ACT.Copy).then_inc(ln_high, 1)

    def ln_tensor(pe, n):
        for t in range(NT):
            pe.wait_ge(ln_norm, n * NT + t + 1)
            if t >= 4:
                pe.wait_ge(ln_low, n * NT + t - 3)
            for k in range(KC):
                done = nc.tensor.transpose(ln_banks[t % 4][:, k * P:(k + 1) * P], xtok[:, t, k * P:(k + 1) * P], ident[:])
            done.then_inc(ln_tr, 1)

    def finish(n):
        with nc.Block() as block:
            @block.vector
            def _(dve):
                ln_vector(dve, n, transposed=False)

            @block.scalar
            def _(act):
                ln_scalar(act, n, transposed=False)

            @block.sync
            def _(sp):
                for t in range(NT):
                    sp.wait_ge(ln_norm, n * NT + t + 1)
                    sp.dma_start(io["out"][:, t, :], xtok[:, t, :]).then_inc(out_done, 16)
                sp.wait_ge(out_done, NT * 16)

    zeroed = sem("zeroed")
    in_x = sem("in_x"); in_xT = sem("in_xT"); in_high = sem("in_high"); in_low = sem("in_low")
    with ExitStack() as mem:
        rawx = sb(mem, "rawx", [P, KC, TOK])
        with nc.Block() as block:
            @block.sync
            def _(sp):
                for k in range(KC):
                    sp.dma_start(rawx[:, k, :], io["xT"][:, k, :]).then_inc(in_xT, 16)
                sp.dma_start(xtok[:], io["x_tok"]).then_inc(in_x, 16)
                sp.dma_start(ident[:], io["ident"]).then_inc(in_x, 16)

            @block.gpsimd
            def _(pool):
                nc.gpsimd.memset(zero[:], 0.0).then_inc(zeroed, 1)
                nc.gpsimd.memset(epsilon[:], EPS).then_inc(zeroed, 1)
                pool.wait_ge(zeroed, 2)

            @block.scalar
            def _(act):
                act.wait_ge(in_xT, 16 * KC)
                act.wait_ge(in_x, 32)
                for k in range(KC):
                    nc.scalar.activation(xT[0][:, k, :], rawx[:, k, :], ACT.Copy).then_inc(in_high, 1)

            @block.vector
            def _(dve):
                for k in range(KC):
                    dve.wait_ge(in_high, k + 1)
                    nc.vector.tensor_tensor(xT[1][:, k, :], rawx[:, k, :], f32(xT[0][:, k, :]), ALU.subtract).then_inc(in_low, 1)

    cmem = ExitStack()
    cT = [sb(cmem, f"cT{i}", [P, KC, TOK], F32R) for i in range(2)]

    def softmax_stages(tag):
        return {k: sem(f"{tag}_{k}") for k in ("masked", "max", "sub", "exp", "sum", "inv", "prob")}

    if phases >= 1:
        QUADS = B // 4
        UNITS = 4 * QUADS * 4
        w_raw = [sem(f"A_raw{i}") for i in range(NRAW)]
        w_high = sem("A_whigh"); w_low = sem("A_wlow")
        small = sem("A_small"); padded = sem("A_padded"); pbias = sem("A_pbias")
        a_ready = sem("A_aready"); v_done = sem("A_vdone"); q_done = sem("A_qdone"); k_done = sem("A_kdone")
        s_ready = sem("A_sready"); st = softmax_stages("A")
        t_ready = sem("A_tready"); pt_done = sem("A_ptdone"); o_ready = sem("A_oready")
        o_even = sem("A_oeven"); o_odd = sem("A_oodd"); o_high = sem("A_ohigh"); o_low = sem("A_olow")
        y_ready = sem("A_yready"); y_done = sem("A_ydone"); pv_last = sem("A_pvlast")
        with ExitStack() as mem:
            raw = [sb(mem, f"Araw{i}", [P, BLK]) for i in range(NRAW)]
            wbig = [sb(mem, f"Awbig{i}", [P, KC, D], F32R) for i in range(2)]
            wqk = [sb(mem, f"Awqk{i}", [P, 2, KC, P], F32R) for i in range(2)]
            V = sb(mem, "AV", [P, NT, D])
            qm = sb(mem, "Aqm", [P, B, 2, S])
            kt = sb(mem, "Akt", [P, WINDOW])
            oT = [sb(mem, f"AoT{i}", [P, KC, TOK], F32R) for i in range(2)]
            alibi = sb(mem, "Aalibi", [P, NH // 2, S])
            bqk = sb(mem, "Abqk", [P, 2, KC]); bv = sb(mem, "Abv", [P, D]); bp = sb(mem, "Abp", [P, D])
            parity = sb(mem, "Aparity", [P, 2])
            sc = [sb(mem, f"Asc{i}", [P, 2, 2, S]) for i in range(2)]
            pt = [sb(mem, f"Apt{i}", [P, 2, P]) for i in range(2)]
            mx = sb(mem, "Amx", [P, 2, 4]); sm = sb(mem, "Asm", [P, 2, 4]); ri = sb(mem, "Ari", [P, 2, 4])
            oc = sb(mem, "Aoc", [P, 2, 2, S]); od = sb(mem, "Aod", [P, 2, 2, S])
            sbank = [bankA[0], bankA[1], bankY[0], bankY[1]]
            blocks = [(io["wv"][:, i * BLK:(i + 1) * BLK], [w[:].rearrange("p k n -> p (k n)")[:, i * BLK:(i + 1) * BLK] for w in wbig]) for i in range(2)]
            blocks += [(io["wqk"][c], [w[:].rearrange("p a k n -> p (a k n)") for w in wqk]) for c in range(KC)]
            blocks += [(io["wp"][:, i * BLK:(i + 1) * BLK], [w[:].rearrange("p k n -> p (k n)")[:, i * BLK:(i + 1) * BLK] for w in wbig]) for i in range(2)]
            blocks += [(io["ctxT"][:, k, :], [c[:, k, :] for c in cT]) for k in range(KC)]

            with nc.Block() as block:
                @block.sync
                def _(sp):
                    for n, (src, _) in enumerate(blocks):
                        if n >= NRAW:
                            sp.wait_ge(w_low, n - NRAW + 1)
                        sp.dma_start(raw[n % NRAW][:], src).then_inc(w_raw[n % NRAW], 16)
                        if n == 1:
                            sp.dma_start(bqk[:], io["bqk"]).then_inc(small, 16)
                            sp.dma_start(parity[:], io["parity"]).then_inc(small, 16)
                            sp.dma_start(alibi[:], io["alibi"]).then_inc(small, 16)
                            sp.dma_start(bv[:], io["bv"].to_broadcast([P, D])).then_inc(small, 16)
                            sp.dma_start(bp[:], io["bp"].to_broadcast([P, D])).then_inc(small, 16)

                @block.gpsimd
                def _(pool):
                    nc.gpsimd.memset(kt[:], 0.0).then_inc(padded, 1)
                    for n, (_, dst) in enumerate(blocks):
                        pool.wait_ge(w_raw[n % NRAW], 16 * (n // NRAW + 1))
                        if 3 <= n < 2 + KC:
                            pool.wait_ge(a_ready, 8 // 2 + 4 * (n - 2))
                        if n == 2 + KC:
                            pool.wait_ge(a_ready, 4)
                        high_part(dst[0], raw[n % NRAW][:]).then_inc(w_high, 1)
                        pool.wait_ge(w_high, n + 1)
                        nc.gpsimd.tensor_tensor(dst[1], raw[n % NRAW][:], f32(dst[0]), ALU.subtract).then_inc(w_low, 1)

                @block.tensor
                def _(pe):
                    pe.wait_ge(w_low, 2)
                    for t in range(NT):
                        if t >= 2:
                            pe.wait_ge(v_done, t - 1)
                        tok = slice(t * P, (t + 1) * P)
                        done = product(bankA[t % 2][:], [x for k in range(KC) for x in three([w[:, k, tok] for w in xT], [w[:, k, :] for w in wbig])])
                        if t % 2:
                            done.then_inc(a_ready, 1)
                        else:
                            done.then_inc(pv_last, 1)
                    pe.wait_ge(v_done, NT)

                    def scores(n):
                        c, quad, m = n // 16, n // 4 % 4, n % 4
                        if quad == 0 and m == 0:
                            project(c)
                        if n % 16 == 0:
                            pe.wait_ge(q_done, 4 * (c + 1))
                            pe.wait_ge(k_done, 2 * (c + 1))
                        if n >= 4:
                            pe.wait_ge(st["masked"], n - 3)
                        rows = slice(32 * m, 32 * m + 32)
                        for j in range(4):
                            b = quad * 4 + j
                            done = nc.tensor.matmul(sbank[m][:, j * P:(j + 1) * P], qm[rows, b].rearrange("p e q -> p (e q)"), window(kt, b, rows), start=True, stop=True)
                        done.then_inc(s_ready, 1)

                    def project(c):
                        pe.wait_ge(w_low, 3 + c)
                        if c:
                            pe.wait_ge(st["masked"], 16 * c)
                        for a in range(2):
                            for h in range(2):
                                if a:
                                    pe.wait_ge(q_done, 4 * c + 2 * (h + 1))
                                cols = slice(h * HALF, (h + 1) * HALF)
                                product(bankA[h][:], [x for k in range(KC) for x in three([w[:, a, k, :] for w in wqk], [w[:, k, cols] for w in xT])]).then_inc(a_ready, 1)

                    scores(0)
                    for n in range(UNITS):
                        c, quad, m = n // 16, n // 4 % 4, n % 4
                        if n + 1 < UNITS and n % 16 != 15:
                            scores(n + 1)
                        pe.wait_ge(st["prob"], n + 1)
                        if n >= 2:
                            pe.wait_ge(pt_done, n - 1)
                        for j in range(2):
                            done = nc.tensor.transpose(bankT[n % 2][:, j * P:(j + 1) * P], sc[n % 2][:, j].rearrange("p b k -> p (b k)"), ident[:])
                        done.then_inc(t_ready, 1)
                        if n % 16 == 15 and n + 1 < UNITS:
                            scores(n + 1)
                        pe.wait_ge(pt_done, n + 1)
                        if m == 0 and n:
                            pe.wait_ge(o_low, n // 4)
                        for j in range(4):
                            b, par, bpair = quad * 4 + j, j % 2, j // 2
                            rows = slice(S * par, S * par + S)
                            done = nc.tensor.matmul(bankO[32 * m:32 * m + 32, par, bpair * P:(bpair + 1) * P],
                                                    V[rows, b // 2, c * P + 32 * m:c * P + 32 * m + 32], pt[n % 2][rows, bpair, :], start=True, stop=True)
                        done.then_inc(o_ready, 1)
                    pe.wait_ge(w_low, 4 + KC)
                    pe.wait_ge(o_low, 16)
                    for t in range(NT):
                        if t >= 2:
                            pe.wait_ge(y_done, t - 1)
                        tok = slice(t * P, (t + 1) * P)
                        product(bankY[t % 2][:], [x for k in range(KC) for x in three([w[:, k, tok] for w in oT], [w[:, k, :] for w in wbig])]).then_inc(y_ready, 1)

                @block.scalar
                def _(act):
                    act.wait_ge(small, 80)
                    act.wait_ge(padded, 1)

                    def keys(c):
                        for h in range(2):
                            act.wait_ge(a_ready, 4 + 4 * c + 3 + h)
                            nc.scalar.activation(kt[:, S + h * HALF:S + (h + 1) * HALF], bankA[h][:], ACT.Identity, bias=bqk[:, 1, c:c + 1]).then_inc(k_done, 1)

                    keys(0)
                    for n in range(UNITS):
                        c, quad, m = n // 16, n // 4 % 4, n % 4
                        act.wait_ge(st["sub"], n + 1)
                        flat = sc[n % 2][:].rearrange("p a b k -> p (a b k)")
                        nc.scalar.activation(flat, flat, ACT.Exp).then_inc(st["exp"], 1)
                        act.wait_ge(t_ready, n + 1)
                        nc.scalar.activation(pt[n % 2][:].rearrange("p a b -> p (a b)"), bankT[n % 2][:, 0:256], ACT.Copy).then_inc(pt_done, 1)
                        if n % 16 == 15 and n + 1 < UNITS:
                            keys(c + 1)
                        if m == 3:
                            act.wait_ge(o_odd, 2 * (n // 4 + 1))
                            nc.scalar.activation(oT[0][:, c, quad * 256:(quad + 1) * 256], od[:].rearrange("p a b k -> p (a b k)"), ACT.Copy).then_inc(o_high, 1)

                @block.vector
                def _(dve):
                    dve.wait_ge(small, 80)
                    for t in range(NT):
                        dve.wait_ge(a_ready if t % 2 else pv_last, t // 2 + 1)
                        nc.vector.tensor_tensor(V[:, t, :], bankA[t % 2][:], bv[:], ALU.add).then_inc(v_done, 1)
                    for t in range(NT):
                        nc.vector.tensor_tensor(xtok[:, t, :], xtok[:, t, :], bp[:], ALU.add).then_inc(pbias, 1)

                    def front(n):
                        c, m = n // 16, n % 4
                        if n % 16 == 0:
                            for h in range(2):
                                dve.wait_ge(a_ready, 4 + 4 * c + 1 + h)
                                for e in range(2):
                                    nc.vector.tensor_scalar(qm[:, h * B // 2:(h + 1) * B // 2, e, :], bankA[h][:].rearrange("p (b q) -> p b q", q=S), bqk[:, 0, c:c + 1], parity[:, e:e + 1],
                                                            ALU.add, ALU.mult).then_inc(q_done, 1)
                        dve.wait_ge(s_ready, n + 1)
                        if n >= 2:
                            dve.wait_ge(t_ready, n - 1)
                        view = sbank[m][:].rearrange("p (a c) -> p a c", a=2)[:, :, S:S + P].rearrange("p a (b k) -> p a b k", b=2)
                        bias = alibi[:, c * 4 + m, :].unsqueeze(1).to_broadcast([P, 2, S])
                        for a in range(2):
                            last = nc.vector.scalar_tensor_tensor(sc[n % 2][:, a], view[:, a], 1.0 / A_HD, bias, ALU.mult, ALU.add)
                            last.then_inc(st["masked"] if a else pbias, 1)
                        dve.wait_ge(st["masked"], n + 1)
                        dve.wait_ge(pbias, NT + n + 1)
                        s4 = sc[n % 2][:].rearrange("p a b k -> p (a b) k")
                        nc.vector.tensor_reduce(mx[:, n % 2, :], s4, AXX, ALU.max).then_inc(st["max"], 1)
                        dve.wait_ge(st["max"], n + 1)
                        nc.vector.tensor_tensor(s4, s4, mx[:, n % 2, :].unsqueeze(2).to_broadcast([P, 4, S]), ALU.subtract).then_inc(st["sub"], 1)

                    def back(n):
                        s4 = sc[n % 2][:].rearrange("p a b k -> p (a b) k")
                        dve.wait_ge(st["exp"], n + 1)
                        nc.vector.tensor_reduce(sm[:, n % 2, :], s4, AXX, ALU.add).then_inc(st["sum"], 1)
                        dve.wait_ge(st["sum"], n + 1)
                        nc.vector.reciprocal(ri[:, n % 2, :], sm[:, n % 2, :]).then_inc(st["inv"], 1)
                        dve.wait_ge(st["inv"], n + 1)
                        nc.vector.tensor_tensor(s4, s4, ri[:, n % 2, :].unsqueeze(2).to_broadcast([P, 4, S]), ALU.mult).then_inc(st["prob"], 1)

                    def gather(g):
                        c, quad = g // 4, g % 4
                        dve.wait_ge(o_ready, 4 * g + 4)
                        if g:
                            dve.wait_ge(o_low, g)
                        for par in range(2):
                            nc.vector.tensor_scalar(oc[:, :, par, :], bankO[:, par, 0:256].rearrange("p (a c) -> p a c", a=2)[:, :, 0:S],
                                                    parity[:, 0:1], None, ALU.mult).then_inc(o_even, 1)
                        dve.wait_ge(o_even, 2 * g + 2)
                        for par in range(2):
                            nc.vector.scalar_tensor_tensor(od[:, :, par, :], bankO[:, par, 0:256].rearrange("p (a c) -> p a c", a=2)[:, :, S:P],
                                                           parity[:, 1:2], oc[:, :, par, :], ALU.mult, ALU.add).then_inc(o_odd, 1)
                        dve.wait_ge(o_high, g + 1)
                        cols = slice(quad * 256, (quad + 1) * 256)
                        nc.vector.tensor_tensor(oT[1][:, c, cols], od[:].rearrange("p a b k -> p (a b k)"), f32(oT[0][:, c, cols]), ALU.subtract).then_inc(o_low, 1)

                    front(0)
                    for n in range(UNITS):
                        if n + 1 < UNITS and n % 16 != 15:
                            front(n + 1)
                        back(n)
                        if n % 16 == 15 and n + 1 < UNITS:
                            front(n + 1)
                        if n % 4 == 3:
                            gather(n // 4)
                    for t in range(NT):
                        dve.wait_ge(y_ready, t + 1)
                        dve.wait_ge(pbias, t + 1)
                        nc.vector.tensor_tensor(xtok[:, t, :], xtok[:, t, :], bankY[t % 2][:], ALU.add).then_inc(y_done, 1)
        if phases == 1:
            finish(0)
            return
    def grouped_attention(tag, norm, w_dram, source, rope, mask_of):
        TURN_BLOCKS, TURN_BANKS, TURN_QK = 10, 40, 20
        w_raw = [sem(f"{tag}_raw{i}") for i in range(2)]
        w_high = sem(f"{tag}_whigh"); w_low = sem(f"{tag}_wlow")
        padded = sem(f"{tag}_padded"); a_ready = sem(f"{tag}_aready")
        swapped = sem(f"{tag}_swapped"); roped = sem(f"{tag}_roped"); turned = sem(f"{tag}_turned")
        qk_done = sem(f"{tag}_qkdone"); v_done = sem(f"{tag}_vdone")
        st = softmax_stages(tag)
        t_ready = sem(f"{tag}_tready"); pt_done = sem(f"{tag}_ptdone")
        o_ready = sem(f"{tag}_oready"); o_high = sem(f"{tag}_ohigh"); o_low = sem(f"{tag}_olow")
        y_ready = sem(f"{tag}_yready"); y_done = sem(f"{tag}_ydone")
        with ExitStack() as mem:
            raw = [sb(mem, f"{tag}raw{i}", [P, BLK]) for i in range(2)]
            wk = [sb(mem, f"{tag}wk{i}", [P, 2, KC, HD], F32R) for i in range(2)]
            wv = [sb(mem, f"{tag}wv{i}", [P, KC, 2 * HD], F32R) for i in range(2)]
            wq = [sb(mem, f"{tag}wq{i}", [P, GROUP, KC, HD], F32R) for i in range(2)]
            wo = [sb(mem, f"{tag}wo{i}", [P, GROUP, D], F32R) for i in range(2)]
            qT = sb(mem, f"{tag}qT", [P, B, GROUP, S])
            kt = sb(mem, f"{tag}kt", [P, 2, WINDOW])
            V = sb(mem, f"{tag}V", [P, NT, 2 * HD])
            sw = [sb(mem, f"{tag}sw{i}", [P, HALF]) for i in range(2)] if rope else None
            sc = [sb(mem, f"{tag}sc{i}", [P, 2, 2, S]) for i in range(3)]
            pt = [sb(mem, f"{tag}pt{i}", [P, GROUP * S]) for i in range(2)]
            oT = [[sb(mem, f"{tag}oT{i}{p}", [P, GROUP, 2, S], F32R) for p in range(2)] for i in range(2)]
            mx = sb(mem, f"{tag}mx", [P, 2, 4]); sm = sb(mem, f"{tag}sm", [P, 2, 4]); ri = sb(mem, f"{tag}ri", [P, 2, 4])

            def halves(pair, pattern):
                flat = [w[:].rearrange(pattern) for w in pair]
                return [[f[:, i * BLK:(i + 1) * BLK] for f in flat] for i in range(2)]

            turn_blocks = [[w[:].rearrange("p h k n -> p (h k n)") for w in wk], [w[:].rearrange("p k n -> p (k n)") for w in wv]]
            turn_blocks += 2 * (halves(wq, "p h k n -> p (h k n)") + halves(wo, "p h n -> p (h n)"))

            with nc.Block() as block:
                @block.sync
                def _(sp):
                    with sp.Fori(0, NPAIR) as it:
                        for n in range(TURN_BLOCKS):
                            sp.wait_ge(w_low, it * TURN_BLOCKS + n + 1)
                            sp.dma_start(raw[n % 2][:], w_dram[bass.ds(it, 1), n].rearrange("a p c -> p (a c)")).then_inc(w_raw[n % 2], 16)

                @block.gpsimd
                def _(pool):
                    nc.gpsimd.memset(kt[:], 0.0).then_inc(padded, 1)
                    pool.sem_inc(w_low, 2)
                    with pool.Fori(0, NPAIR) as it:
                        for n, dst in enumerate(turn_blocks):
                            if n < 2:
                                pool.wait_ge(v_done, it * 4 + 1)
                            elif n in (2, 3):
                                pool.wait_ge(qk_done, it * TURN_QK + 2)
                            elif n in (6, 7):
                                pool.wait_ge(qk_done, it * TURN_QK + 12 + 2)
                            elif n in (4, 5):
                                pool.wait_ge(y_done, it * 16 + 2)
                            else:
                                pool.wait_ge(y_done, it * 16 + 8 + 2)
                            pool.wait_ge(w_raw[n % 2], it * (16 * TURN_BLOCKS // 2) + 16 * (n // 2 + 1))
                            high_part(dst[0], raw[n % 2][:]).then_inc(w_high, 1)
                            pool.wait_ge(w_high, it * TURN_BLOCKS + n + 1)
                            nc.gpsimd.tensor_tensor(dst[1], raw[n % 2][:], f32(dst[0]), ALU.subtract).then_inc(w_low, 1)

                @block.tensor
                def _(pe):
                    pe.wait_ge(padded, 1)
                    ln_tensor(pe, norm)
                    pe.wait_ge(ln_low, (norm + 1) * NT)
                    with pe.Fori(0, NPAIR) as it:
                        def weights(n):
                            pe.wait_ge(w_low, it * TURN_BLOCKS + n + 3)

                        def take(a):
                            v = a - 2
                            if v < 0:
                                pe.wait_ge(st["masked"], it * 16 + 1)
                            elif 4 <= v < 8:
                                pe.wait_ge(v_done, it * 4 + v - 2)
                            elif v >= 8 and (v - 8) % 16 >= 8:
                                pe.wait_ge(st["masked"], it * 16 + (v - 8) // 16 * 8 + (v - 8) % 16 - 6)
                            else:
                                r = v if v < 4 else 4 + (v - 8) // 16 * 8 + (v - 8) % 16
                                if rope:
                                    pe.wait_ge(roped, it * TURN_QK + r + 1)
                                else:
                                    pe.wait_ge(qk_done, it * TURN_QK + r + 3)
                            return bankA[a % 2]

                        weights(0)
                        for a in range(4):
                            cols = slice(a % 2 * HALF, (a % 2 + 1) * HALF)
                            product(take(a)[:], [x for k in range(KC) for x in three([w[:, a // 2, k, :] for w in wk], [s[:, k, cols] for s in source])]).then_inc(a_ready, 1)
                        weights(1)
                        for t in range(NT):
                            bank = take(4 + t // 2) if t % 2 == 0 else bankA[t // 2 % 2]
                            done = product(bank[:, t % 2 * 256:t % 2 * 256 + 256],
                                           [x for k in range(KC) for x in three([s[:, k, t * P:(t + 1) * P] for s in source], [w[:, k, :] for w in wv])])
                            if t % 2:
                                done.then_inc(a_ready, 1)
                        for j in range(2):
                            base = 8 + 16 * j
                            unit = lambda t: it * 16 + j * 8 + t

                            weights(3 + 4 * j)
                            for n in range(8):
                                cols = slice(n // 4 * HALF, (n // 4 + 1) * HALF)
                                product(take(base + n)[:], [x for k in range(KC) for x in three([w[:, n % 4, k, :] for w in wq], [s[:, k, cols] for s in xT])]).then_inc(a_ready, 1)

                            def scores(t):
                                if t in (0, NT // 2):
                                    pe.wait_ge(qk_done, it * TURN_QK + 4 + 8 * j + (4 if t == 0 else 8) + 2)
                                bank = take(base + 8 + t)
                                for hp in range(2):
                                    for b in range(2):
                                        at = (hp * 2 + b) * P
                                        done = nc.tensor.matmul(bank[:, at:at + P], qT[:, 2 * t + b, 2 * hp:2 * hp + 2, :].rearrange("p h q -> p (h q)"),
                                                                window(kt, 2 * t + b, slice(None), j), start=True, stop=True)
                                done.then_inc(a_ready, 1)

                            def output(t):
                                if t == 0:
                                    weights(5 + 4 * j)
                                pe.wait_ge(o_low, unit(t) + 2)
                                pe.wait_ge(y_done, unit(t) + 1)
                                product(bankY[t % 2][:], [x for h in range(GROUP) for x in
                                        three([o[:, h].rearrange("p b q -> p (b q)") for o in oT[t % 2]], [w[:, h, :] for w in wo])]).then_inc(y_ready, 1)

                            scores(0)
                            scores(1)
                            for t in range(NT):
                                pe.wait_ge(st["prob"], unit(t) + 1)
                                pe.wait_ge(pt_done, unit(t) + 1)
                                for hp in range(2):
                                    done = nc.tensor.transpose(bankT[t % 2][:, hp * P:(hp + 1) * P], sc[t % 3][:, hp].rearrange("p b k -> p (b k)"), ident[:])
                                done.then_inc(t_ready, 1)
                                if t + 2 < NT:
                                    scores(t + 2)
                                pe.wait_ge(pt_done, unit(t) + 3)
                                pe.wait_ge(o_low, unit(t) + 1)
                                for b in range(2):
                                    rows = slice(S * b, S * b + S)
                                    done = nc.tensor.matmul(bankO[:, b, 0:GROUP * S], V[rows, t, j * HD:(j + 1) * HD], pt[t % 2][rows, :], start=True, stop=True)
                                done.then_inc(o_ready, 1)
                                if t:
                                    output(t - 1)
                            output(NT - 1)

                @block.scalar
                def _(act):
                    ln_scalar(act, norm)
                    if not rope:
                        act.sem_inc(qk_done, 2)
                    act.sem_inc(v_done, 1)
                    act.sem_inc(pt_done, 2)
                    with act.Fori(0, NPAIR) as it:
                        def ready(a):
                            act.wait_ge(a_ready, it * TURN_BANKS + a + 1)

                        def queries_or_keys(a, r, dst):
                            ready(a)
                            if rope:
                                act.wait_ge(qk_done, it * TURN_QK + r + 1)
                                for i in range(2):
                                    nc.scalar.activation(sw[r % 2][64 * i:64 * i + 64, :], bankA[a % 2][64 - 64 * i:P - 64 * i, :], ACT.Copy).then_inc(swapped, 1)
                            else:
                                nc.scalar.activation(dst, bankA[a % 2][:].rearrange("p (b s) -> p b s", s=S), ACT.Copy).then_inc(qk_done, 1)
                        for a in range(4):
                            at = S + a % 2 * HALF
                            queries_or_keys(a, a, kt[:, a // 2, at:at + HALF].rearrange("p (b s) -> p b s", s=S))
                        for i in range(4):
                            ready(4 + i)
                            nc.scalar.activation(V[:, 2 * i:2 * i + 2, :].rearrange("p t n -> p (t n)"), bankA[i % 2][:], ACT.Copy).then_inc(v_done, 1)
                        for j in range(2):
                            unit = lambda t: it * 16 + j * 8 + t
                            for n in range(8):
                                half = n // 4
                                queries_or_keys(8 + 16 * j + n, 4 + 8 * j + n, qT[:, half * B // 2:(half + 1) * B // 2, n % 4, :])

                            def exp(t):
                                act.wait_ge(st["sub"], unit(t) + 1)
                                flat = sc[t % 3][:].rearrange("p a b k -> p (a b k)")
                                nc.scalar.activation(flat, flat, ACT.Exp, scale=HD ** -0.5).then_inc(st["exp"], 1)
                            exp(0)
                            exp(1)
                            for t in range(NT):
                                act.wait_ge(t_ready, unit(t) + 1)
                                nc.scalar.activation(pt[t % 2][:], bankT[t % 2][:, 0:GROUP * S], ACT.Copy).then_inc(pt_done, 1)
                                act.wait_ge(o_ready, unit(t) + 1)
                                nc.scalar.activation(oT[t % 2][0][:].rearrange("p h b q -> p b h q"),
                                                     bankO[:, :, 0:GROUP * S].rearrange("p b (h q) -> p b h q", h=GROUP), ACT.Copy).then_inc(o_high, 1)
                                if t + 2 < NT:
                                    exp(t + 2)

                def residual(dve, t, unit):
                    dve.wait_ge(y_ready, unit(t) + 1)
                    nc.vector.tensor_tensor(xtok[:, t, :], xtok[:, t, :], bankY[t % 2][:], ALU.add).then_inc(y_done, 1)

                @block.vector
                def _(dve):
                    ln_vector(dve, norm)
                    if rope:
                        dve.sem_inc(qk_done, 2)
                    dve.sem_inc(st["masked"], 1)
                    dve.sem_inc(o_low, 1)
                    dve.sem_inc(y_done, 2)
                    with dve.Fori(0, NPAIR) as it:
                        def rope_first(a, r, dst):
                            dve.wait_ge(swapped, it * (2 * TURN_QK) + 2 * r + 2)
                            half = slice(*((0, HALF) if dst[1] == 0 else (HALF, TOK)))
                            nc.vector.tensor_tensor(dst[0], bankA[a % 2][:].rearrange("p (b s) -> p b s", s=S),
                                                    rope[0][:, half].rearrange("p (b s) -> p b s", s=S), ALU.mult).then_inc(roped, 1)
                            nc.vector.tensor_tensor(sw[r % 2][:], sw[r % 2][:], rope[1][:, half], ALU.mult).then_inc(turned, 1)

                        def rope_second(r, dst):
                            dve.wait_ge(roped, it * TURN_QK + r + 1)
                            dve.wait_ge(turned, it * TURN_QK + r + 1)
                            nc.vector.tensor_tensor(dst[0], dst[0], sw[r % 2][:].rearrange("p (b s) -> p b s", s=S), ALU.add).then_inc(qk_done, 1)

                        def rope_all(items):
                            for i, (a, r, dst) in enumerate(items):
                                rope_first(a, r, dst)
                                if i:
                                    rope_second(*items[i - 1][1:])
                            rope_second(*items[-1][1:])
                        if rope:
                            rope_all([(a, a, (kt[:, a // 2, S + a % 2 * HALF:S + a % 2 * HALF + HALF].rearrange("p (b s) -> p b s", s=S), a % 2)) for a in range(4)])
                        for j in range(2):
                            unit = lambda t: it * 16 + j * 8 + t
                            if rope:
                                rope_all([(8 + 16 * j + n, 4 + 8 * j + n, (qT[:, n // 4 * B // 2:(n // 4 + 1) * B // 2, n % 4, :], n // 4)) for n in range(8)])

                            def front(t):
                                a = 16 + 16 * j + t
                                s3 = sc[t % 3][:].rearrange("p a b k -> p a (b k)")
                                s4 = sc[t % 3][:].rearrange("p a b k -> p (a b) k")
                                dve.wait_ge(a_ready, it * TURN_BANKS + a + 1)
                                nc.vector.tensor_tensor(s3, bankA[a % 2][:].rearrange("p (a c) -> p a c", a=2)[:, :, S:S + P],
                                                        mask_of(t).unsqueeze(1).to_broadcast([P, 2, P]), ALU.min).then_inc(st["masked"], 1)
                                yield
                                dve.wait_ge(st["masked"], unit(t) + 2)
                                nc.vector.tensor_reduce(mx[:, t % 2, :], s4, AXX, ALU.max).then_inc(st["max"], 1)
                                yield
                                dve.wait_ge(st["max"], unit(t) + 1)
                                nc.vector.tensor_tensor(s4, s4, mx[:, t % 2, :].unsqueeze(2).to_broadcast([P, 4, S]), ALU.subtract).then_inc(st["sub"], 1)
                                yield

                            def back(t):
                                s4 = sc[t % 3][:].rearrange("p a b k -> p (a b) k")
                                dve.wait_ge(st["exp"], unit(t) + 1)
                                nc.vector.tensor_reduce(sm[:, t % 2, :], s4, AXX, ALU.add).then_inc(st["sum"], 1)
                                yield
                                dve.wait_ge(st["sum"], unit(t) + 1)
                                nc.vector.reciprocal(ri[:, t % 2, :], sm[:, t % 2, :]).then_inc(st["inv"], 1)
                                yield
                                dve.wait_ge(st["inv"], unit(t) + 1)
                                nc.vector.tensor_tensor(s4, s4, ri[:, t % 2, :].unsqueeze(2).to_broadcast([P, 4, S]), ALU.mult).then_inc(st["prob"], 1)
                                yield

                            def both(f, b):
                                for _ in range(3):
                                    if f:
                                        next(f)
                                    if b:
                                        next(b)

                            both(front(0), None)
                            both(front(1), back(0))
                            for t in range(NT):
                                both(front(t + 2) if t + 2 < NT else None, back(t + 1) if t + 1 < NT else None)
                                if t > 1:
                                    residual(dve, t - 2, unit)
                                dve.wait_ge(o_high, unit(t) + 1)
                                nc.vector.tensor_tensor(oT[t % 2][1][:].rearrange("p h b q -> p b h q"), bankO[:, :, 0:GROUP * S].rearrange("p b (h q) -> p b h q", h=GROUP),
                                                        f32(oT[t % 2][0][:]).rearrange("p h b q -> p b h q"), ALU.subtract).then_inc(o_low, 1)
                            residual(dve, NT - 2, unit)
                            residual(dve, NT - 1, unit)

    tmem = ExitStack()
    if phases >= 2:
        setup = sem("R_setup"); clamped = sem("R_clamped"); gathered = sem("R_gathered"); flipped = sem("R_flipped")
        tabled = sem("R_tabled"); bound_sem = sem("R_bound")
        cosT = sb(tmem, "cosT", [P, TOK]); sinT = sb(tmem, "sinT", [P, TOK]); bound = sb(tmem, "bound", [P, NT, P])
        with ExitStack() as mem:
            pos = sb(mem, "pos", [P, NT], I32); row = sb(mem, "row", [P, NT], U32)
            rows = sb(mem, "rows", [P, NT, 2 * P]); mask = sb(mem, "mask", [P, NT, P], I32)
            hidden = sb(mem, "hidden", [P, NT, P])
            with nc.Block() as block:
                @block.sync
                def _(sp):
                    sp.dma_start(pos[:], io["pos"]).then_inc(setup, 16)
                    sp.dma_start(mask[:], io["mask"]).then_inc(setup, 16)

                @block.gpsimd
                def _(pool):
                    pool.wait_ge(clamped, 1)
                    for t in range(NT):
                        nc.gpsimd.indirect_dma_start(out=rows[:, t, :], out_offset=None, in_=io["rope"],
                                                     in_offset=bass.IndirectOffsetOnAxis(ap=row[:, t:t + 1], axis=0)).then_inc(gathered, 16)

                @block.tensor
                def _(pe):
                    pe.wait_ge(gathered, 16 * NT)
                    for t in range(NT):
                        if t >= 2:
                            pe.wait_ge(tabled, 2 * (t - 1))
                        for i in range(2):
                            done = nc.tensor.transpose(bankA[t % 2][:, i * P:(i + 1) * P], rows[:, t, i * P:(i + 1) * P], ident[:])
                        done.then_inc(flipped, 1)

                @block.vector
                def _(dve):
                    dve.wait_ge(setup, 32)
                    nc.vector.tensor_scalar(row[:], pos[:], 0, ROPE_ROWS - 1, ALU.max, ALU.min).then_inc(clamped, 1)
                    nc.vector.tensor_scalar(hidden[:], mask[:], 0, -1.0e9 * HD ** 0.5, ALU.is_equal, ALU.mult).then_inc(bound_sem, 1)
                    nc.vector.tensor_scalar(bound[:], mask[:], 0, -OFF, ALU.not_equal, ALU.mult).then_inc(bound_sem, 1)
                    dve.wait_ge(bound_sem, 2)
                    nc.vector.tensor_tensor(bound[:], bound[:], hidden[:], ALU.add).then_inc(bound_sem, 1)
                    for t in range(NT):
                        dve.wait_ge(flipped, t + 1)
                        for i, dst in enumerate((cosT, sinT)):
                            nc.vector.tensor_copy(dst[:, t * P:(t + 1) * P], bankA[t % 2][:, i * P:(i + 1) * P]).then_inc(tabled, 1)
        grouped_attention("B", 0, io["w_attn0"], cT, (cosT, sinT), lambda t: bound[:, t, :])
        tmem.close()
        if phases == 2:
            finish(1)
            return

    def block_loader(sp, blocks, raw, w_raw, w_low):
        for n, (src, rows, cols, *_) in enumerate(blocks):
            if n >= len(raw):
                sp.wait_ge(w_low, n - len(raw) + 1)
            sp.dma_start(raw[n % len(raw)][0:rows, 0:cols], src).then_inc(w_raw[n % len(raw)], 16)

    def split_block(pool, n, rows, cols, dst, raw, w_raw, w_high, w_low):
        src = raw[n % len(raw)][0:rows, 0:cols]
        pool.wait_ge(w_raw[n % len(raw)], 16 * (n // len(raw) + 1))
        high_part(dst[0], src).then_inc(w_high, 1)
        pool.wait_ge(w_high, n + 1)
        nc.gpsimd.tensor_tensor(dst[1], src, f32(dst[0]), ALU.subtract).then_inc(w_low, 1)

    if phases >= 3:
        w_raw = [sem(f"C_raw{i}") for i in range(2)]; w_high = sem("C_whigh"); w_low = sem("C_wlow")
        small = sem("C_small"); a_ready = sem("C_aready"); a_done = sem("C_adone"); route = sem("C_route"); route_exp = sem("C_rexp")
        t_ready = sem("C_tready"); m_high = sem("C_mhigh"); m_low = sem("C_mlow"); y_ready = sem("C_yready"); y_done = sem("C_ydone")
        ER = EXPERTS * RANK
        with ExitStack() as mem:
            raw = [sb(mem, f"Craw{i}", [P, BLK]) for i in range(2)]
            war = [sb(mem, f"Cwar{i}", [P, KC, 256], F32R) for i in range(2)]
            wb = [sb(mem, f"Cwb{i}", [P, KC, D], F32R) for i in range(2)]
            wup = [sb(mem, f"Cwup{i}", [P, D], F32R) for i in range(2)]
            mid = sb(mem, "Cmid", [P, NT, ER]); lg = sb(mem, "Clg", [P, NT, EXPERTS])
            earlier = sb(mem, "Cearlier", [P, EXPERTS, EXPERTS])
            top = sb(mem, "Ctop", [P, NT]); pr = sb(mem, "Cpr", [P, NT, EXPERTS]); gate = sb(mem, "Cgate", [P, NT, EXPERTS])
            above = sb(mem, "Cabove", [P, NT, EXPERTS, EXPERTS]); ties = sb(mem, "Cties", [P, NT, EXPERTS, EXPERTS])
            mT = [sb(mem, f"CmT{i}", [P, TOK], F32R) for i in range(2)]
            flat = lambda pair: [w[:].rearrange("p k n -> p (k n)") for w in pair]
            blocks = [(io["war"], P, BLK, flat(war))]
            blocks += [(io["wb"][:, i * BLK:(i + 1) * BLK], P, BLK, [w[:, i * BLK:(i + 1) * BLK] for w in flat(wb)]) for i in range(2)]
            blocks += [(io["wup"], P, D, [w[:] for w in wup])]
            with nc.Block() as block:
                @block.sync
                def _(sp):
                    sp.dma_start(earlier[:], io["earlier"]).then_inc(small, 16)
                    block_loader(sp, blocks, raw, w_raw, w_low)

                @block.gpsimd
                def _(pool):
                    for n, (_, rows, cols, dst) in enumerate(blocks):
                        split_block(pool, n, rows, cols, dst, raw, w_raw, w_high, w_low)

                @block.tensor
                def _(pe):
                    tok = lambda t: slice(t * P, (t + 1) * P)
                    ln_tensor(pe, 1)
                    pe.wait_ge(w_low, 1)
                    for t in range(NT):
                        pe.wait_ge(ln_low, NT + t + 1)
                        if t >= 2:
                            pe.wait_ge(a_done, 2 * (t - 1))
                        product(bankA[t % 2][:, 0:256], [x for k in range(KC) for x in three([s[:, k, tok(t)] for s in xT], [w[:, k, :] for w in war])]).then_inc(a_ready, 1)

                    def dense(t):
                        if t >= 2:
                            pe.wait_ge(y_done, t - 1)
                        product(bankY[t % 2][:], [x for k in range(KC) for x in three([s[:, k, tok(t)] for s in xT], [w[:, k, :] for w in wb])], stop=False)

                    pe.wait_ge(w_low, 3)
                    dense(0)
                    dense(1)
                    pe.wait_ge(w_low, 4)
                    pe.wait_ge(route, 15)
                    for t in range(NT):
                        if t >= 2:
                            pe.wait_ge(m_low, t - 1)
                        nc.tensor.transpose(bankT[t % 2][:, 0:P], mid[:, t, :], ident[:]).then_inc(t_ready, 1)
                    
                        if t:
                            experts = t - 1
                            pe.wait_ge(m_low, experts + 1)
                            product(bankY[experts % 2][:], three([m[:, tok(experts)] for m in mT], [w[:] for w in wup]), start=False).then_inc(y_ready, 1)
                            if experts + 2 < NT:
                                dense(experts + 2)
                    pe.wait_ge(m_low, NT)
                    product(bankY[(NT - 1) % 2][:], three([m[:, tok(NT - 1)] for m in mT], [w[:] for w in wup]), start=False).then_inc(y_ready, 1)

                @block.scalar
                def _(act):
                    ln_scalar(act, 1)
                    for t in range(NT):
                        act.wait_ge(a_ready, t + 1)
                        nc.scalar.activation(mid[:, t, :], bankA[t % 2][:, 0:ER], ACT.Copy).then_inc(a_done, 1)
                        nc.scalar.activation(lg[:, t, :], bankA[t % 2][:, ER:ER + EXPERTS], ACT.Copy).then_inc(a_done, 1)
                    act.wait_ge(route, 2)
                    nc.scalar.activation(pr[:].rearrange("p t e -> p (t e)"), pr[:].rearrange("p t e -> p (t e)"), ACT.Exp).then_inc(route_exp, 1)
                    for t in range(NT):
                        act.wait_ge(t_ready, t + 1)
                        nc.scalar.activation(mT[0][:, t * P:(t + 1) * P], bankT[t % 2][:, 0:P], ACT.Copy).then_inc(m_high, 1)

                def add(dve, t):
                    dve.wait_ge(y_ready, t + 1)
                    nc.vector.tensor_tensor(xtok[:, t, :], xtok[:, t, :], bankY[t % 2][:], ALU.add).then_inc(y_done, 1)

                @block.vector
                def _(dve):
                    ln_vector(dve, 1)
                    wide = lambda v: v[:].unsqueeze(2).to_broadcast([P, NT, EXPERTS])
                    pairs = [P, NT, EXPERTS, EXPERTS]
                    steps = [0]

                    def step(ins):
                        ins.then_inc(route, 1)
                        steps[0] += 1
                        dve.wait_ge(route, steps[0])

                    dve.wait_ge(a_done, 2 * NT)
                    dve.wait_ge(small, 16)
                    step(nc.vector.tensor_reduce(top[:], lg[:], AXX, ALU.max))
                    nc.vector.tensor_tensor(pr[:], lg[:], wide(top), ALU.subtract).then_inc(route, 1)
                    steps[0] += 1
                    dve.wait_ge(route_exp, 1)
                    step(nc.vector.tensor_reduce(top[:], pr[:], AXX, ALU.add))
                    step(nc.vector.reciprocal(top[:], top[:]))
                    step(nc.vector.tensor_tensor(pr[:], pr[:], wide(top), ALU.mult))
                    other, own = pr[:].unsqueeze(2).to_broadcast(pairs), pr[:].unsqueeze(3).to_broadcast(pairs)
                    step(nc.vector.tensor_tensor(above[:], other, own, ALU.is_gt))
                    step(nc.vector.tensor_tensor(ties[:], other, own, ALU.is_equal))
                    step(nc.vector.tensor_tensor(ties[:].rearrange("p t a b -> p t (a b)"), ties[:].rearrange("p t a b -> p t (a b)"),
                                                 earlier[:].rearrange("p a b -> p (a b)").unsqueeze(1).to_broadcast([P, NT, EXPERTS * EXPERTS]), ALU.mult))
                    step(nc.vector.tensor_tensor(above[:], above[:], ties[:], ALU.add))
                    step(nc.vector.tensor_reduce(gate[:].rearrange("p t e -> p (t e)"), above[:].rearrange("p t a b -> p (t a) b"), AXX, ALU.add))
                    step(nc.vector.scalar_tensor_tensor(gate[:], gate[:], 2.0, pr[:], ALU.is_lt, ALU.mult))
                    step(nc.vector.tensor_reduce(top[:], gate[:], AXX, ALU.add))
                    step(nc.vector.reciprocal(top[:], top[:]))
                    step(nc.vector.scalar_tensor_tensor(gate[:], gate[:], 2.0, wide(top), ALU.mult, ALU.mult))
                    nc.vector.tensor_tensor(mid[:].rearrange("p t (e r) -> p t e r", e=EXPERTS), mid[:].rearrange("p t (e r) -> p t e r", e=EXPERTS),
                                            gate[:].unsqueeze(3).to_broadcast([P, NT, EXPERTS, RANK]), ALU.mult).then_inc(route, 1)
                    for t in range(NT):
                        dve.wait_ge(m_high, t + 1)
                        nc.vector.tensor_tensor(mT[1][:, t * P:(t + 1) * P], bankT[t % 2][:, 0:P], f32(mT[0][:, t * P:(t + 1) * P]), ALU.subtract).then_inc(m_low, 1)
                        if t:
                            add(dve, t - 1)
                    add(dve, NT - 1)
        if phases == 3:
            finish(2)
            return

    if phases >= 4:
        with ExitStack() as mem:
            causal = sb(mem, "causal", [P, P])
            loaded = sem("D_loaded")
            with nc.Block() as block:
                @block.sync
                def _(sp):
                    sp.dma_start(causal[:], io["causal"]).then_inc(loaded, 16)
                    sp.wait_ge(loaded, 16)
            grouped_attention("D", 2, io["w_attn1"], xT, None, lambda t: causal[:])
        if phases == 4:
            finish(3)
            return

    if phases >= 5:
        w_raw = [sem(f"E_raw{i}") for i in range(2)]; w_high = sem("E_whigh"); w_low = sem("E_wlow")
        small = sem("E_small"); a_ready = sem("E_aready"); q_done = sem("E_qdone"); s_ready = sem("E_sready"); st = softmax_stages("E")
        t_ready = sem("E_tready"); p_high = sem("E_phigh"); p_low = sem("E_plow"); y_ready = sem("E_yready"); y_done = sem("E_ydone")
        with ExitStack() as mem:
            raw = [sb(mem, f"Eraw{i}", [P, BLK]) for i in range(2)]
            w2 = [[sb(mem, f"Ew{a}{i}", [P, KC, KC, P], F32R) for i in range(2)] for a in range(2)]
            ft = [sb(mem, f"Eft{i}", [P, NT, D], F32R) for i in range(2)]
            qk = [sb(mem, f"Eqk{a}", [P, KC, TOK]) for a in range(2)]
            bias = sb(mem, "Ebias", [P, 2, KC]); same = sb(mem, "Esame", [P, P])
            sc = [sb(mem, f"Esc{i}", [P, 4, P]) for i in range(2)]
            pT = [sb(mem, f"EpT{i}", [P, NT, P], F32R) for i in range(2)]
            mx = sb(mem, "Emx", [P, 2, 4])
            blocks = []
            for a, name in enumerate(("wq2", "wk2")):
                fl = [w[:].rearrange("p m k n -> p (m k n)") for w in w2[a]]
                blocks += [(io[name][:, i * BLK:(i + 1) * BLK], P, BLK, [f[:, i * BLK:(i + 1) * BLK] for f in fl]) for i in range(2)]
            blocks += [(io["ctx_tok"][:, i * BLK:(i + 1) * BLK], P, BLK, [f[:].rearrange("p t n -> p (t n)")[:, i * BLK:(i + 1) * BLK] for f in ft]) for i in range(4)]
            with nc.Block() as block:
                @block.sync
                def _(sp):
                    sp.dma_start(bias[:], io["bias2"]).then_inc(small, 16)
                    sp.dma_start(same[:], io["same"]).then_inc(small, 16)
                    block_loader(sp, blocks, raw, w_raw, w_low)

                @block.gpsimd
                def _(pool):
                    for n, (_, rows, cols, dst) in enumerate(blocks):
                        split_block(pool, n, rows, cols, dst, raw, w_raw, w_high, w_low)

                @block.tensor
                def _(pe):
                    ln_tensor(pe, 3)
                    pe.wait_ge(ln_low, 4 * NT)
                    for n in range(16):
                        a, m, h = n // 8, n // 2 % 4, n % 2
                        if n % 4 == 0:
                            pe.wait_ge(w_low, n // 4 + 1)
                        if n >= 2:
                            pe.wait_ge(q_done, n - 1)
                        cols = slice(h * HALF, (h + 1) * HALF)
                        product(bankA[n % 2][:], [x for k in range(KC) for x in three([w[:, m, k, :] for w in w2[a]], [s[:, k, cols] for s in (xT, cT)[a]])]).then_inc(a_ready, 1)
                    pe.wait_ge(q_done, 16)
                    for t in range(NT):
                        tok = slice(t * P, (t + 1) * P)
                        done = product(bankA[t // 4][:, t % 4 * P:t % 4 * P + P], [(qk[0][:, m, tok], qk[1][:, m, tok]) for m in range(KC)])
                        if t % 4 == 3:
                            done.then_inc(s_ready, 1)
                    for u in range(2):
                        pe.wait_ge(st["prob"], u + 1)
                        for j in range(4):
                            done = nc.tensor.transpose(bankT[u][:, j * P:(j + 1) * P], sc[u][:, j, :], ident[:])
                        done.then_inc(t_ready, 1)
                    pe.wait_ge(w_low, 8)
                    for t in range(NT):
                        pe.wait_ge(p_low, t // 4 + 1)
                        if t >= 2:
                            pe.wait_ge(y_done, t - 1)
                        product(bankY[t % 2][:], three([p[:, t, :] for p in pT], [f[:, t, :] for f in ft])).then_inc(y_ready, 1)

                @block.scalar
                def _(act):
                    ln_scalar(act, 3)
                    act.wait_ge(small, 32)
                    for n in range(16):
                        a, m, h = n // 8, n // 2 % 4, n % 2
                        act.wait_ge(a_ready, n + 1)
                        nc.scalar.activation(qk[a][:, m, h * HALF:(h + 1) * HALF], bankA[n % 2][:], ACT.Identity, bias=bias[:, a, m:m + 1]).then_inc(q_done, 1)
                    for u in range(2):
                        act.wait_ge(st["sub"], u + 1)
                        fl = sc[u][:].rearrange("p t k -> p (t k)")
                        nc.scalar.activation(fl, fl, ACT.Exp, scale=D ** -0.5).then_inc(st["exp"], 1)
                    for u in range(2):
                        act.wait_ge(t_ready, u + 1)
                        nc.scalar.activation(pT[0][:, 4 * u:4 * u + 4, :].rearrange("p t k -> p (t k)"), bankT[u][:], ACT.Copy).then_inc(p_high, 1)

                @block.vector
                def _(dve):
                    ln_vector(dve, 3)
                    dve.wait_ge(small, 32)
                    wide = lambda u: mx[:, u, :].unsqueeze(2).to_broadcast([P, 4, P])
                    for u in range(2):
                        dve.wait_ge(s_ready, u + 1)
                        nc.vector.tensor_tensor(sc[u][:], bankA[u][:].rearrange("p (t k) -> p t k", t=4), same[:].unsqueeze(1).to_broadcast([P, 4, P]), ALU.min).then_inc(st["masked"], 1)
                        dve.wait_ge(st["masked"], u + 1)
                        nc.vector.tensor_reduce(mx[:, u, :], sc[u][:], AXX, ALU.max).then_inc(st["max"], 1)
                        dve.wait_ge(st["max"], u + 1)
                        nc.vector.tensor_tensor(sc[u][:], sc[u][:], wide(u), ALU.subtract).then_inc(st["sub"], 1)
                    for u in range(2):
                        dve.wait_ge(st["exp"], u + 1)
                        nc.vector.tensor_reduce(mx[:, u, :], sc[u][:], AXX, ALU.add).then_inc(st["sum"], 1)
                        dve.wait_ge(st["sum"], u + 1)
                        nc.vector.reciprocal(mx[:, u, :], mx[:, u, :]).then_inc(st["inv"], 1)
                        dve.wait_ge(st["inv"], u + 1)
                        nc.vector.tensor_tensor(sc[u][:], sc[u][:], wide(u), ALU.mult).then_inc(st["prob"], 1)
                    for u in range(2):
                        dve.wait_ge(p_high, u + 1)
                        part = [p[:, 4 * u:4 * u + 4, :].rearrange("p t k -> p (t k)") for p in pT]
                        nc.vector.tensor_tensor(part[1], bankT[u][:], f32(part[0]), ALU.subtract).then_inc(p_low, 1)
                    for t in range(NT):
                        dve.wait_ge(y_ready, t + 1)
                        nc.vector.tensor_tensor(xtok[:, t, :], xtok[:, t, :], bankY[t % 2][:], ALU.add).then_inc(y_done, 1)
        if phases == 5:
            finish(4)
            return
    cmem.close()

    if phases >= 6:
        FB = 512
        ZERO, STEP, LR = 7.5, 0.005, 0.02
        w_raw = [sem(f"F_raw{i}") for i in range(2)]; w_high = sem("F_whigh"); w_low = sem("F_wlow")
        small = sem("F_small"); lr_ready = sem("F_lrready"); lr_high = sem("F_lrhigh"); lr_low = sem("F_lrlow")
        gu_ready = sem("F_guready"); scaled = sem("F_scaled"); g_sum = sem("F_gsum"); u_sum = sem("F_usum"); act_done = sem("F_act")
        h_done = sem("F_h"); h_high = sem("F_hhigh"); h_low = sem("F_hlow"); d_ready = sem("F_dready")
        y_ready = sem("F_yready"); y_scaled = sem("F_yscaled"); y_sum = sem("F_ysum"); y_done = sem("F_ydone")
        NU = NI * 2
        with ExitStack() as mem:
            raw = [sb(mem, f"Fraw{i}", [P, FB]) for i in range(2)]
            wgu = [[sb(mem, f"Fwgu{i}{a}", [P, KC, P], F32R) for a in range(2)] for i in range(2)]
            wd = sb(mem, "Fwd", [P, NI, D], F32R)
            a_gu = [sb(mem, f"Fagu{i}", [P, KC, 2 * LR_RANK], F32R) for i in range(2)]
            b_gu = sb(mem, "Fbgu", [3 * LR_RANK, 2, NI * P], F32R)
            a_d = [sb(mem, f"Fad{i}", [P, NI, LR_RANK], F32R) for i in range(2)]
            b_d = sb(mem, "Fbd", [3 * LR_RANK, D], F32R)
            stack = [sb(mem, f"Fstack{i}", [3 * LR_RANK, TOK], F32R) for i in range(2)]
            hT = [sb(mem, f"FhT{i}", [P, NI, TOK], F32R) for i in range(2)]
            gs = [sb(mem, f"Fgs{i}", [P, HALF]) for i in range(2)]; us = [sb(mem, f"Fus{i}", [P, HALF]) for i in range(2)]
            scale = sb(mem, "Fscale", [P, 2, NI]); dscale = sb(mem, "Fdscale", [P, D])
            bgu_flat = b_gu[:].rearrange("p a n -> p (a n)")
            blocks = [(io["a_gu"], P, KC * 2 * LR_RANK, "split", [w[:].rearrange("p k n -> p (k n)") for w in a_gu])]
            for at in range(0, 2 * NI * P, FB):
                n = min(FB, 2 * NI * P - at)
                blocks.append((io["b_gu"][:, at:at + n], 3 * LR_RANK, n, "stack", bgu_flat[:, at:at + n]))
            first_gu = len(blocks)
            for i in range(NI):
                for a in range(2):
                    blocks.append((io["q_gu"][i, a].bitcast(F32), P, FB, "levels", wgu[i % 2][a][:].rearrange("p k n -> p (k n)")))
            first_d = len(blocks)
            blocks.append((io["a_d"], P, NI * LR_RANK, "split", [w[:].rearrange("p k n -> p (k n)") for w in a_d]))
            blocks.append((io["b_d"], 3 * LR_RANK, D, "stack", b_d[:]))
            blocks += [(io["q_d"][i].bitcast(F32), P, FB, "levels", wd[:, i, :]) for i in range(NI)]
            sets = [(bankA[0][:], bankA[1][:], bankY[0][:], bankY[1][:]), (bankT[0][:], bankT[1][:], bankO[:, 0, :], bankO[:, 1, :])]
            with nc.Block() as block:
                @block.sync
                def _(sp):
                    sp.dma_start(scale[:], io["gu_scale"]).then_inc(small, 16)
                    sp.dma_start(dscale[:], io["d_scale"].to_broadcast([P, D])).then_inc(small, 16)
                    block_loader(sp, blocks, raw, w_raw, w_low)

                @block.gpsimd
                def _(pool):
                    for n, (_, rows, cols, kind, dst) in enumerate(blocks):
                        src = raw[n % 2][0:rows, 0:cols]
                        if kind == "split":
                            split_block(pool, n, rows, cols, dst, raw, w_raw, w_high, w_low)
                        elif kind == "stack":
                            low = slice(2 * LR_RANK, 3 * LR_RANK)
                            pool.wait_ge(w_raw[n % 2], 16 * (n // 2 + 1))
                            high_part(dst, src).then_inc(w_high, 1)
                            pool.wait_ge(w_high, n + 1)
                            nc.gpsimd.tensor_tensor(dst[low], src[low], f32(dst[low]), ALU.subtract).then_inc(w_low, 1)
                            pool.wait_ge(w_low, n + 1)
                        else:
                            i = (n - first_gu) // 2
                            if n < first_d and i >= 2:
                                pool.wait_ge(gu_ready, 4 * (i - 1))
                            pool.wait_ge(w_raw[n % 2], 16 * (n // 2 + 1))
                            nc.gpsimd.tensor_scalar(dst, src.bitcast(I32), -ZERO, 1.0, ALU.add, ALU.mult).then_inc(w_low, 1)
                            pool.sem_inc(w_high, 1)

                @block.tensor
                def _(pe):
                    ln_tensor(pe, 4)
                    pe.wait_ge(ln_low, 5 * NT)
                    pe.wait_ge(w_low, 1)
                    for h in range(2):
                        cols = slice(h * HALF, (h + 1) * HALF)
                        product(bankT[h][0:2 * LR_RANK, :], [x for k in range(KC) for x in three([w[:, k, :] for w in a_gu], [s[:, k, cols] for s in xT])]).then_inc(lr_ready, 1)
                    for n in range(NU):
                        i, h = n // 2, n % 2
                        cols = slice(h * HALF, (h + 1) * HALF)
                        if h == 0:
                            pe.wait_ge(w_low, first_gu + 2 * i + 2)
                        if n == 0:
                            pe.wait_ge(lr_low, 4)
                        if n >= 2:
                            pe.wait_ge(g_sum, n - 1)
                            pe.wait_ge(u_sum, n - 1)
                        for a in range(2):
                            product(sets[h][a], [(wgu[i % 2][a][:, k, :], s[:, k, cols]) for k in range(KC) for s in xT])
                            nc.tensor.matmul(sets[h][2 + a], b_gu[:, a, i * P:(i + 1) * P], stack[a][:, cols], start=True, stop=True).then_inc(gu_ready, 1)
                    pe.wait_ge(w_low, first_d + 1)
                    pe.wait_ge(h_low, NU)
                    for h in range(2):
                        cols = slice(h * HALF, (h + 1) * HALF)
                        product(bankA[h][0:LR_RANK, :], [x for i in range(NI) for x in three([w[:, i, :] for w in a_d], [s[:, i, cols] for s in hT])]).then_inc(d_ready, 1)
                    pe.wait_ge(w_low, len(blocks))
                    for t in range(NT):
                        tok = slice(t * P, (t + 1) * P)
                        if t >= 2:
                            pe.wait_ge(y_sum, t - 1)
                        product(bankY[t % 2][:], [(s[:, i, tok], wd[:, i, :]) for i in range(NI) for s in hT])
                        if t == 0:
                            pe.wait_ge(lr_low, 6)
                        nc.tensor.matmul(bankT[t % 2][:], stack[0][:, tok], b_d[:], start=True, stop=True).then_inc(y_ready, 1)

                R0, R1, R2 = (slice(LR_RANK * i, LR_RANK * (i + 1)) for i in range(3))

                @block.scalar
                def _(act):
                    ln_scalar(act, 4)
                    act.wait_ge(small, 34)
                    for h in range(2):
                        cols = slice(h * HALF, (h + 1) * HALF)
                        act.wait_ge(lr_ready, h + 1)
                        for dst, src in ((stack[0][R0, cols], R0), (stack[0][R2, cols], R0), (stack[1][R1, cols], R1), (stack[1][R2, cols], R1)):
                            nc.scalar.activation(dst, bankT[h][src, :], ACT.Copy, scale=LR).then_inc(lr_high, 1)
                    for n in range(NU):
                        i, h = n // 2, n % 2
                        act.wait_ge(gu_ready, 2 * n + 1)
                        if n >= 2:
                            act.wait_ge(h_done, n - 1)
                        nc.scalar.activation(gs[h][:], sets[h][0], ACT.Copy, scale=scale[:, 0, i:i + 1]).then_inc(scaled, 1)
                        act.wait_ge(gu_ready, 2 * n + 2)
                        if n >= 2:
                            act.wait_ge(h_low, n - 1)
                        nc.scalar.activation(us[h][:], sets[h][3], ACT.Copy).then_inc(scaled, 1)
                        act.wait_ge(g_sum, n + 1)
                        nc.scalar.activation(gs[h][:], gs[h][:], ACT.Silu).then_inc(act_done, 1)
                        act.wait_ge(h_done, n + 1)
                        nc.scalar.activation(hT[0][:, i, h * HALF:(h + 1) * HALF], us[h][:], ACT.Copy).then_inc(h_high, 1)
                    for h in range(2):
                        cols = slice(h * HALF, (h + 1) * HALF)
                        act.wait_ge(d_ready, h + 1)
                        for dst in (R0, R2):
                            nc.scalar.activation(stack[0][dst, cols], bankA[h][R0, :], ACT.Copy, scale=LR).then_inc(lr_high, 1)

                @block.vector
                def _(dve):
                    ln_vector(dve, 4)
                    dve.wait_ge(small, 32)
                    nc.vector.tensor_scalar(scale[:], scale[:], STEP, None, ALU.mult).then_inc(small, 1)
                    nc.vector.tensor_scalar(dscale[:], dscale[:], STEP, None, ALU.mult).then_inc(small, 1)
                    dve.wait_ge(small, 34)
                    for h in range(2):
                        cols = slice(h * HALF, (h + 1) * HALF)
                        dve.wait_ge(lr_high, 4 * h + 4)
                        nc.vector.scalar_tensor_tensor(stack[0][R1, cols], bankT[h][R0, :], LR, f32(stack[0][R0, cols]), ALU.mult, ALU.subtract).then_inc(lr_low, 1)
                        nc.vector.scalar_tensor_tensor(stack[1][R0, cols], bankT[h][R1, :], LR, f32(stack[1][R1, cols]), ALU.mult, ALU.subtract).then_inc(lr_low, 1)
                    for n in range(NU):
                        i, h = n // 2, n % 2
                        dve.wait_ge(scaled, 2 * n + 1)
                        nc.vector.tensor_tensor(gs[h][:], gs[h][:], sets[h][2], ALU.add).then_inc(g_sum, 1)
                        dve.wait_ge(scaled, 2 * n + 2)
                        nc.vector.scalar_tensor_tensor(us[h][:], sets[h][1], scale[:, 1, i:i + 1], us[h][:], ALU.mult, ALU.add).then_inc(u_sum, 1)
                        dve.wait_ge(u_sum, n + 1)
                        dve.wait_ge(act_done, n + 1)
                        nc.vector.tensor_tensor(us[h][:], us[h][:], gs[h][:], ALU.mult).then_inc(h_done, 1)
                        dve.wait_ge(h_high, n + 1)
                        cols = slice(h * HALF, (h + 1) * HALF)
                        nc.vector.tensor_tensor(hT[1][:, i, cols], us[h][:], f32(hT[0][:, i, cols]), ALU.subtract).then_inc(h_low, 1)
                    for h in range(2):
                        cols = slice(h * HALF, (h + 1) * HALF)
                        dve.wait_ge(lr_high, 8 + 2 * h + 2)
                        nc.vector.scalar_tensor_tensor(stack[0][R1, cols], bankA[h][R0, :], LR, f32(stack[0][R0, cols]), ALU.mult, ALU.subtract).then_inc(lr_low, 1)
                    for t in range(NT):
                        dve.wait_ge(y_ready, t + 1)
                        nc.vector.tensor_tensor(gs[t % 2][:], bankY[t % 2][:], dscale[:], ALU.mult).then_inc(y_scaled, 1)
                        dve.wait_ge(y_scaled, t + 1)
                        nc.vector.tensor_tensor(gs[t % 2][:], gs[t % 2][:], bankT[t % 2][:], ALU.add).then_inc(y_sum, 1)
                        dve.wait_ge(y_sum, t + 1)
                        nc.vector.tensor_tensor(xtok[:, t, :], xtok[:, t, :], gs[t % 2][:], ALU.add).then_inc(y_done, 1)
        finish(5)
    ctx.close()


def layouts(i):
    def feat(w):
        return w.reshape(-1, P, w.shape[1]).transpose(1, 0, 2)

    a = {}
    a["x_tok"] = i["x"].reshape(NT, P, D).transpose(1, 0, 2)
    a["xT"] = feat(i["x"].reshape(TOK, D).T)
    a["ctxT"] = feat(i["ctx_4096"].reshape(TOK, D).T)
    a["ident"] = np.eye(P, dtype=np.float32)
    w, b = i["L0_attn_w_attn"], i["L0_attn_b_attn"]
    qk = np.stack([feat(w[:, 0:D]), feat(w[:, D:2 * D])], 1).reshape(P, 2, KC, KC, P)
    a["wqk"] = qk.transpose(3, 0, 1, 2, 4).reshape(KC, P, BLK)
    a["wv"] = feat(w[:, 2 * D:]).reshape(P, KC * D)
    a["wp"] = feat(i["L0_attn_w_proj"]).reshape(P, KC * D)
    a["bqk"] = b[:2 * D].reshape(2, KC, P).transpose(2, 0, 1)
    a["bv"] = b[2 * D:].reshape(1, D)
    a["bp"] = i["L0_attn_b_proj"].reshape(1, D)
    base = 2 ** (-2 ** (-(math.log2(NH) - 3)))
    slopes = (base ** np.arange(1, NH + 1, dtype=np.float32)).astype(np.float32)
    rel = (np.arange(S)[None, :] - np.arange(S)[:, None])
    bias = np.where(rel[None] <= 0, slopes[:, None, None] * rel[None].astype(np.float32), np.float32(OFF)).astype(np.float32)
    a["alibi"] = bias.reshape(NH // 2, 2 * S, S).transpose(1, 0, 2)
    even = (np.arange(P) % 32 < 16).astype(np.float32)
    a["parity"] = np.stack([even, 1 - even], 1)

    def attention_blocks(wq, wk, wv, wo):
        heads = lambda w: w.reshape(KC, P, -1, HD).transpose(1, 2, 0, 3)
        q, k, o = heads(wq), heads(wk), wo.reshape(NH, HD, D).transpose(1, 0, 2)
        v = wv.reshape(KC, P, NPAIR, 2 * HD).transpose(1, 2, 0, 3)
        turns = []
        for it in range(NPAIR):
            blocks = [k[:, 2 * it:2 * it + 2], v[:, it]]
            for j in range(2):
                h = (2 * it + j) * GROUP
                blocks += [q[:, h:h + 2], q[:, h + 2:h + 4], o[:, h:h + 2], o[:, h + 2:h + 4]]
            turns.append(np.stack([x.reshape(P, BLK) for x in blocks]))
        return np.stack(turns)

    a["w_attn0"] = attention_blocks(*(i["L0_xattn_W" + c] for c in "qkvo"))
    a["pos"] = i["pos_BxS2"].reshape(NT, P).T
    m = i["mask_BxSxS2_ik0"].transpose(1, 0, 2)
    a["mask"] = np.concatenate([m, m]).reshape(P, NT, P)
    inv = (1.0 / np.float32(10000.0) ** (np.arange(0, HD, 2, dtype=np.float32) / HD)).astype(np.float32)
    angle = np.arange(ROPE_ROWS, dtype=np.float32)[:, None] * inv[None]
    cos, sin = np.cos(angle).astype(np.float32), np.sin(angle).astype(np.float32)
    a["rope"] = np.concatenate([cos, cos, -sin, sin], 1)

    far = np.float32(-OFF)
    a["earlier"] = np.broadcast_to(np.tril(np.ones((EXPERTS, EXPERTS), np.float32), -1), (P, EXPERTS, EXPERTS))
    a["causal"] = np.tile(np.where(np.tril(np.ones((S, S))) > 0, far, -far).astype(np.float32), (2, 2))
    a["same"] = np.where(np.kron(np.eye(2), np.ones((S, S))) > 0, far, -far).astype(np.float32)
    down = i["L0_ffn_lora_A"].transpose(1, 0, 2).reshape(D, EXPERTS * RANK)
    war = np.concatenate([down, i["L0_ffn_router_W"].T, np.zeros((D, 256 - EXPERTS * RANK - EXPERTS), np.float32)], 1)
    a["war"] = feat(war).reshape(P, BLK)
    a["wb"] = feat(i["L0_ffn_base_W"].T).reshape(P, KC * D)
    a["wup"] = i["L0_ffn_lora_B"].reshape(EXPERTS * RANK, D)
    a["w_attn1"] = attention_blocks(*(i["L1_attn_w" + c].T for c in "qkvo"))
    for name in "qk":
        a["w" + name + "2"] = feat(i["L1_xattn_W" + name].T).reshape(P, KC, KC, P).transpose(0, 2, 1, 3).reshape(P, KC * D)
    a["ctx_tok"] = i["ctx_4096"].reshape(NT, P, D).transpose(1, 0, 2).reshape(P, NT * D)
    a["bias2"] = np.stack([i["L1_xattn_bq"], i["L1_xattn_bk"]]).reshape(2, KC, P).transpose(2, 0, 1)
    pad = NI * P - INNER
    grow = lambda w, axis: np.pad(w, [(0, pad if x == axis else 0) for x in range(w.ndim)])
    a["a_gu"] = feat(np.concatenate([i["L1_ffn_gate_A"], i["L1_ffn_up_A"]], 1)).reshape(P, KC * 2 * LR_RANK)
    bgu = np.concatenate([grow(i["L1_ffn_gate_B"], 1), grow(i["L1_ffn_up_B"], 1)], 1)
    a["b_gu"] = np.concatenate([bgu, bgu, bgu])
    q = np.stack([grow(i["L1_ffn_gate_q"], 0), grow(i["L1_ffn_up_q"], 0)])
    a["q_gu"] = q.reshape(2, NI, P, KC, P).transpose(1, 0, 4, 3, 2).reshape(NI, 2, P, KC * P)
    a["gu_scale"] = np.stack([grow(i["L1_ffn_gate_scale"], 0), grow(i["L1_ffn_up_scale"], 0)]).reshape(2, NI, P).transpose(2, 0, 1)
    a["a_d"] = grow(i["L1_ffn_down_A"], 0).reshape(NI, P, LR_RANK).transpose(1, 0, 2).reshape(P, NI * LR_RANK)
    a["b_d"] = np.concatenate([i["L1_ffn_down_B"]] * 3)
    a["q_d"] = grow(i["L1_ffn_down_q"], 1).T.reshape(NI, P, D)
    a["d_scale"] = i["L1_ffn_down_scale"].reshape(1, D)
    return {k: np.ascontiguousarray(v) for k, v in a.items()}


def kernel(**inputs):
    import concourse.bacc as _bacc
    from concourse.bass_utils import run_bass_kernel_spmd as _run

    nc = _bacc.Bacc("TRN2", target_bir_lowering=False, num_devices=1)
    arrays = layouts({k: np.asarray(v) for k, v in inputs.items()})
    io = {k: nc.dram_tensor("in_" + k, v.shape, mybir.dt.from_np(v.dtype), kind="ExternalInput").ap() for k, v in arrays.items()}
    io["out"] = nc.dram_tensor("out_dram", (P, NT, D), F32, kind="ExternalOutput").ap()
    build_program(nc, io)
    r = _run(nc, [{"in_" + k: v for k, v in arrays.items()}], core_ids=[0])
    return np.asarray(r.results[0]["out_dram"]).transpose(1, 0, 2).reshape(B, S, D)
```

```python
import math
from contextlib import ExitStack

import concourse.bass as bass
import numpy as np
from concourse import mybir

F32 = mybir.dt.float32
F32R = mybir.dt.float32r
I32 = mybir.dt.int32
U32 = mybir.dt.uint32
ALU = mybir.AluOpType
ACT = mybir.ActivationFunctionType
AXX = mybir.AxisListType.X

P = 128
B, S, D = 16, 64, 512
TOK = B * S
NT = TOK // P
KC = D // P
HALF = TOK // 2
NH, HD = 32, 128
KVH = 8
GROUP = NH // KVH
NPAIR = KVH // 2
A_HD = D // NH
WINDOW = S + TOK + S
EXPERTS, RANK = 8, 16
INNER, LR_RANK = 1376, 32
NI = -(-INNER // P)
EPS = 1e-5
OFF = -3.0e38
ROPE_ROWS = 512
BLK = 1024
NRAW = 2


def f32(ap):
    return ap.bitcast(F32)


def build_program(nc, io, phases=9):
    ctx = ExitStack()

    def sb(stack, name, shape, dt=F32):
        return stack.enter_context(nc.sbuf_tensor("sb_" + name, shape, dt))

    def sem(name):
        return ctx.enter_context(nc.semaphore(name))

    xtok = sb(ctx, "xtok", [P, NT, D])
    xT = [sb(ctx, f"xT{i}", [P, KC, TOK], F32R) for i in range(2)]
    ident = sb(ctx, "ident", [P, P])
    zero = sb(ctx, "zero", [P, 1])
    bankA = [ctx.enter_context(nc.psum_tensor(f"bankA{i}", [P, 512], F32)) for i in range(2)]
    bankT = [ctx.enter_context(nc.psum_tensor(f"bankT{i}", [P, 512], F32)) for i in range(2)]
    bankY = [ctx.enter_context(nc.psum_tensor(f"bankY{i}", [P, 512], F32)) for i in range(2)]
    bankO = ctx.enter_context(nc.psum_tensor("bankO", [P, 2, 512], F32))

    def high_part(dst, src):
        return nc.gpsimd.tensor_tensor(dst, src, zero[0:src.shape[0]].to_broadcast([src.shape[0], src.shape[1]]), ALU.add)

    def product(out, pairs, start=True, stop=True):
        for i, (lhs, rhs) in enumerate(pairs):
            last = nc.tensor.matmul(out, lhs, rhs, start=start and i == 0, stop=stop and i == len(pairs) - 1)
        return last

    def three(lhs, rhs):
        return [(lhs[0], rhs[0]), (lhs[0], rhs[1]), (lhs[1], rhs[0])]

    def window(kt, b, *lead):
        at = S + b * S - (S if b % 2 == 0 else 0)
        return kt[(*lead, slice(at, at + P))]

    ln_stat = sem("ln_stat"); ln_mean = sem("ln_mean"); ln_sqrt = sem("ln_sqrt"); ln_rstd = sem("ln_rstd")
    ln_norm = sem("ln_norm"); ln_tr = sem("ln_tr"); ln_high = sem("ln_high"); ln_low = sem("ln_low"); out_done = sem("out_done")
    stats = sb(ctx, "ln_stats", [P, NT, 6])
    moments = sb(ctx, "ln_moments", [P, NT, 2])
    rstd = sb(ctx, "ln_rstd", [P, NT])
    epsilon = sb(ctx, "ln_epsilon", [P, 1])
    ln_banks = [bankT[0], bankT[1], bankY[0], bankY[1]]

    def ln_statistics(dve, n, t):
        nc.vector.bn_stats(stats[:, t, :], xtok[:, t, :]).then_inc(ln_stat, 1)
        dve.wait_ge(ln_stat, n * NT + t + 1)
        nc.vector.bn_aggr(moments[:, t, :], stats[:, t, :]).then_inc(ln_mean, 1)

    def ln_vector(dve, n, transposed=True):
        dve.wait_ge(ln_sqrt, n + 1)
        nc.vector.reciprocal(rstd[:], rstd[:]).then_inc(ln_rstd, 1)
        dve.wait_ge(ln_rstd, n + 1)
        for t in range(NT + 2):
            if t < NT:
                nc.vector.tensor_scalar(xtok[:, t, :], xtok[:, t, :], moments[:, t, 0:1], rstd[:, t:t + 1],
                                        ALU.subtract, ALU.mult).then_inc(ln_norm, 1)
            if transposed and t >= 2:
                at = slice((t - 2) * P, (t - 1) * P)
                dve.wait_ge(ln_high, n * NT + t - 1)
                nc.vector.tensor_tensor(xT[1][:, :, at], ln_banks[(t - 2) % 4][:].rearrange("p (k c) -> p k c", k=KC),
                                        f32(xT[0][:, :, at]), ALU.subtract).then_inc(ln_low, 1)

    def ln_scalar(act, n, transposed=True):
        act.wait_ge(ln_mean, (n + 1) * NT)
        nc.scalar.activation(rstd[:], moments[:, :, 1], ACT.Sqrt, bias=epsilon[:]).then_inc(ln_sqrt, 1)
        if transposed:
            for t in range(NT):
                act.wait_ge(ln_tr, n * NT + t + 1)
                nc.scalar.activation(xT[0][:, :, t * P:(t + 1) * P],
                                     ln_banks[t % 4][:].rearrange("p (k c) -> p k c", k=KC), ACT.Copy).then_inc(ln_high, 1)

    def ln_tensor(pe, n):
        for t in range(NT):
            pe.wait_ge(ln_norm, n * NT + t + 1)
            if t >= 4:
                pe.wait_ge(ln_low, n * NT + t - 3)
            for k in range(KC):
                done = nc.tensor.transpose(ln_banks[t % 4][:, k * P:(k + 1) * P], xtok[:, t, k * P:(k + 1) * P], ident[:])
            done.then_inc(ln_tr, 1)

    def finish(n):
        with nc.Block() as block:
            @block.vector
            def _(dve):
                ln_vector(dve, n, transposed=False)

            @block.scalar
            def _(act):
                ln_scalar(act, n, transposed=False)

            @block.sync
            def _(sp):
                for t in range(NT):
                    sp.wait_ge(ln_norm, n * NT + t + 1)
                    sp.dma_start(io["out"][:, t, :], xtok[:, t, :]).then_inc(out_done, 16)
                sp.wait_ge(out_done, NT * 16)

    cmem = ExitStack()
    cT = [sb(cmem, f"cT{i}", [P, KC, TOK], F32R) for i in range(2)]

    def softmax_stages(tag):
        return {k: sem(f"{tag}_{k}") for k in ("masked", "max", "sub", "exp", "sum", "inv", "prob")}

    def in_turns(*steps):
        steps = [s for s in steps if s]
        while steps:
            steps = [s for s in steps if next(s, steps) is not steps]

    QUADS = B // 4
    PER_CHUNK = QUADS * 4
    UNITS = KC * PER_CHUNK
    HEADS = NH // KC
    OUTPUT_AT = UNITS - PER_CHUNK + 6
    AHEAD = 3
    v_raw = [sem(f"A_vraw{k}") for k in range(KC)]; w_raw = [sem(f"A_raw{i}") for i in range(NRAW)]
    w_high = sem("A_whigh"); w_low = sem("A_wlow"); zeroed = sem("A_zeroed")
    in_xT = [sem(f"A_inxT{k}") for k in range(KC)]; in_high = sem("A_inhigh"); in_low = sem("A_inlow"); in_tok = sem("A_intok")
    clamped = sem("A_clamped"); gathered = sem("A_gathered"); small = sem("A_small"); pbias = sem("A_pbias")
    a_ready = sem("A_aready"); v_done = sem("A_vdone"); q_done = sem("A_qdone"); k_done = sem("A_kdone"); m_done = sem("A_mdone")
    s_ready = sem("A_sready"); st = softmax_stages("A")
    t_ready = sem("A_tready"); pt_done = sem("A_ptdone"); o_ready = sem("A_oready")
    o_even = sem("A_oeven"); o_odd = sem("A_oodd"); o_high = sem("A_ohigh"); o_low = sem("A_olow")
    y_ready = sem("A_yready"); y_done = sem("A_ydone")
    with ExitStack() as mem:
        with ExitStack() as early:
            table_rows = sb(early, "table_rows", [P, NT, 2 * P])
        wqk = [sb(mem, f"Awqk{i}", [P, 2, KC, P], F32R) for i in range(2)]
        raw = [sb(mem, f"Araw{i}", [P, BLK]) for i in range(NRAW)]
        wbig = [sb(mem, f"Awbig{i}", [P, KC, D], F32R) for i in range(2)]
        V = sb(mem, "AV", [P, NT, D])
        q = sb(mem, "Aq", [P, TOK])
        qm = [sb(mem, f"Aqm{i}", [P, 4, HEADS, S]) for i in range(2)]
        kt = [sb(mem, f"Akt{i}", [P, WINDOW]) for i in range(2)]
        with ExitStack() as early:
            rawx = sb(early, "rawx", [P, KC, TOK])
            rawv = sb(early, "rawv", [P, KC, D])
        oT = [sb(mem, f"AoT{i}", [P, KC, TOK], F32R) for i in range(2)]
        ring = [rawv[:, k, :] for k in range(KC)]
        alibi = sb(mem, "Aalibi", [P, NH // 2, P])
        bqk = sb(mem, "Abqk", [P, 2, KC]); bp = sb(mem, "Abp", [P, D])
        pos = sb(mem, "Apos", [P, NT], I32); row = sb(mem, "Arow", [P, NT], U32)
        parity = sb(mem, "Aparity", [P, 2])
        own = sb(mem, "Aown", [P, HEADS])
        with ExitStack() as early:
            bv = sb(early, "Abv", [P, D])
        sc = [sb(mem, f"Asc{i}", [P, 2, 2, S]) for i in range(3)]
        pt = [sb(mem, f"Apt{i}", [P, 2, P]) for i in range(2)]
        mx = sb(mem, "Amx", [P, 2, 4]); sm = sb(mem, "Asm", [P, 2, 4]); ri = sb(mem, "Ari", [P, 2, 4])
        oc = sb(mem, "Aoc", [P, 2, 2, S]); od = sb(mem, "Aod", [P, 2, 2, S])
        vbank = [bankY[0][:], bankY[1][:], bankA[0][:], bankA[1][:], bankT[0][:], bankT[1][:], bankO[:, 0, :], bankO[:, 1, :]]
        flat = lambda ws: [w[:].rearrange("p k n -> p (k n)") for w in ws]
        blocks = [(io["wv"][:, k * D:(k + 1) * D], [w[:, k, :] for w in wbig]) for k in range(KC)]
        blocks += [(io["wqk"][c, a], [w[:, a].rearrange("p k n -> p (k n)") for w in wqk]) for c in range(KC) for a in range(2)]
        blocks += [(io["wp"][:, i * BLK:(i + 1) * BLK], [w[:, i * BLK:(i + 1) * BLK] for w in flat(wbig)]) for i in range(2)]
        blocks += [(io["ctxT"][:, k, :], [c[:, k, :] for c in cT]) for k in range(KC)]
        ring += [raw[(n - KC) % NRAW][:, 0:blocks[n][0].shape[1]] for n in range(KC, len(blocks))]
        banks_before = lambda c, i: NT + 4 * c + i

        def slot(n):
            return n // PER_CHUNK, n // 4 % QUADS, n % 4

        with nc.Block() as block:
            @block.sync
            def _(sp):
                for n, (src, dst) in enumerate(blocks):
                    if n < KC:
                        sp.dma_start(rawx[:, n, :], io["xT"][:, n, :]).then_inc(in_xT[n], 16)
                    if n >= KC + NRAW:
                        sp.wait_ge(w_low, n - NRAW + 1)
                    sp.dma_start(ring[n], src).then_inc(v_raw[n] if n < KC else w_raw[n % NRAW], 16)
                    if n == KC:
                        for dst, name in ((pos, "pos"), (bqk, "bqk"), (parity, "parity"), (own, "own"), (alibi, "alibi"), (ident, "ident")):
                            sp.dma_start(dst[:], io[name]).then_inc(small, 16)
                        for dst, name in ((bv, "bv"), (bp, "bp")):
                            sp.dma_start(dst[:], io[name].to_broadcast([P, D])).then_inc(small, 16)
                        sp.dma_start(xtok[:], io["x_tok"]).then_inc(in_tok, 16)

            @block.gpsimd
            def _(pool):
                nc.gpsimd.memset(zero[:], 0.0).then_inc(zeroed, 1)
                nc.gpsimd.memset(epsilon[:], EPS).then_inc(zeroed, 1)
                pool.wait_ge(zeroed, 2)
                for n, (_, dst) in enumerate(blocks):
                    if n < KC:
                        pool.wait_ge(v_raw[n], 16)
                    else:
                        pool.wait_ge(w_raw[n % NRAW], 16 * ((n - KC) // NRAW + 1))
                    if KC + 2 <= n < 3 * KC:
                        c, a = (n - KC) // 2, (n - KC) % 2
                        pool.wait_ge(a_ready, banks_before(c - 1, 3 + a))
                    high_part(dst[0], ring[n]).then_inc(w_high, 1)
                    pool.wait_ge(w_high, n + 1)
                    nc.gpsimd.tensor_tensor(dst[1], ring[n], f32(dst[0]), ALU.subtract).then_inc(w_low, 1)
                    if n == KC - 1:
                        for k in kt:
                            nc.gpsimd.memset(k[:], 0.0).then_inc(zeroed, 1)
                    if n == KC + 3:
                        pool.wait_ge(small, 128)
                        pool.wait_ge(in_tok, 16)
                        for t in range(NT):
                            nc.gpsimd.tensor_tensor(xtok[:, t, :], xtok[:, t, :], bp[:], ALU.add).then_inc(pbias, 1)
                pool.wait_ge(clamped, 1)
                pool.wait_ge(a_ready, banks_before(KC, 0))
                for t in range(NT):
                    nc.gpsimd.indirect_dma_start(out=table_rows[:, t, :], out_offset=None, in_=io["rope"],
                                                 in_offset=bass.IndirectOffsetOnAxis(ap=row[:, t:t + 1], axis=0)).then_inc(gathered, 16)

            @block.tensor
            def _(pe):
                for k in range(KC):
                    pe.wait_ge(w_low, k + 1)
                    pe.wait_ge(in_low, k + 1)
                    for t in range(NT):
                        done = product(vbank[t], three([w[:, k, t * P:(t + 1) * P] for w in xT], [w[:, k, :] for w in wbig]), start=k == 0, stop=k == KC - 1)
                        if k == KC - 1:
                            done.then_inc(a_ready, 1)

                def project(c, i, chunks):
                    a, h = i % 2, i // 2
                    if 0 in chunks:
                        if h == 0:
                            pe.wait_ge(w_low, KC + 2 * c + a + 1)
                        if c == 0 and h == 0:
                            pe.wait_ge(v_done, a + 1)
                        else:
                            pe.wait_ge((k_done, q_done)[a], 2 * c + h)
                    cols = slice(h * HALF, (h + 1) * HALF)
                    done = product(bankY[a][:], [x for k in chunks for x in three([w[:, a, k, :] for w in wqk], [w[:, k, cols] for w in xT])],
                                   start=0 in chunks, stop=KC - 1 in chunks)
                    if KC - 1 in chunks:
                        done.then_inc(a_ready, 1)

                def scores(n):
                    c, quad, m = slot(n)
                    if n == 0:
                        pe.wait_ge(v_done, 4)
                    if n % PER_CHUNK == 0:
                        pe.wait_ge(k_done, 2 * (c + 1))
                    if m == 0:
                        pe.wait_ge(m_done, HEADS * (n // 4 + 1))
                    if n >= 2:
                        pe.wait_ge(st["masked"], n - 1)
                    for j in range(4):
                        done = nc.tensor.matmul(bankA[n % 2][:, j * P:(j + 1) * P], qm[quad % 2][:, j, 2 * m:2 * m + 2, :].rearrange("p e q -> p (e q)"),
                                                window(kt[c % 2], quad * 4 + j, slice(None)), start=True, stop=True)
                    done.then_inc(s_ready, 1)

                def output(t, half):
                    if t == 0 and half == 0:
                        pe.wait_ge(w_low, 3 * KC + 2)
                        pe.wait_ge(k_done, 2 * KC)
                        pe.wait_ge(q_done, 2 * KC)
                    if half == 0:
                        pe.wait_ge(o_low, 3 * QUADS + t // 2 + 1)
                        if t >= 2:
                            pe.wait_ge(y_done, t - 1)
                    done = product(bankY[t % 2][:], [x for k in (2 * half, 2 * half + 1) for x in three([w[:, k, t * P:(t + 1) * P] for w in oT], [w[:, k, :] for w in wbig])],
                                   start=half == 0, stop=half == 1)
                    if half:
                        done.then_inc(y_ready, 1)

                for i in range(4):
                    project(0, i, range(KC))
                for n in range(AHEAD):
                    scores(n)
                pe.wait_ge(small, 128)
                pe.wait_ge(v_done, NT)
                for n in range(UNITS):
                    c, quad, m = slot(n)
                    pe.wait_ge(st["prob"], n + 1)
                    if n >= 2:
                        pe.wait_ge(pt_done, n - 1)
                    for j in range(2):
                        done = nc.tensor.transpose(bankT[n % 2][:, j * P:(j + 1) * P], sc[n % 3][:, j].rearrange("p b k -> p (b k)"), ident[:])
                    done.then_inc(t_ready, 1)
                    if n + AHEAD < UNITS:
                        scores(n + AHEAD)
                    if c + 1 < KC:
                        project(c + 1, n // 4 % 4, [n % 4])
                    if n >= OUTPUT_AT:
                        output((n - OUTPUT_AT) // 2, n % 2)
                    pe.wait_ge(pt_done, n + 1)
                    if m == 0 and n:
                        pe.wait_ge(o_even, n // 2)
                        pe.wait_ge(o_odd, n // 2)
                    for j in range(4):
                        b, par, bpair = quad * 4 + j, j % 2, j // 2
                        rows = slice(S * par, S * par + S)
                        done = nc.tensor.matmul(bankO[32 * m:32 * m + 32, par, bpair * P:(bpair + 1) * P],
                                                V[rows, b // 2, c * P + 32 * m:c * P + 32 * m + 32], pt[n % 2][rows, bpair, :], start=True, stop=True)
                    done.then_inc(o_ready, 1)
                for t in range((UNITS - OUTPUT_AT) // 2, NT):
                    output(t, 0)
                    output(t, 1)

            @block.scalar
            def _(act):
                for k in range(KC):
                    act.wait_ge(in_xT[k], 16)
                    nc.scalar.activation(xT[0][:, k, :], rawx[:, k, :], ACT.Copy).then_inc(in_high, 1)

                def drain(c, i):
                    h, half = i // 2, slice(i // 2 * HALF, (i // 2 + 1) * HALF)
                    act.wait_ge(a_ready, banks_before(c, i) + 1)
                    if i % 2 == 0:
                        if c >= 2:
                            act.wait_ge(s_ready, PER_CHUNK * (c - 1))
                        nc.scalar.activation(kt[c % 2][:, S + half.start:S + half.stop], bankY[0][:], ACT.Identity, bias=bqk[:, 1, c:c + 1]).then_inc(k_done, 1)
                    else:
                        if c:
                            act.wait_ge(m_done, HEADS * (4 * c - 2 + 2 * h))
                        nc.scalar.activation(q[:, half], bankY[1][:], ACT.Identity, bias=bqk[:, 0, c:c + 1]).then_inc(q_done, 1)

                def by_head(step):
                    g, part = step // 4, step % 4
                    if part == 0:
                        act.wait_ge(q_done, g // 2 + 1)
                        if g >= 2:
                            act.wait_ge(s_ready, 4 * (g - 1))
                    for e in (2 * part, 2 * part + 1):
                        nc.scalar.activation(qm[g % 2][:, :, e, :], q[:, g % QUADS * 256:(g % QUADS + 1) * 256].rearrange("p (b s) -> p b s", s=S),
                                             ACT.Copy, scale=own[:, e:e + 1]).then_inc(m_done, 1)

                def exp(n):
                    act.wait_ge(st["sub"], n + 1)
                    tile = sc[n % 3][:].rearrange("p a b k -> p (a b k)")
                    nc.scalar.activation(tile, tile, ACT.Exp).then_inc(st["exp"], 1)

                def split(g):
                    c, quad = g // QUADS, g % QUADS
                    act.wait_ge(o_odd, 2 * (g + 1))
                    nc.scalar.activation(oT[0][:, c, quad * 256:(quad + 1) * 256], od[:].rearrange("p a b k -> p (a b k)"), ACT.Copy).then_inc(o_high, 1)

                act.wait_ge(small, 128)
                act.wait_ge(zeroed, 4)
                for i in range(4):
                    drain(0, i)
                    if i == 1:
                        for step in range(4):
                            by_head(step)
                for step in range(4, 7):
                    by_head(step)
                exp(0)
                exp(1)
                for n in range(UNITS):
                    act.wait_ge(t_ready, n + 1)
                    if n >= 2:
                        act.wait_ge(o_ready, n - 1)
                    nc.scalar.activation(pt[n % 2][:].rearrange("p a b -> p (a b)"), bankT[n % 2][:, 0:256], ACT.Copy).then_inc(pt_done, 1)
                    if n % 4 == 0 and n:
                        if n <= UNITS - PER_CHUNK:
                            drain((n + 12) // PER_CHUNK, (n // 4 - 1) % 4)
                        split(n // 4 - 1)
                    if n + 2 < UNITS:
                        exp(n + 2)
                    if n + 7 < UNITS:
                        by_head(n + 7)
                split(UNITS // 4 - 1)

            @block.vector
            def _(dve):
                for k in range(KC):
                    dve.wait_ge(in_high, k + 1)
                    nc.vector.tensor_tensor(xT[1][:, k, :], rawx[:, k, :], f32(xT[0][:, k, :]), ALU.subtract).then_inc(in_low, 1)

                def values(t):
                    dve.wait_ge(a_ready, t + 1)
                    nc.vector.tensor_tensor(V[:, t, :], vbank[t], bv[:], ALU.add).then_inc(v_done, 1)

                def front(n):
                    c, quad, m = slot(n)
                    s4 = sc[n % 3][:].rearrange("p a b k -> p (a b) k")
                    dve.wait_ge(s_ready, n + 1)
                    if n >= 3:
                        dve.wait_ge(t_ready, n - 2)
                    nc.vector.scalar_tensor_tensor(sc[n % 3][:].rearrange("p a b k -> p a (b k)"), bankA[n % 2][:].rearrange("p (a c) -> p a c", a=2)[:, :, S:S + P], 1.0 / A_HD,
                                                   alibi[:, c * 4 + m, :].unsqueeze(1).to_broadcast([P, 2, P]), ALU.mult, ALU.add).then_inc(st["masked"], 1)
                    yield
                    dve.wait_ge(st["masked"], n + 1)
                    nc.vector.tensor_reduce(mx[:, n % 2, :], s4, AXX, ALU.max).then_inc(st["max"], 1)
                    yield
                    dve.wait_ge(st["max"], n + 1)
                    nc.vector.tensor_tensor(s4, s4, mx[:, n % 2, :].unsqueeze(2).to_broadcast([P, 4, S]), ALU.subtract).then_inc(st["sub"], 1)

                def back(n):
                    s4 = sc[n % 3][:].rearrange("p a b k -> p (a b) k")
                    dve.wait_ge(st["exp"], n + 1)
                    nc.vector.tensor_reduce(sm[:, n % 2, :], s4, AXX, ALU.add).then_inc(st["sum"], 1)
                    yield
                    dve.wait_ge(st["sum"], n + 1)
                    nc.vector.reciprocal(ri[:, n % 2, :], sm[:, n % 2, :]).then_inc(st["inv"], 1)
                    yield
                    dve.wait_ge(st["inv"], n + 1)
                    nc.vector.tensor_tensor(s4, s4, ri[:, n % 2, :].unsqueeze(2).to_broadcast([P, 4, S]), ALU.mult).then_inc(st["prob"], 1)

                def gather(g):
                    dve.wait_ge(o_ready, 4 * g + 4)
                    for par in range(2):
                        nc.vector.tensor_scalar(oc[:, :, par, :], bankO[:, par, 0:256].rearrange("p (a c) -> p a c", a=2)[:, :, 0:S],
                                                parity[:, 0:1], None, ALU.mult).then_inc(o_even, 1)
                    yield
                    dve.wait_ge(o_even, 2 * g + 2)
                    if g:
                        dve.wait_ge(o_low, g)
                    for par in range(2):
                        nc.vector.scalar_tensor_tensor(od[:, :, par, :], bankO[:, par, 0:256].rearrange("p (a c) -> p a c", a=2)[:, :, S:P],
                                                       parity[:, 1:2], oc[:, :, par, :], ALU.mult, ALU.add).then_inc(o_odd, 1)

                def low(g):
                    c, cols = g // QUADS, slice(g % QUADS * 256, (g % QUADS + 1) * 256)
                    dve.wait_ge(o_high, g + 1)
                    nc.vector.tensor_tensor(oT[1][:, c, cols], od[:].rearrange("p a b k -> p (a b k)"), f32(oT[0][:, c, cols]), ALU.subtract).then_inc(o_low, 1)

                def residual(t):
                    dve.wait_ge(y_ready, t + 1)
                    dve.wait_ge(pbias, t + 1)
                    nc.vector.tensor_tensor(xtok[:, t, :], xtok[:, t, :], bankY[t % 2][:], ALU.add).then_inc(y_done, 1)
                    dve.wait_ge(y_done, t + 1)
                    ln_statistics(dve, 0, t)

                dve.wait_ge(small, 128)
                nc.vector.tensor_scalar(row[:], pos[:], 0, ROPE_ROWS - 1, ALU.max, ALU.min).then_inc(clamped, 1)
                for t in range(NT):
                    values(t)
                dve.wait_ge(v_done, NT)
                in_turns(front(0))
                in_turns(front(1), back(0))
                for n in range(UNITS):
                    in_turns(gather(n // 4 - 1) if n % 4 == 0 and n else None, front(n + 2) if n + 2 < UNITS else None, back(n + 1) if n + 1 < UNITS else None)
                    if n % 4 == 1 and n > 4:
                        low(n // 4 - 1)
                    if n > OUTPUT_AT and n % 2:
                        residual((n - OUTPUT_AT) // 2)
                in_turns(gather(UNITS // 4 - 1))
                low(UNITS // 4 - 1)
                for t in range((UNITS - OUTPUT_AT) // 2, NT):
                    residual(t)
    if phases == 1:
        finish(0)
        return
    SLOTS = 2 * NT
    KEYS_AT = SLOTS - 3
    VALUES_AT = {10: 4, 12: 5, 14: 6, 15: 7}

    def slot_banks(u, final):
        banks = []
        if u + 2 < SLOTS or not final:
            banks.append(("S", u + 2))
        if u in VALUES_AT and not final:
            banks.append(("V", VALUES_AT[u]))
        if u + 6 < SLOTS or not final:
            banks.append(("Q", u + 6))
        if u == KEYS_AT and not final:
            banks += [("K", n) for n in range(4, 8)]
        return banks

    def late(u):
        return u % 4 == 2

    START = [("V", n) for n in range(4)] + [("K", n) for n in range(4)] + [("Q", n) for n in range(4)] + [("S", 0), ("Q", 4), ("S", 1), ("Q", 5)]
    TURN = [x for u in range(SLOTS) for x in slot_banks(u, False)]
    LAST = [x for u in range(SLOTS) for x in slot_banks(u, True)]
    only_qk = lambda order: [x for x in order if x[0] in "QK"]
    TURN_BANKS, TURN_QK = len(TURN), len(only_qk(TURN))
    START_BLOCKS = ["v", "k", "q0", "q1"]
    TURN_BLOCKS = ["o0", "o1", "q0", "q1", "k", "v", "o2", "o3", "q2", "q3"]
    LAST_BLOCKS = ["o0", "o1", "q0", "q1", "o2", "o3"]

    class Part:
        def __init__(self, it, order, blocks):
            started = order is not START
            self.it, self.order, self.blocks, self.final = it, order, blocks, order is LAST
            self.banks, self.qks, self.weights = it * TURN_BANKS, it * TURN_QK, it * len(TURN_BLOCKS)
            if started:
                self.banks, self.qks, self.weights = self.banks + len(START), self.qks + len(only_qk(START)), self.weights + len(START_BLOCKS)

        def bank(self, x):
            return self.banks + (self.order.index(x) if x in self.order else -1)

        def qk(self, x):
            return self.qks + (only_qk(self.order).index(x) if x in self.order else -1)

        def buffer(self, x):
            return (self.order.index(x) if x in self.order else -1) % 2

        def swap(self, x):
            return (only_qk(self.order).index(x) if x in self.order else -1) % 2

        def block(self, name):
            return self.weights + self.blocks.index(name) + 1

        def unit(self, u):
            return self.it * SLOTS + u

    assert not any(len(x) % 2 for x in (START, TURN, LAST, START_BLOCKS, TURN_BLOCKS, LAST_BLOCKS))
    group_names = ("w_high", "w_low", "padded", "a_ready", "swapped", "roped", "turned", "qk_done", "v_done",
                   "t_ready", "pt_done", "o_ready", "o_high", "o_low", "wo_used", "y_ready", "y_done")
    group_sems = [[sem("G_raw0"), sem("G_raw1")], softmax_stages("G")] + [sem("G_" + name) for name in group_names]
    tabled = sem("G_tabled"); flipped = sem("G_flipped"); bounded = sem("G_bounded"); in_bound = sem("G_inbound")

    def grouped_attention(tag, norm, first, source, rope):
        w_raw, st, w_high, w_low, padded, a_ready, swapped, roped, turned, qk_done, v_done, \
            t_ready, pt_done, o_ready, o_high, o_low, wo_used, y_ready, y_done = group_sems
        final = first + NPAIR - 1
        with ExitStack() as mem:
            with ExitStack() as early:
                sb(early, f"{tag}rows", [P, NT, 2 * P])
                mask = sb(early, f"{tag}mask", [P, NT, P], I32); hidden = sb(early, f"{tag}hidden", [P, NT, P])
            qT = sb(mem, f"{tag}qT", [P, B, GROUP, S])
            raw = [sb(mem, f"{tag}raw{i}", [P, BLK]) for i in range(2)]
            wk = [sb(mem, f"{tag}wk{i}", [P, 2, KC, HD], F32R) for i in range(2)]
            wv = [sb(mem, f"{tag}wv{i}", [P, KC, 2 * HD], F32R) for i in range(2)]
            wq = [sb(mem, f"{tag}wq{i}", [P, GROUP, KC, HD], F32R) for i in range(2)]
            wo = [sb(mem, f"{tag}wo{i}", [P, GROUP, D], F32R) for i in range(2)]
            kt = sb(mem, f"{tag}kt", [P, 2, WINDOW])
            V = sb(mem, f"{tag}V", [P, NT, 2 * HD])
            sc = [sb(mem, f"{tag}sc{i}", [P, 2, 2, S]) for i in range(4)]
            pt = [sb(mem, f"{tag}pt{i}", [P, GROUP * S]) for i in range(2)]
            oT = [[sb(mem, f"{tag}oT{i}{p}", [P, GROUP, 2, S], F32R) for p in range(2)] for i in range(2)]
            mx = sb(mem, f"{tag}mx", [P, 2, 4]); sm = sb(mem, f"{tag}sm", [P, 2, 4]); ri = sb(mem, f"{tag}ri", [P, 2, 4])
            if rope:
                sw = [sb(mem, f"{tag}sw{i}", [P, HALF]) for i in range(2)]
                table = sb(mem, f"{tag}table", [P, 2, TOK]); bound = sb(mem, f"{tag}bound", [P, NT, P])
            else:
                bound = sb(mem, f"{tag}bound", [P, P])
            bound_of = lambda u: bound[:, u % NT, :] if rope else bound[:]

            def halves(pair, pattern):
                flat = [w[:].rearrange(pattern) for w in pair]
                return [[f[:, i * BLK:(i + 1) * BLK] for f in flat] for i in range(2)]

            dst = {"k": [w[:].rearrange("p h k n -> p (h k n)") for w in wk], "v": [w[:].rearrange("p k n -> p (k n)") for w in wv]}
            for i, (q, o) in enumerate(zip(halves(wq, "p h k n -> p (h k n)"), halves(wo, "p h n -> p (h n)"))):
                dst[f"q{i}"] = dst[f"q{i + 2}"] = q
                dst[f"o{i}"] = dst[f"o{i + 2}"] = o

            def run(engine, start, turn):
                start(Part(first, START, START_BLOCKS))
                with engine.Fori(first, final) as it:
                    turn(Part(it, TURN, TURN_BLOCKS))
                turn(Part(final, LAST, LAST_BLOCKS))

            with nc.Block() as block:
                @block.sync
                def _(sp):
                    if rope:
                        sp.dma_start(mask[:], io["mask"]).then_inc(in_bound, 16)
                    else:
                        sp.dma_start(bound[:], io["causal"]).then_inc(in_bound, 16)

                    def load(part):
                        for n in range(len(part.blocks)):
                            at = part.weights + n
                            if first or part.order is not START or n >= 2:
                                sp.wait_ge(w_low, at - 1)
                            src = io["w_attn"][at] if part.order is not TURN else io["w_attn"][bass.ds(at, 1)].rearrange("a p c -> p (a c)")
                            sp.dma_start(raw[n % 2][:], src).then_inc(w_raw[n % 2], 16)
                    run(sp, load, load)

                @block.gpsimd
                def _(pool):
                    nc.gpsimd.memset(kt[:], 0.0).then_inc(padded, 1)

                    def split(part):
                        for n, name in enumerate(part.blocks):
                            if part.order is not START:
                                if name == "o0":
                                    pool.wait_ge(wo_used, part.it * 2 + 1)
                                elif name == "o1":
                                    pool.wait_ge(y_done, part.it * SLOTS + 2)
                                elif name == "o2":
                                    pool.wait_ge(wo_used, part.it * 2 + 2)
                                elif name == "o3":
                                    pool.wait_ge(y_done, part.it * SLOTS + NT + 2)
                                else:
                                    used = {"q0": ("Q", 5), "q1": ("Q", 7), "k": ("Q", 5), "v": ("Q", 5), "q2": ("Q", 13), "q3": ("Q", 15)}[name]
                                    pool.wait_ge(a_ready, part.bank(used) + 1)
                            pool.wait_ge(w_raw[n % 2], (part.weights + n - n % 2) * 8 + 16)
                            high_part(dst[name][0], raw[n % 2][:]).then_inc(w_high, 1)
                            pool.wait_ge(w_high, part.weights + n + 1)
                            nc.gpsimd.tensor_tensor(dst[name][1], raw[n % 2][:], f32(dst[name][0]), ALU.subtract).then_inc(w_low, 1)
                    run(pool, split, split)

                @block.tensor
                def _(pe):
                    if first == 0:
                        pe.sem_inc(wo_used, 1)
                    pe.wait_ge(padded, first // NPAIR + 1)
                    ln_tensor(pe, norm)
                    if rope:
                        pe.wait_ge(gathered, 16 * NT)
                        for t in range(NT):
                            if t >= 2:
                                pe.wait_ge(tabled, t - 1)
                            for i in range(2):
                                done = nc.tensor.transpose(bankO[:, t % 2, i * P:(i + 1) * P], table_rows[:, t, i * P:(i + 1) * P], ident[:])
                            done.then_inc(flipped, 1)
                        pe.wait_ge(tabled, NT)
                    pe.wait_ge(ln_low, (norm + 1) * NT)

                    def wait_drained(part, x):
                        kind, n = x
                        if kind == "S":
                            pe.wait_ge(st["masked"], part.unit(n) + 1)
                        elif kind == "V":
                            pe.wait_ge(v_done, part.it * 4 + n + 1)
                        else:
                            pe.wait_ge(roped if rope else qk_done, part.qk(x) + 1)

                    def take(part, x):
                        at = part.order.index(x)
                        if at >= 2:
                            wait_drained(part, part.order[at - 2])
                        elif part.order is not START:
                            wait_drained(part, ("Q", 5) if at else ("S", 1))
                            if at == 0:
                                wait_drained(part, ("V", 3))
                        return bankA[part.buffer(x)]

                    def project(part, x):
                        bank, (kind, n) = take(part, x), x
                        if kind == "K":
                            if n % 4 == 0:
                                pe.wait_ge(w_low, part.block("k"))
                            cols = slice(n % 2 * HALF, (n % 2 + 1) * HALF)
                            done = product(bank[:], [x for k in range(KC) for x in three([w[:, n // 2 % 2, k, :] for w in wk], [s[:, k, cols] for s in source])])
                        elif kind == "Q":
                            if n % 8 in (0, 2):
                                pe.wait_ge(w_low, part.block({0: "q0", 2: "q1", 8: "q0", 10: "q1", 16: "q2", 18: "q3"}[n]))
                            cols = slice(n // 4 % 2 * HALF, (n // 4 % 2 + 1) * HALF)
                            done = product(bank[:], [x for k in range(KC) for x in three([w[:, n % 4, k, :] for w in wq], [s[:, k, cols] for s in xT])])
                        elif kind == "V":
                            if n % 4 == 0:
                                pe.wait_ge(w_low, part.block("v"))
                            for t in (n % 4 * 2, n % 4 * 2 + 1):
                                done = product(bank[:, t % 2 * 256:t % 2 * 256 + 256],
                                               [x for k in range(KC) for x in three([s[:, k, t * P:(t + 1) * P] for s in source], [w[:, k, :] for w in wv])])
                        else:
                            t, j = n % NT, n // NT % 2
                            if n % 4 == 0:
                                needed = ("K", 7) if n == SLOTS else ("Q", n // NT * 8 + (3 if t == 0 else 7))
                                pe.wait_ge(qk_done, part.qk(needed) + 1)
                            for hp in range(2):
                                for b in range(2):
                                    at = (hp * 2 + b) * P
                                    done = nc.tensor.matmul(bank[:, at:at + P], qT[:, 2 * t + b, 2 * hp:2 * hp + 2, :].rearrange("p h q -> p (h q)"),
                                                            window(kt, 2 * t + b, slice(None), j), start=True, stop=True)
                        done.then_inc(a_ready, 1)

                    def output(part, u):
                        if u % NT == 0:
                            pe.wait_ge(w_low, part.block("o3" if u else "o1"))
                        pe.wait_ge(o_low, part.unit(u) + 2)
                        pe.wait_ge(y_done, part.unit(u) + 1)
                        pairs = [x for h in range(GROUP) for x in three([o[:, h].rearrange("p b q -> p (b q)") for o in oT[u % 2]], [w[:, h, :] for w in wo])]
                        if u % NT == NT - 1:
                            product(bankY[u % 2][:], pairs[:len(pairs) // 2], stop=False).then_inc(wo_used, 1)
                            product(bankY[u % 2][:], pairs[len(pairs) // 2:], start=False).then_inc(y_ready, 1)
                        else:
                            product(bankY[u % 2][:], pairs).then_inc(y_ready, 1)

                    def start(part):
                        for x in START:
                            project(part, x)

                    def turn(part):
                        for u in range(SLOTS):
                            banks = slot_banks(u, part.final)
                            pe.wait_ge(st["prob"], part.unit(u) + 1)
                            pe.wait_ge(pt_done, part.unit(u) + 1)
                            for hp in range(2):
                                done = nc.tensor.transpose(bankT[u % 2][:, hp * P:(hp + 1) * P], sc[u % 4][:, hp].rearrange("p b k -> p (b k)"), ident[:])
                            done.then_inc(t_ready, 1)
                            if banks and banks[0][0] == "S" and not late(u):
                                project(part, banks[0])
                            if u < NT and u % 2 == 0:
                                pe.wait_ge(v_done, part.it * 4 + u // 2 + 1)
                            pe.wait_ge(pt_done, part.unit(u) + 3)
                            pe.wait_ge(o_low, part.unit(u) + 1)
                            for b in range(2):
                                rows = slice(S * b, S * b + S)
                                done = nc.tensor.matmul(bankO[:, b, 0:GROUP * S], V[rows, u % NT, u // NT * HD:(u // NT + 1) * HD], pt[u % 2][rows, :], start=True, stop=True)
                            done.then_inc(o_ready, 1)
                            if u % NT:
                                output(part, u - 1)
                            for x in banks:
                                if x[0] != "S" or late(u):
                                    project(part, x)
                            if u % NT == NT - 1:
                                output(part, u)
                    run(pe, start, turn)

                def projected(u, final):
                    return [("Q", u + 5)] * (u + 5 < SLOTS or not final) + [("K", n) for n in range(4, 8) if u == KEYS_AT + 1 and not final]

                def half_of(x):
                    kind, n = x
                    h = n % 2 if kind == "K" else n // 4 % 2
                    if kind == "K":
                        return kt[:, n // 2 % 2, S + h * HALF:S + h * HALF + HALF].rearrange("p (b s) -> p b s", s=S), h
                    return qT[:, h * B // 2:(h + 1) * B // 2, n % 4, :], h

                @block.scalar
                def _(act):
                    ln_scalar(act, norm)
                    if first == 0:
                        act.sem_inc(pt_done, 2)

                    def queries_or_keys(part, x):
                        act.wait_ge(a_ready, part.bank(x) + 1)
                        if rope:
                            if part.order is not START or only_qk(START).index(x) >= 2:
                                act.wait_ge(qk_done, part.qk(x) - 1)
                            for i in range(2):
                                nc.scalar.activation(sw[part.swap(x)][64 * i:64 * i + 64, :], bankA[part.buffer(x)][64 - 64 * i:P - 64 * i, :], ACT.Copy).then_inc(swapped, 1)
                        else:
                            nc.scalar.activation(half_of(x)[0], bankA[part.buffer(x)][:].rearrange("p (b s) -> p b s", s=S), ACT.Copy).then_inc(qk_done, 1)

                    def values(part, n):
                        act.wait_ge(a_ready, part.bank(("V", n)) + 1)
                        i = n % 4 * 2
                        nc.scalar.activation(V[:, i:i + 2, :].rearrange("p t n -> p (t n)"), bankA[part.buffer(("V", n))][:], ACT.Copy).then_inc(v_done, 1)

                    def exp(part, u):
                        act.wait_ge(st["sub"], part.unit(u) + 1)
                        flat = sc[u % 4][:].rearrange("p a b k -> p (a b k)")
                        nc.scalar.activation(flat, flat, ACT.Exp, scale=HD ** -0.5).then_inc(st["exp"], 1)

                    def start(part):
                        for x in START[:-1]:
                            if x[0] == "V":
                                values(part, x[1])
                            elif x[0] == "S":
                                if x[1]:
                                    exp(part, 0)
                            else:
                                queries_or_keys(part, x)
                        exp(part, 1)

                    def turn(part):
                        for u in range(SLOTS):
                            banks = projected(u, part.final)
                            if len(banks) > 1:
                                for x in banks:
                                    queries_or_keys(part, x)
                            act.wait_ge(t_ready, part.unit(u) + 1)
                            nc.scalar.activation(pt[u % 2][:], bankT[u % 2][:, 0:GROUP * S], ACT.Copy).then_inc(pt_done, 1)
                            if len(banks) == 1:
                                queries_or_keys(part, banks[0])
                            act.wait_ge(o_ready, part.unit(u) + 1)
                            nc.scalar.activation(oT[u % 2][0][:].rearrange("p h b q -> p b h q"),
                                                 bankO[:, :, 0:GROUP * S].rearrange("p b (h q) -> p b h q", h=GROUP), ACT.Copy).then_inc(o_high, 1)
                            if u + 2 < SLOTS or not part.final:
                                exp(part, u + 2)
                            if u in VALUES_AT and not part.final:
                                values(part, VALUES_AT[u])
                    run(act, start, turn)

                @block.vector
                def _(dve):
                    ln_vector(dve, norm)
                    if first == 0:
                        dve.sem_inc(o_low, 1)
                        dve.sem_inc(y_done, 2)
                    dve.wait_ge(in_bound, 16 * (first // NPAIR + 1))
                    if rope:
                        nc.vector.tensor_scalar(hidden[:], mask[:], 0, -1.0e9 * HD ** 0.5, ALU.is_equal, ALU.mult).then_inc(bounded, 1)
                        nc.vector.tensor_scalar(bound[:], mask[:], 0, -OFF, ALU.not_equal, ALU.mult).then_inc(bounded, 1)
                        for t in range(NT):
                            dve.wait_ge(flipped, t + 1)
                            nc.vector.tensor_copy(table[:, :, t * P:(t + 1) * P], bankO[:, t % 2, 0:2 * P].rearrange("p (a c) -> p a c", a=2)).then_inc(tabled, 1)
                        dve.wait_ge(bounded, 2)
                        nc.vector.tensor_tensor(bound[:], bound[:], hidden[:], ALU.add).then_inc(bounded, 1)
                        dve.wait_ge(bounded, 3)
                        dve.wait_ge(tabled, NT)

                    def rotate(part, *banks):
                        for x in banks:
                            to, h = half_of(x)
                            half, b = slice(h * HALF, (h + 1) * HALF), sw[part.swap(x)]
                            dve.wait_ge(swapped, part.qk(x) * 2 + 2)
                            nc.vector.tensor_tensor(to, bankA[part.buffer(x)][:].rearrange("p (b s) -> p b s", s=S),
                                                    table[:, 0, half].rearrange("p (b s) -> p b s", s=S), ALU.mult).then_inc(roped, 1)
                            nc.vector.tensor_tensor(b[:], b[:], table[:, 1, half], ALU.mult).then_inc(turned, 1)
                            yield
                            dve.wait_ge(roped, part.qk(x) + 1)
                            dve.wait_ge(turned, part.qk(x) + 1)
                            nc.vector.tensor_tensor(to, to, b[:].rearrange("p (b s) -> p b s", s=S), ALU.add).then_inc(qk_done, 1)
                            yield

                    def front(part, u):
                        s3 = sc[u % 4][:].rearrange("p a b k -> p a (b k)")
                        s4 = sc[u % 4][:].rearrange("p a b k -> p (a b) k")
                        dve.wait_ge(a_ready, part.bank(("S", u)) + 1)
                        nc.vector.tensor_tensor(s3, bankA[part.buffer(("S", u))][:].rearrange("p (a c) -> p a c", a=2)[:, :, S:S + P],
                                                bound_of(u).unsqueeze(1).to_broadcast([P, 2, P]), ALU.min).then_inc(st["masked"], 1)
                        yield
                        dve.wait_ge(st["masked"], part.unit(u) + 1)
                        nc.vector.tensor_reduce(mx[:, u % 2, :], s4, AXX, ALU.max).then_inc(st["max"], 1)
                        yield
                        dve.wait_ge(st["max"], part.unit(u) + 1)
                        nc.vector.tensor_tensor(s4, s4, mx[:, u % 2, :].unsqueeze(2).to_broadcast([P, 4, S]), ALU.subtract).then_inc(st["sub"], 1)

                    def back(part, u):
                        s4 = sc[u % 4][:].rearrange("p a b k -> p (a b) k")
                        dve.wait_ge(st["exp"], part.unit(u) + 1)
                        nc.vector.tensor_reduce(sm[:, u % 2, :], s4, AXX, ALU.add).then_inc(st["sum"], 1)
                        yield
                        dve.wait_ge(st["sum"], part.unit(u) + 1)
                        nc.vector.reciprocal(ri[:, u % 2, :], sm[:, u % 2, :]).then_inc(st["inv"], 1)
                        yield
                        dve.wait_ge(st["inv"], part.unit(u) + 1)
                        nc.vector.tensor_tensor(s4, s4, ri[:, u % 2, :].unsqueeze(2).to_broadcast([P, 4, S]), ALU.mult).then_inc(st["prob"], 1)

                    def residual(part, u):
                        t = u % NT
                        dve.wait_ge(y_ready, part.unit(u) + 1)
                        nc.vector.tensor_tensor(xtok[:, t, :], xtok[:, t, :], bankY[u % 2][:], ALU.add).then_inc(y_done, 1)
                        if part.final and u >= NT:
                            dve.wait_ge(y_done, part.unit(u) + 3)
                            ln_statistics(dve, norm + 1, t)

                    def start(part):
                        if rope:
                            in_turns(rotate(part, *only_qk(START)[:8]))
                        in_turns(rotate(part, ("Q", 4)) if rope else None, front(part, 0))
                        in_turns(front(part, 1), back(part, 0))

                    def turn(part):
                        for u in range(SLOTS):
                            banks = projected(u, part.final)
                            scores = front(part, u + 2) if u + 2 < SLOTS or not part.final else None
                            in_turns(rotate(part, *banks) if rope and banks else None,
                                     None if late(u) else scores,
                                     back(part, u + 1) if u + 1 < SLOTS or not part.final else None)
                            if u % NT >= 2:
                                residual(part, u - 2)
                            dve.wait_ge(o_high, part.unit(u) + 1)
                            nc.vector.tensor_tensor(oT[u % 2][1][:].rearrange("p h b q -> p b h q"), bankO[:, :, 0:GROUP * S].rearrange("p b (h q) -> p b h q", h=GROUP),
                                                    f32(oT[u % 2][0][:]).rearrange("p h b q -> p b h q"), ALU.subtract).then_inc(o_low, 1)
                            if late(u):
                                in_turns(scores)
                            if u % NT == NT - 1:
                                residual(part, u - 1)
                                residual(part, u)
                    run(dve, start, turn)

    if phases >= 2:
        grouped_attention("B", 0, 0, cT, True)
        if phases == 2:
            finish(1)
            return

    def block_loader(sp, blocks, raw, w_raw, w_low):
        for n, (src, rows, cols, *_) in enumerate(blocks):
            if n >= len(raw):
                sp.wait_ge(w_low, n - len(raw) + 1)
            sp.dma_start(raw[n % len(raw)][0:rows, 0:cols], src).then_inc(w_raw[n % len(raw)], 16)

    def split_block(pool, n, rows, cols, dst, raw, w_raw, w_high, w_low):
        src = raw[n % len(raw)][0:rows, 0:cols]
        pool.wait_ge(w_raw[n % len(raw)], 16 * (n // len(raw) + 1))
        high_part(dst[0], src).then_inc(w_high, 1)
        pool.wait_ge(w_high, n + 1)
        nc.gpsimd.tensor_tensor(dst[1], src, f32(dst[0]), ALU.subtract).then_inc(w_low, 1)

    if phases >= 3:
        w_raw = [sem(f"C_raw{i}") for i in range(2)]; w_high = sem("C_whigh"); w_low = sem("C_wlow")
        small = sem("C_small"); a_ready = sem("C_aready"); a_done = sem("C_adone"); route = sem("C_route"); route_exp = sem("C_rexp")
        t_ready = sem("C_tready"); m_high = sem("C_mhigh"); m_low = sem("C_mlow"); y_ready = sem("C_yready"); y_done = sem("C_ydone")
        ER = EXPERTS * RANK
        with ExitStack() as mem:
            raw = [sb(mem, f"Craw{i}", [P, BLK]) for i in range(2)]
            war = [sb(mem, f"Cwar{i}", [P, KC, 256], F32R) for i in range(2)]
            wb = [sb(mem, f"Cwb{i}", [P, KC, D], F32R) for i in range(2)]
            wup = [sb(mem, f"Cwup{i}", [P, D], F32R) for i in range(2)]
            mid = sb(mem, "Cmid", [P, NT, ER]); lg = sb(mem, "Clg", [P, NT, EXPERTS])
            earlier = sb(mem, "Cearlier", [P, EXPERTS, EXPERTS])
            top = sb(mem, "Ctop", [P, NT]); pr = sb(mem, "Cpr", [P, NT, EXPERTS]); gate = sb(mem, "Cgate", [P, NT, EXPERTS])
            above = sb(mem, "Cabove", [P, NT, EXPERTS, EXPERTS]); ties = sb(mem, "Cties", [P, NT, EXPERTS, EXPERTS])
            mT = [sb(mem, f"CmT{i}", [P, TOK], F32R) for i in range(2)]
            flat = lambda pair: [w[:].rearrange("p k n -> p (k n)") for w in pair]
            blocks = [(io["war"], P, BLK, flat(war))]
            blocks += [(io["wb"][:, i * BLK:(i + 1) * BLK], P, BLK, [w[:, i * BLK:(i + 1) * BLK] for w in flat(wb)]) for i in range(2)]
            blocks += [(io["wup"], P, D, [w[:] for w in wup])]
            with nc.Block() as block:
                @block.sync
                def _(sp):
                    sp.dma_start(earlier[:], io["earlier"]).then_inc(small, 16)
                    block_loader(sp, blocks, raw, w_raw, w_low)

                @block.gpsimd
                def _(pool):
                    for n, (_, rows, cols, dst) in enumerate(blocks):
                        split_block(pool, n, rows, cols, dst, raw, w_raw, w_high, w_low)

                @block.tensor
                def _(pe):
                    tok = lambda t: slice(t * P, (t + 1) * P)
                    ln_tensor(pe, 1)
                    pe.wait_ge(w_low, 1)
                    for t in range(NT):
                        pe.wait_ge(ln_low, NT + t + 1)
                        if t >= 2:
                            pe.wait_ge(a_done, 2 * (t - 1))
                        product(bankA[t % 2][:, 0:256], [x for k in range(KC) for x in three([s[:, k, tok(t)] for s in xT], [w[:, k, :] for w in war])]).then_inc(a_ready, 1)

                    def dense(t):
                        if t >= 2:
                            pe.wait_ge(y_done, t - 1)
                        product(bankY[t % 2][:], [x for k in range(KC) for x in three([s[:, k, tok(t)] for s in xT], [w[:, k, :] for w in wb])], stop=False)

                    pe.wait_ge(w_low, 3)
                    dense(0)
                    dense(1)
                    pe.wait_ge(w_low, 4)
                    pe.wait_ge(route, 15)
                    for t in range(NT):
                        if t >= 2:
                            pe.wait_ge(m_low, t - 1)
                        nc.tensor.transpose(bankT[t % 2][:, 0:P], mid[:, t, :], ident[:]).then_inc(t_ready, 1)
                    
                        if t:
                            experts = t - 1
                            pe.wait_ge(m_low, experts + 1)
                            product(bankY[experts % 2][:], three([m[:, tok(experts)] for m in mT], [w[:] for w in wup]), start=False).then_inc(y_ready, 1)
                            if experts + 2 < NT:
                                dense(experts + 2)
                    pe.wait_ge(m_low, NT)
                    product(bankY[(NT - 1) % 2][:], three([m[:, tok(NT - 1)] for m in mT], [w[:] for w in wup]), start=False).then_inc(y_ready, 1)

                @block.scalar
                def _(act):
                    ln_scalar(act, 1)
                    for t in range(NT):
                        act.wait_ge(a_ready, t + 1)
                        nc.scalar.activation(mid[:, t, :], bankA[t % 2][:, 0:ER], ACT.Copy).then_inc(a_done, 1)
                        nc.scalar.activation(lg[:, t, :], bankA[t % 2][:, ER:ER + EXPERTS], ACT.Copy).then_inc(a_done, 1)
                    act.wait_ge(route, 2)
                    nc.scalar.activation(pr[:].rearrange("p t e -> p (t e)"), pr[:].rearrange("p t e -> p (t e)"), ACT.Exp).then_inc(route_exp, 1)
                    for t in range(NT):
                        act.wait_ge(t_ready, t + 1)
                        nc.scalar.activation(mT[0][:, t * P:(t + 1) * P], bankT[t % 2][:, 0:P], ACT.Copy).then_inc(m_high, 1)

                def add(dve, t):
                    dve.wait_ge(y_ready, t + 1)
                    nc.vector.tensor_tensor(xtok[:, t, :], xtok[:, t, :], bankY[t % 2][:], ALU.add).then_inc(y_done, 1)
                    dve.wait_ge(y_done, t + 1)
                    ln_statistics(dve, 2, t)

                @block.vector
                def _(dve):
                    ln_vector(dve, 1)
                    wide = lambda v: v[:].unsqueeze(2).to_broadcast([P, NT, EXPERTS])
                    pairs = [P, NT, EXPERTS, EXPERTS]
                    steps = [0]

                    def step(ins):
                        ins.then_inc(route, 1)
                        steps[0] += 1
                        dve.wait_ge(route, steps[0])

                    dve.wait_ge(a_done, 2 * NT)
                    dve.wait_ge(small, 16)
                    step(nc.vector.tensor_reduce(top[:], lg[:], AXX, ALU.max))
                    nc.vector.tensor_tensor(pr[:], lg[:], wide(top), ALU.subtract).then_inc(route, 1)
                    steps[0] += 1
                    dve.wait_ge(route_exp, 1)
                    step(nc.vector.tensor_reduce(top[:], pr[:], AXX, ALU.add))
                    step(nc.vector.reciprocal(top[:], top[:]))
                    step(nc.vector.tensor_tensor(pr[:], pr[:], wide(top), ALU.mult))
                    other, own = pr[:].unsqueeze(2).to_broadcast(pairs), pr[:].unsqueeze(3).to_broadcast(pairs)
                    step(nc.vector.tensor_tensor(above[:], other, own, ALU.is_gt))
                    step(nc.vector.tensor_tensor(ties[:], other, own, ALU.is_equal))
                    step(nc.vector.tensor_tensor(ties[:].rearrange("p t a b -> p t (a b)"), ties[:].rearrange("p t a b -> p t (a b)"),
                                                 earlier[:].rearrange("p a b -> p (a b)").unsqueeze(1).to_broadcast([P, NT, EXPERTS * EXPERTS]), ALU.mult))
                    step(nc.vector.tensor_tensor(above[:], above[:], ties[:], ALU.add))
                    step(nc.vector.tensor_reduce(gate[:].rearrange("p t e -> p (t e)"), above[:].rearrange("p t a b -> p (t a) b"), AXX, ALU.add))
                    step(nc.vector.scalar_tensor_tensor(gate[:], gate[:], 2.0, pr[:], ALU.is_lt, ALU.mult))
                    step(nc.vector.tensor_reduce(top[:], gate[:], AXX, ALU.add))
                    step(nc.vector.reciprocal(top[:], top[:]))
                    step(nc.vector.scalar_tensor_tensor(gate[:], gate[:], 2.0, wide(top), ALU.mult, ALU.mult))
                    nc.vector.tensor_tensor(mid[:].rearrange("p t (e r) -> p t e r", e=EXPERTS), mid[:].rearrange("p t (e r) -> p t e r", e=EXPERTS),
                                            gate[:].unsqueeze(3).to_broadcast([P, NT, EXPERTS, RANK]), ALU.mult).then_inc(route, 1)
                    for t in range(NT):
                        dve.wait_ge(m_high, t + 1)
                        nc.vector.tensor_tensor(mT[1][:, t * P:(t + 1) * P], bankT[t % 2][:, 0:P], f32(mT[0][:, t * P:(t + 1) * P]), ALU.subtract).then_inc(m_low, 1)
                        if t:
                            add(dve, t - 1)
                    add(dve, NT - 1)
        if phases == 3:
            finish(2)
            return

    if phases >= 4:
        grouped_attention("D", 2, NPAIR, xT, False)
        if phases == 4:
            finish(3)
            return

    if phases >= 5:
        w_raw = [sem(f"E_raw{i}") for i in range(2)]; w_high = sem("E_whigh"); w_low = sem("E_wlow")
        small = sem("E_small"); a_ready = sem("E_aready"); q_done = sem("E_qdone"); s_ready = sem("E_sready"); st = softmax_stages("E")
        t_ready = sem("E_tready"); p_high = sem("E_phigh"); p_low = sem("E_plow"); y_ready = sem("E_yready"); y_done = sem("E_ydone")
        with ExitStack() as mem:
            raw = [sb(mem, f"Eraw{i}", [P, BLK]) for i in range(2)]
            w2 = [[sb(mem, f"Ew{a}{i}", [P, KC, KC, P], F32R) for i in range(2)] for a in range(2)]
            ft = [sb(mem, f"Eft{i}", [P, NT, D], F32R) for i in range(2)]
            qk = [sb(mem, f"Eqk{a}", [P, KC, TOK]) for a in range(2)]
            bias = sb(mem, "Ebias", [P, 2, KC]); same = sb(mem, "Esame", [P, P])
            sc = [sb(mem, f"Esc{i}", [P, 4, P]) for i in range(2)]
            pT = [sb(mem, f"EpT{i}", [P, NT, P], F32R) for i in range(2)]
            mx = sb(mem, "Emx", [P, 2, 4])
            blocks = []
            for a, name in enumerate(("wq2", "wk2")):
                fl = [w[:].rearrange("p m k n -> p (m k n)") for w in w2[a]]
                blocks += [(io[name][:, i * BLK:(i + 1) * BLK], P, BLK, [f[:, i * BLK:(i + 1) * BLK] for f in fl]) for i in range(2)]
            blocks += [(io["ctx_tok"][:, i * BLK:(i + 1) * BLK], P, BLK, [f[:].rearrange("p t n -> p (t n)")[:, i * BLK:(i + 1) * BLK] for f in ft]) for i in range(4)]
            with nc.Block() as block:
                @block.sync
                def _(sp):
                    sp.dma_start(bias[:], io["bias2"]).then_inc(small, 16)
                    sp.dma_start(same[:], io["same"]).then_inc(small, 16)
                    block_loader(sp, blocks, raw, w_raw, w_low)

                @block.gpsimd
                def _(pool):
                    for n, (_, rows, cols, dst) in enumerate(blocks):
                        split_block(pool, n, rows, cols, dst, raw, w_raw, w_high, w_low)

                @block.tensor
                def _(pe):
                    ln_tensor(pe, 3)
                    pe.wait_ge(ln_low, 4 * NT)
                    for n in range(16):
                        a, m, h = n // 8, n // 2 % 4, n % 2
                        if n % 4 == 0:
                            pe.wait_ge(w_low, n // 4 + 1)
                        if n >= 2:
                            pe.wait_ge(q_done, n - 1)
                        cols = slice(h * HALF, (h + 1) * HALF)
                        product(bankA[n % 2][:], [x for k in range(KC) for x in three([w[:, m, k, :] for w in w2[a]], [s[:, k, cols] for s in (xT, cT)[a]])]).then_inc(a_ready, 1)
                    pe.wait_ge(q_done, 16)
                    for t in range(NT):
                        tok = slice(t * P, (t + 1) * P)
                        done = product(bankA[t // 4][:, t % 4 * P:t % 4 * P + P], [(qk[0][:, m, tok], qk[1][:, m, tok]) for m in range(KC)])
                        if t % 4 == 3:
                            done.then_inc(s_ready, 1)
                    for u in range(2):
                        pe.wait_ge(st["prob"], u + 1)
                        for j in range(4):
                            done = nc.tensor.transpose(bankT[u][:, j * P:(j + 1) * P], sc[u][:, j, :], ident[:])
                        done.then_inc(t_ready, 1)
                    pe.wait_ge(w_low, 8)
                    for t in range(NT):
                        pe.wait_ge(p_low, t // 4 + 1)
                        if t >= 2:
                            pe.wait_ge(y_done, t - 1)
                        product(bankY[t % 2][:], three([p[:, t, :] for p in pT], [f[:, t, :] for f in ft])).then_inc(y_ready, 1)

                @block.scalar
                def _(act):
                    ln_scalar(act, 3)
                    act.wait_ge(small, 32)
                    for n in range(16):
                        a, m, h = n // 8, n // 2 % 4, n % 2
                        act.wait_ge(a_ready, n + 1)
                        nc.scalar.activation(qk[a][:, m, h * HALF:(h + 1) * HALF], bankA[n % 2][:], ACT.Identity, bias=bias[:, a, m:m + 1]).then_inc(q_done, 1)
                    for u in range(2):
                        act.wait_ge(st["sub"], u + 1)
                        fl = sc[u][:].rearrange("p t k -> p (t k)")
                        nc.scalar.activation(fl, fl, ACT.Exp, scale=D ** -0.5).then_inc(st["exp"], 1)
                    for u in range(2):
                        act.wait_ge(t_ready, u + 1)
                        nc.scalar.activation(pT[0][:, 4 * u:4 * u + 4, :].rearrange("p t k -> p (t k)"), bankT[u][:], ACT.Copy).then_inc(p_high, 1)

                @block.vector
                def _(dve):
                    ln_vector(dve, 3)
                    dve.wait_ge(small, 32)
                    wide = lambda u: mx[:, u, :].unsqueeze(2).to_broadcast([P, 4, P])
                    for u in range(2):
                        dve.wait_ge(s_ready, u + 1)
                        nc.vector.tensor_tensor(sc[u][:], bankA[u][:].rearrange("p (t k) -> p t k", t=4), same[:].unsqueeze(1).to_broadcast([P, 4, P]), ALU.min).then_inc(st["masked"], 1)
                        dve.wait_ge(st["masked"], u + 1)
                        nc.vector.tensor_reduce(mx[:, u, :], sc[u][:], AXX, ALU.max).then_inc(st["max"], 1)
                        dve.wait_ge(st["max"], u + 1)
                        nc.vector.tensor_tensor(sc[u][:], sc[u][:], wide(u), ALU.subtract).then_inc(st["sub"], 1)
                    for u in range(2):
                        dve.wait_ge(st["exp"], u + 1)
                        nc.vector.tensor_reduce(mx[:, u, :], sc[u][:], AXX, ALU.add).then_inc(st["sum"], 1)
                        dve.wait_ge(st["sum"], u + 1)
                        nc.vector.reciprocal(mx[:, u, :], mx[:, u, :]).then_inc(st["inv"], 1)
                        dve.wait_ge(st["inv"], u + 1)
                        nc.vector.tensor_tensor(sc[u][:], sc[u][:], wide(u), ALU.mult).then_inc(st["prob"], 1)
                    for u in range(2):
                        dve.wait_ge(p_high, u + 1)
                        part = [p[:, 4 * u:4 * u + 4, :].rearrange("p t k -> p (t k)") for p in pT]
                        nc.vector.tensor_tensor(part[1], bankT[u][:], f32(part[0]), ALU.subtract).then_inc(p_low, 1)
                    for t in range(NT):
                        dve.wait_ge(y_ready, t + 1)
                        nc.vector.tensor_tensor(xtok[:, t, :], xtok[:, t, :], bankY[t % 2][:], ALU.add).then_inc(y_done, 1)
                        dve.wait_ge(y_done, t + 1)
                        ln_statistics(dve, 4, t)
        if phases == 5:
            finish(4)
            return
    cmem.close()

    if phases >= 6:
        FB = 512
        ZERO, STEP, LR = 7.5, 0.005, 0.02
        w_raw = [sem(f"F_raw{i}") for i in range(2)]; w_high = sem("F_whigh"); w_low = sem("F_wlow")
        small = sem("F_small"); lr_ready = sem("F_lrready"); lr_high = sem("F_lrhigh"); lr_low = sem("F_lrlow")
        gu_ready = sem("F_guready"); scaled = sem("F_scaled"); g_sum = sem("F_gsum"); u_sum = sem("F_usum"); act_done = sem("F_act")
        h_done = sem("F_h"); h_high = sem("F_hhigh"); h_low = sem("F_hlow"); d_ready = sem("F_dready")
        y_ready = sem("F_yready"); y_scaled = sem("F_yscaled"); y_sum = sem("F_ysum"); y_done = sem("F_ydone")
        NU = NI * 2
        with ExitStack() as mem:
            raw = [sb(mem, f"Fraw{i}", [P, FB]) for i in range(2)]
            wgu = [[sb(mem, f"Fwgu{i}{a}", [P, KC, P], F32R) for a in range(2)] for i in range(2)]
            wd = sb(mem, "Fwd", [P, NI, D], F32R)
            a_gu = [sb(mem, f"Fagu{i}", [P, KC, 2 * LR_RANK], F32R) for i in range(2)]
            b_gu = sb(mem, "Fbgu", [3 * LR_RANK, 2, NI * P], F32R)
            a_d = [sb(mem, f"Fad{i}", [P, NI, LR_RANK], F32R) for i in range(2)]
            b_d = sb(mem, "Fbd", [3 * LR_RANK, D], F32R)
            stack = [sb(mem, f"Fstack{i}", [3 * LR_RANK, TOK], F32R) for i in range(2)]
            hT = [sb(mem, f"FhT{i}", [P, NI, TOK], F32R) for i in range(2)]
            gs = [sb(mem, f"Fgs{i}", [P, HALF]) for i in range(2)]; us = [sb(mem, f"Fus{i}", [P, HALF]) for i in range(2)]
            scale = sb(mem, "Fscale", [P, 2, NI]); dscale = sb(mem, "Fdscale", [P, D])
            bgu_flat = b_gu[:].rearrange("p a n -> p (a n)")
            blocks = [(io["a_gu"], P, KC * 2 * LR_RANK, "split", [w[:].rearrange("p k n -> p (k n)") for w in a_gu])]
            for at in range(0, 2 * NI * P, FB):
                n = min(FB, 2 * NI * P - at)
                blocks.append((io["b_gu"][:, at:at + n], 3 * LR_RANK, n, "stack", bgu_flat[:, at:at + n]))
            first_gu = len(blocks)
            for i in range(NI):
                for a in range(2):
                    blocks.append((io["q_gu"][i, a].bitcast(F32), P, FB, "levels", wgu[i % 2][a][:].rearrange("p k n -> p (k n)")))
            first_d = len(blocks)
            blocks.append((io["a_d"], P, NI * LR_RANK, "split", [w[:].rearrange("p k n -> p (k n)") for w in a_d]))
            blocks.append((io["b_d"], 3 * LR_RANK, D, "stack", b_d[:]))
            blocks += [(io["q_d"][i].bitcast(F32), P, FB, "levels", wd[:, i, :]) for i in range(NI)]
            sets = [(bankA[0][:], bankA[1][:], bankY[0][:], bankY[1][:]), (bankT[0][:], bankT[1][:], bankO[:, 0, :], bankO[:, 1, :])]
            with nc.Block() as block:
                @block.sync
                def _(sp):
                    sp.dma_start(scale[:], io["gu_scale"]).then_inc(small, 16)
                    sp.dma_start(dscale[:], io["d_scale"].to_broadcast([P, D])).then_inc(small, 16)
                    block_loader(sp, blocks, raw, w_raw, w_low)

                @block.gpsimd
                def _(pool):
                    for n, (_, rows, cols, kind, dst) in enumerate(blocks):
                        src = raw[n % 2][0:rows, 0:cols]
                        if kind == "split":
                            split_block(pool, n, rows, cols, dst, raw, w_raw, w_high, w_low)
                        elif kind == "stack":
                            low = slice(2 * LR_RANK, 3 * LR_RANK)
                            pool.wait_ge(w_raw[n % 2], 16 * (n // 2 + 1))
                            high_part(dst, src).then_inc(w_high, 1)
                            pool.wait_ge(w_high, n + 1)
                            nc.gpsimd.tensor_tensor(dst[low], src[low], f32(dst[low]), ALU.subtract).then_inc(w_low, 1)
                            pool.wait_ge(w_low, n + 1)
                        else:
                            i = (n - first_gu) // 2
                            if n < first_d and i >= 2:
                                pool.wait_ge(gu_ready, 4 * (i - 1))
                            pool.wait_ge(w_raw[n % 2], 16 * (n // 2 + 1))
                            nc.gpsimd.tensor_scalar(dst, src.bitcast(I32), -ZERO, 1.0, ALU.add, ALU.mult).then_inc(w_low, 1)
                            pool.sem_inc(w_high, 1)

                @block.tensor
                def _(pe):
                    ln_tensor(pe, 4)
                    pe.wait_ge(ln_low, 5 * NT)
                    pe.wait_ge(w_low, 1)
                    for h in range(2):
                        cols = slice(h * HALF, (h + 1) * HALF)
                        product(bankT[h][0:2 * LR_RANK, :], [x for k in range(KC) for x in three([w[:, k, :] for w in a_gu], [s[:, k, cols] for s in xT])]).then_inc(lr_ready, 1)
                    for n in range(NU):
                        i, h = n // 2, n % 2
                        cols = slice(h * HALF, (h + 1) * HALF)
                        if h == 0:
                            pe.wait_ge(w_low, first_gu + 2 * i + 2)
                        if n == 0:
                            pe.wait_ge(lr_low, 4)
                        if n >= 2:
                            pe.wait_ge(g_sum, n - 1)
                            pe.wait_ge(u_sum, n - 1)
                        for a in range(2):
                            product(sets[h][a], [(wgu[i % 2][a][:, k, :], s[:, k, cols]) for k in range(KC) for s in xT])
                            nc.tensor.matmul(sets[h][2 + a], b_gu[:, a, i * P:(i + 1) * P], stack[a][:, cols], start=True, stop=True).then_inc(gu_ready, 1)
                    pe.wait_ge(w_low, first_d + 1)
                    pe.wait_ge(h_low, NU)
                    for h in range(2):
                        cols = slice(h * HALF, (h + 1) * HALF)
                        product(bankA[h][0:LR_RANK, :], [x for i in range(NI) for x in three([w[:, i, :] for w in a_d], [s[:, i, cols] for s in hT])]).then_inc(d_ready, 1)
                    pe.wait_ge(w_low, len(blocks))
                    for t in range(NT):
                        tok = slice(t * P, (t + 1) * P)
                        if t >= 2:
                            pe.wait_ge(y_sum, t - 1)
                        product(bankY[t % 2][:], [(s[:, i, tok], wd[:, i, :]) for i in range(NI) for s in hT])
                        if t == 0:
                            pe.wait_ge(lr_low, 6)
                        nc.tensor.matmul(bankT[t % 2][:], stack[0][:, tok], b_d[:], start=True, stop=True).then_inc(y_ready, 1)

                R0, R1, R2 = (slice(LR_RANK * i, LR_RANK * (i + 1)) for i in range(3))

                @block.scalar
                def _(act):
                    ln_scalar(act, 4)
                    act.wait_ge(small, 34)
                    for h in range(2):
                        cols = slice(h * HALF, (h + 1) * HALF)
                        act.wait_ge(lr_ready, h + 1)
                        for dst, src in ((stack[0][R0, cols], R0), (stack[0][R2, cols], R0), (stack[1][R1, cols], R1), (stack[1][R2, cols], R1)):
                            nc.scalar.activation(dst, bankT[h][src, :], ACT.Copy, scale=LR).then_inc(lr_high, 1)
                    for n in range(NU):
                        i, h = n // 2, n % 2
                        act.wait_ge(gu_ready, 2 * n + 1)
                        if n >= 2:
                            act.wait_ge(h_done, n - 1)
                        nc.scalar.activation(gs[h][:], sets[h][0], ACT.Copy, scale=scale[:, 0, i:i + 1]).then_inc(scaled, 1)
                        act.wait_ge(gu_ready, 2 * n + 2)
                        if n >= 2:
                            act.wait_ge(h_low, n - 1)
                        nc.scalar.activation(us[h][:], sets[h][3], ACT.Copy).then_inc(scaled, 1)
                        act.wait_ge(g_sum, n + 1)
                        nc.scalar.activation(gs[h][:], gs[h][:], ACT.Silu).then_inc(act_done, 1)
                        act.wait_ge(h_done, n + 1)
                        nc.scalar.activation(hT[0][:, i, h * HALF:(h + 1) * HALF], us[h][:], ACT.Copy).then_inc(h_high, 1)
                    for h in range(2):
                        cols = slice(h * HALF, (h + 1) * HALF)
                        act.wait_ge(d_ready, h + 1)
                        for dst in (R0, R2):
                            nc.scalar.activation(stack[0][dst, cols], bankA[h][R0, :], ACT.Copy, scale=LR).then_inc(lr_high, 1)

                @block.vector
                def _(dve):
                    ln_vector(dve, 4)
                    dve.wait_ge(small, 32)
                    nc.vector.tensor_scalar(scale[:], scale[:], STEP, None, ALU.mult).then_inc(small, 1)
                    nc.vector.tensor_scalar(dscale[:], dscale[:], STEP, None, ALU.mult).then_inc(small, 1)
                    dve.wait_ge(small, 34)
                    for h in range(2):
                        cols = slice(h * HALF, (h + 1) * HALF)
                        dve.wait_ge(lr_high, 4 * h + 4)
                        nc.vector.scalar_tensor_tensor(stack[0][R1, cols], bankT[h][R0, :], LR, f32(stack[0][R0, cols]), ALU.mult, ALU.subtract).then_inc(lr_low, 1)
                        nc.vector.scalar_tensor_tensor(stack[1][R0, cols], bankT[h][R1, :], LR, f32(stack[1][R1, cols]), ALU.mult, ALU.subtract).then_inc(lr_low, 1)
                    for n in range(NU):
                        i, h = n // 2, n % 2
                        dve.wait_ge(scaled, 2 * n + 1)
                        nc.vector.tensor_tensor(gs[h][:], gs[h][:], sets[h][2], ALU.add).then_inc(g_sum, 1)
                        dve.wait_ge(scaled, 2 * n + 2)
                        nc.vector.scalar_tensor_tensor(us[h][:], sets[h][1], scale[:, 1, i:i + 1], us[h][:], ALU.mult, ALU.add).then_inc(u_sum, 1)
                        dve.wait_ge(u_sum, n + 1)
                        dve.wait_ge(act_done, n + 1)
                        nc.vector.tensor_tensor(us[h][:], us[h][:], gs[h][:], ALU.mult).then_inc(h_done, 1)
                        dve.wait_ge(h_high, n + 1)
                        cols = slice(h * HALF, (h + 1) * HALF)
                        nc.vector.tensor_tensor(hT[1][:, i, cols], us[h][:], f32(hT[0][:, i, cols]), ALU.subtract).then_inc(h_low, 1)
                    for h in range(2):
                        cols = slice(h * HALF, (h + 1) * HALF)
                        dve.wait_ge(lr_high, 8 + 2 * h + 2)
                        nc.vector.scalar_tensor_tensor(stack[0][R1, cols], bankA[h][R0, :], LR, f32(stack[0][R0, cols]), ALU.mult, ALU.subtract).then_inc(lr_low, 1)
                    for t in range(NT):
                        dve.wait_ge(y_ready, t + 1)
                        nc.vector.tensor_tensor(gs[t % 2][:], bankY[t % 2][:], dscale[:], ALU.mult).then_inc(y_scaled, 1)
                        dve.wait_ge(y_scaled, t + 1)
                        nc.vector.tensor_tensor(gs[t % 2][:], gs[t % 2][:], bankT[t % 2][:], ALU.add).then_inc(y_sum, 1)
                        dve.wait_ge(y_sum, t + 1)
                        nc.vector.tensor_tensor(xtok[:, t, :], xtok[:, t, :], gs[t % 2][:], ALU.add).then_inc(y_done, 1)
                        dve.wait_ge(y_done, t + 1)
                        ln_statistics(dve, 5, t)
        finish(5)
    ctx.close()


def layouts(i):
    def feat(w):
        return w.reshape(-1, P, w.shape[1]).transpose(1, 0, 2)

    a = {}
    a["x_tok"] = i["x"].reshape(NT, P, D).transpose(1, 0, 2)
    a["xT"] = feat(i["x"].reshape(TOK, D).T)
    a["ctxT"] = feat(i["ctx_4096"].reshape(TOK, D).T)
    a["ident"] = np.eye(P, dtype=np.float32)
    w, b = i["L0_attn_w_attn"], i["L0_attn_b_attn"]
    kq = np.stack([feat(w[:, D:2 * D]), feat(w[:, 0:D])], 1).reshape(P, 2, KC, KC, P)
    a["wqk"] = kq.transpose(3, 1, 0, 2, 4).reshape(KC, 2, P, D)
    a["wv"] = feat(w[:, 2 * D:]).reshape(P, KC * D)
    a["wp"] = feat(i["L0_attn_w_proj"]).reshape(P, KC * D)
    a["bqk"] = b[:2 * D].reshape(2, KC, P).transpose(2, 0, 1)
    a["bv"] = b[2 * D:].reshape(1, D)
    a["bp"] = i["L0_attn_b_proj"].reshape(1, D)
    base = 2 ** (-2 ** (-(math.log2(NH) - 3)))
    slopes = (base ** np.arange(1, NH + 1, dtype=np.float32)).astype(np.float32)
    rel = (np.arange(S)[None, :] - np.arange(S)[:, None])
    bias = np.where(rel[None] <= 0, slopes[:, None, None] * rel[None].astype(np.float32), np.float32(OFF)).astype(np.float32)
    a["alibi"] = np.concatenate([bias, bias], 2).reshape(NH // 2, 2 * S, 2 * S).transpose(1, 0, 2)
    even = (np.arange(P) % 32 < 16).astype(np.float32)
    a["parity"] = np.stack([even, 1 - even], 1)
    a["own"] = np.repeat(np.eye(P // A_HD, dtype=np.float32), A_HD, 0)

    def attention_blocks(wq, wk, wv, wo):
        heads = lambda w: w.reshape(KC, P, -1, HD).transpose(1, 2, 0, 3)
        q, k, o = heads(wq), heads(wk), wo.reshape(NH, HD, D).transpose(1, 0, 2)
        v = wv.reshape(KC, P, NPAIR, 2 * HD).transpose(1, 2, 0, 3)
        pair = lambda w, n: [w[:, n:n + 2], w[:, n + 2:n + 4]]
        blocks = [v[:, 0], k[:, 0:2]] + pair(q, 0)
        for it in range(NPAIR):
            h = 2 * it * GROUP
            blocks += pair(o, h) + pair(q, h + GROUP)
            if it + 1 < NPAIR:
                blocks += [k[:, 2 * it + 2:2 * it + 4], v[:, it + 1]]
            blocks += pair(o, h + GROUP)
            if it + 1 < NPAIR:
                blocks += pair(q, h + 2 * GROUP)
        return np.stack([x.reshape(P, BLK) for x in blocks])

    a["w_attn"] = np.concatenate([attention_blocks(*(i["L0_xattn_W" + c] for c in "qkvo")),
                                  attention_blocks(*(i["L1_attn_w" + c].T for c in "qkvo"))])
    a["pos"] = i["pos_BxS2"].reshape(NT, P).T
    m = i["mask_BxSxS2_ik0"].transpose(1, 0, 2)
    a["mask"] = np.concatenate([m, m]).reshape(P, NT, P)
    inv = (1.0 / np.float32(10000.0) ** (np.arange(0, HD, 2, dtype=np.float32) / HD)).astype(np.float32)
    angle = np.arange(ROPE_ROWS, dtype=np.float32)[:, None] * inv[None]
    cos, sin = np.cos(angle).astype(np.float32), np.sin(angle).astype(np.float32)
    a["rope"] = np.concatenate([cos, cos, -sin, sin], 1)

    far = np.float32(-OFF)
    a["earlier"] = np.broadcast_to(np.tril(np.ones((EXPERTS, EXPERTS), np.float32), -1), (P, EXPERTS, EXPERTS))
    a["causal"] = np.tile(np.where(np.tril(np.ones((S, S))) > 0, far, -far).astype(np.float32), (2, 2))
    a["same"] = np.where(np.kron(np.eye(2), np.ones((S, S))) > 0, far, -far).astype(np.float32)
    down = i["L0_ffn_lora_A"].transpose(1, 0, 2).reshape(D, EXPERTS * RANK)
    war = np.concatenate([down, i["L0_ffn_router_W"].T, np.zeros((D, 256 - EXPERTS * RANK - EXPERTS), np.float32)], 1)
    a["war"] = feat(war).reshape(P, BLK)
    a["wb"] = feat(i["L0_ffn_base_W"].T).reshape(P, KC * D)
    a["wup"] = i["L0_ffn_lora_B"].reshape(EXPERTS * RANK, D)
    for name in "qk":
        a["w" + name + "2"] = feat(i["L1_xattn_W" + name].T).reshape(P, KC, KC, P).transpose(0, 2, 1, 3).reshape(P, KC * D)
    a["ctx_tok"] = i["ctx_4096"].reshape(NT, P, D).transpose(1, 0, 2).reshape(P, NT * D)
    a["bias2"] = np.stack([i["L1_xattn_bq"], i["L1_xattn_bk"]]).reshape(2, KC, P).transpose(2, 0, 1)
    pad = NI * P - INNER
    grow = lambda w, axis: np.pad(w, [(0, pad if x == axis else 0) for x in range(w.ndim)])
    a["a_gu"] = feat(np.concatenate([i["L1_ffn_gate_A"], i["L1_ffn_up_A"]], 1)).reshape(P, KC * 2 * LR_RANK)
    bgu = np.concatenate([grow(i["L1_ffn_gate_B"], 1), grow(i["L1_ffn_up_B"], 1)], 1)
    a["b_gu"] = np.concatenate([bgu, bgu, bgu])
    q = np.stack([grow(i["L1_ffn_gate_q"], 0), grow(i["L1_ffn_up_q"], 0)])
    a["q_gu"] = q.reshape(2, NI, P, KC, P).transpose(1, 0, 4, 3, 2).reshape(NI, 2, P, KC * P)
    a["gu_scale"] = np.stack([grow(i["L1_ffn_gate_scale"], 0), grow(i["L1_ffn_up_scale"], 0)]).reshape(2, NI, P).transpose(2, 0, 1)
    a["a_d"] = grow(i["L1_ffn_down_A"], 0).reshape(NI, P, LR_RANK).transpose(1, 0, 2).reshape(P, NI * LR_RANK)
    a["b_d"] = np.concatenate([i["L1_ffn_down_B"]] * 3)
    a["q_d"] = grow(i["L1_ffn_down_q"], 1).T.reshape(NI, P, D)
    a["d_scale"] = i["L1_ffn_down_scale"].reshape(1, D)
    return {k: np.ascontiguousarray(v) for k, v in a.items()}


def kernel(**inputs):
    import concourse.bacc as _bacc
    from concourse.bass_utils import run_bass_kernel_spmd as _run

    nc = _bacc.Bacc("TRN2", target_bir_lowering=False, num_devices=1)
    arrays = layouts({k: np.asarray(v) for k, v in inputs.items()})
    io = {k: nc.dram_tensor("in_" + k, v.shape, mybir.dt.from_np(v.dtype), kind="ExternalInput").ap() for k, v in arrays.items()}
    io["out"] = nc.dram_tensor("out_dram", (P, NT, D), F32, kind="ExternalOutput").ap()
    build_program(nc, io)
    r = _run(nc, [{"in_" + k: v for k, v in arrays.items()}], core_ids=[0])
    return np.asarray(r.results[0]["out_dram"]).transpose(1, 0, 2).reshape(B, S, D)
```

```python
import math
from contextlib import ExitStack

import concourse.bass as bass
import numpy as np
from concourse import mybir

F32 = mybir.dt.float32
F32R = mybir.dt.float32r
I32 = mybir.dt.int32
U32 = mybir.dt.uint32
ALU = mybir.AluOpType
ACT = mybir.ActivationFunctionType
AXX = mybir.AxisListType.X

P = 128
B, S, D = 16, 64, 512
TOK = B * S
NT = TOK // P
KC = D // P
HALF = TOK // 2
NH, HD = 32, 128
KVH = 8
GROUP = NH // KVH
NPAIR = KVH // 2
A_HD = D // NH
WINDOW = S + TOK + S
EXPERTS, RANK = 8, 16
INNER, LR_RANK = 1376, 32
NI = -(-INNER // P)
EPS = 1e-5
OFF = -3.0e38
ROPE_ROWS = 512
BLK = 1024
FB = 512
NRAW = 2


def f32(ap):
    return ap.bitcast(F32)


def build_program(nc, io):
    ctx = ExitStack()

    def sb(stack, name, shape, dt=F32):
        return stack.enter_context(nc.sbuf_tensor("sb_" + name, shape, dt))

    def sem(name):
        return ctx.enter_context(nc.semaphore(name))

    xtok = sb(ctx, "xtok", [P, NT, D])
    xT = [sb(ctx, f"xT{i}", [P, KC, TOK], F32R) for i in range(2)]
    ident = sb(ctx, "ident", [P, P])
    zero = sb(ctx, "zero", [P, 1])
    raw = [sb(ctx, f"raw{i}", [P, BLK]) for i in range(NRAW)]
    bankA = [ctx.enter_context(nc.psum_tensor(f"bankA{i}", [P, 512], F32)) for i in range(2)]
    bankT = [ctx.enter_context(nc.psum_tensor(f"bankT{i}", [P, 512], F32)) for i in range(2)]
    bankY = [ctx.enter_context(nc.psum_tensor(f"bankY{i}", [P, 512], F32)) for i in range(2)]
    bankO = ctx.enter_context(nc.psum_tensor("bankO", [P, 2, 512], F32))

    raw_of = {phase: [sem(f"{phase}_raw{i}") for i in range(NRAW)] for phase in "AGCEF"}

    def load_ahead(sp, w_low, blocks, w_raw, sources):
        sp.wait_ge(w_low, blocks)
        for i, (dst, src) in enumerate(sources):
            sp.dma_start(dst, src).then_inc(w_raw[i], 16)

    def group_sources(first):
        return [(raw[i][:], io["w_attn"][first * 10 + i]) for i in range(NRAW)]

    def high_part(dst, src):
        return nc.gpsimd.tensor_tensor(dst, src, zero[0:src.shape[0]].to_broadcast([src.shape[0], src.shape[1]]), ALU.add)

    def product(out, pairs, start=True, stop=True):
        for i, (lhs, rhs) in enumerate(pairs):
            last = nc.tensor.matmul(out, lhs, rhs, start=start and i == 0, stop=stop and i == len(pairs) - 1)
        return last

    def three(lhs, rhs):
        return [(lhs[0], rhs[0]), (lhs[0], rhs[1]), (lhs[1], rhs[0])]

    def window(kt, b, *lead):
        at = S + b * S - (S if b % 2 == 0 else 0)
        return kt[(*lead, slice(at, at + P))]

    ln_stat = sem("ln_stat"); ln_mean = sem("ln_mean"); ln_sqrt = sem("ln_sqrt"); ln_rstd = sem("ln_rstd"); ln_offset = sem("ln_offset")
    ln_norm = sem("ln_norm"); ln_last = sem("ln_last"); ln_tr = sem("ln_tr"); ln_high = sem("ln_high"); ln_low = sem("ln_low"); out_done = sem("out_done")
    stats = sb(ctx, "ln_stats", [P, NT, 6])
    moments = sb(ctx, "ln_moments", [P, NT, 2])
    rstd = sb(ctx, "ln_rstd", [P, NT]); offset = sb(ctx, "ln_offset", [P, NT])
    epsilon = sb(ctx, "ln_epsilon", [P, 1])
    LN_GROUPS = [(0, 4), (4, 6), (6, 8)]
    ln_banks = [bankT[0], bankT[1], bankY[0], bankY[1]]

    def ln_roots(act, n, g):
        first, end = LN_GROUPS[g]
        act.wait_ge(ln_mean, n * NT + end)
        nc.scalar.activation(rstd[:, first:end], moments[:, first:end, 1], ACT.Sqrt, bias=epsilon[:]).then_inc(ln_sqrt, 1)

    def ln_scale(act, n, g):
        act.wait_ge(ln_offset, n * len(LN_GROUPS) + g + 1)
        for t in range(LN_GROUPS[g][0], min(LN_GROUPS[g][1], NT - 1)):
            nc.scalar.activation(xtok[:, t, :], xtok[:, t, :], ACT.Identity, bias=offset[:, t:t + 1], scale=rstd[:, t:t + 1]).then_inc(ln_norm, 1)

    def ln_rest(act, n):
        ln_scale(act, n, 0)
        ln_roots(act, n, 1)
        ln_scale(act, n, 1)
        ln_roots(act, n, 2)
        ln_scale(act, n, 2)

    def wait_normalised(engine, n, t):
        if t < NT - 1:
            engine.wait_ge(ln_norm, n * (NT - 1) + t + 1)
        else:
            engine.wait_ge(ln_last, n + 1)

    def ln_follow(dve, n, t, early=0):
        nc.vector.bn_stats(stats[:, t, :], xtok[:, t, :]).then_inc(ln_stat, 1)
        dve.wait_ge(ln_stat, n * NT + t + 1)
        nc.vector.bn_aggr(moments[:, t, :], stats[:, t, :]).then_inc(ln_mean, 1)
        g = {5 - early: 0, 6: 1, 7: 2}.get(t)
        if g is not None:
            part = slice(*LN_GROUPS[g])
            dve.wait_ge(ln_sqrt, n * len(LN_GROUPS) + g + 1)
            nc.vector.reciprocal(rstd[:, part], rstd[:, part]).then_inc(ln_rstd, 1)
            dve.wait_ge(ln_rstd, n * len(LN_GROUPS) + g + 1)
            nc.vector.scalar_tensor_tensor(offset[:, part], moments[:, part, 0], -1.0, rstd[:, part], ALU.mult, ALU.mult).then_inc(ln_offset, 1)
        if t == NT - 1:
            dve.wait_ge(ln_offset, (n + 1) * len(LN_GROUPS))
            nc.vector.tensor_scalar(xtok[:, t, :], xtok[:, t, :], rstd[:, t:t + 1], offset[:, t:t + 1], ALU.mult, ALU.add).then_inc(ln_last, 1)

    def ln_low_parts(dve, n):
        for t in range(NT):
            dve.wait_ge(ln_high, n * NT + t + 1)
            nc.vector.tensor_tensor(xT[1][:, :, t * P:(t + 1) * P], ln_banks[t % 4][:].rearrange("p (k c) -> p k c", k=KC),
                                    f32(xT[0][:, :, t * P:(t + 1) * P]), ALU.subtract).then_inc(ln_low, 1)

    def ln_high_parts(act, n):
        for t in range(NT):
            act.wait_ge(ln_tr, n * NT + t + 1)
            nc.scalar.activation(xT[0][:, :, t * P:(t + 1) * P],
                                 ln_banks[t % 4][:].rearrange("p (k c) -> p k c", k=KC), ACT.Copy).then_inc(ln_high, 1)

    def ln_tensor(pe, n):
        for t in range(NT):
            wait_normalised(pe, n, t)
            if t >= 4:
                pe.wait_ge(ln_low, n * NT + t - 3)
            for k in range(KC):
                done = nc.tensor.transpose(ln_banks[t % 4][:, k * P:(k + 1) * P], xtok[:, t, k * P:(k + 1) * P], ident[:])
            done.then_inc(ln_tr, 1)

    raw_small = [raw[0][:, i * FB:(i + 1) * FB] for i in range(NRAW)]

    def store(sp, n):
        for t in range(NT):
            wait_normalised(sp, n, t)
            sp.dma_start(io["out"][:, t, :], xtok[:, t, :]).then_inc(out_done, 16)
        sp.wait_ge(out_done, NT * 16)

    cmem = ExitStack()
    cT = [sb(cmem, f"cT{i}", [P, KC, TOK], F32R) for i in range(2)]

    def softmax_stages(tag):
        return {k: sem(f"{tag}_{k}") for k in ("masked", "max", "sub", "exp", "sum", "inv", "prob")}

    def in_turns(*steps):
        steps = [s for s in steps if s]
        while steps:
            steps = [s for s in steps if next(s, steps) is not steps]

    QUADS = B // 4
    PER_CHUNK = QUADS * 4
    UNITS = KC * PER_CHUNK
    HEADS = NH // KC
    OUTPUT_AT = UNITS - PER_CHUNK + 6
    AHEAD = 3
    v_raw = [sem(f"A_vraw{k}") for k in range(KC)]; w_raw = raw_of["A"]
    w_high = sem("A_whigh"); w_low = sem("A_wlow"); zeroed = sem("A_zeroed")
    in_xT = [sem(f"A_inxT{k}") for k in range(KC)]; in_high = sem("A_inhigh"); in_low = sem("A_inlow"); in_tok = sem("A_intok")
    clamped = sem("A_clamped"); gathered = sem("A_gathered"); small = sem("A_small"); pbias = sem("A_pbias")
    a_ready = sem("A_aready"); v_done = sem("A_vdone"); q_done = sem("A_qdone"); k_done = sem("A_kdone"); m_done = sem("A_mdone")
    s_ready = sem("A_sready"); st = softmax_stages("A")
    t_ready = sem("A_tready"); pt_done = sem("A_ptdone"); o_ready = sem("A_oready")
    o_even = sem("A_oeven"); o_odd = sem("A_oodd"); o_high = sem("A_ohigh"); o_low = sem("A_olow")
    y_ready = sem("A_yready"); y_done = sem("A_ydone")
    with ExitStack() as mem:
        with ExitStack() as early:
            table_rows = sb(early, "table_rows", [P, NT, 2 * P])
        wqk = [sb(mem, f"Awqk{i}", [P, 2, KC, P], F32R) for i in range(2)]
        wbig = [sb(mem, f"Awbig{i}", [P, KC, D], F32R) for i in range(2)]
        V = sb(mem, "AV", [P, NT, D])
        q = sb(mem, "Aq", [P, TOK])
        qm = [sb(mem, f"Aqm{i}", [P, 4, HEADS, S]) for i in range(2)]
        kt = [sb(mem, f"Akt{i}", [P, WINDOW]) for i in range(2)]
        with ExitStack() as early:
            rawx = sb(early, "rawx", [P, KC, TOK])
            rawv = sb(early, "rawv", [P, KC, D])
        oT = [sb(mem, f"AoT{i}", [P, KC, TOK], F32R) for i in range(2)]
        ring = [rawv[:, k, :] for k in range(KC)]
        alibi = sb(mem, "Aalibi", [P, NH // 2, P])
        bqk = sb(mem, "Abqk", [P, 2, KC]); bp = sb(mem, "Abp", [P, D])
        pos = sb(mem, "Apos", [P, NT], I32); row = sb(mem, "Arow", [P, NT], U32)
        parity = sb(mem, "Aparity", [P, 2])
        own = sb(mem, "Aown", [P, HEADS])
        with ExitStack() as early:
            bv = sb(early, "Abv", [P, D])
        sc = [sb(mem, f"Asc{i}", [P, 2, 2, S]) for i in range(3)]
        pt = [sb(mem, f"Apt{i}", [P, 2, P]) for i in range(2)]
        mx = sb(mem, "Amx", [P, 2, 4]); sm = sb(mem, "Asm", [P, 2, 4]); ri = sb(mem, "Ari", [P, 2, 4])
        oc = sb(mem, "Aoc", [P, 2, 2, S]); od = sb(mem, "Aod", [P, 2, 2, S])
        vbank = [bankY[0][:], bankY[1][:], bankA[0][:], bankA[1][:], bankT[0][:], bankT[1][:], bankO[:, 0, :], bankO[:, 1, :]]
        flat = lambda ws: [w[:].rearrange("p k n -> p (k n)") for w in ws]
        blocks = [(io["wv"][:, k * D:(k + 1) * D], [w[:, k, :] for w in wbig]) for k in range(KC)]
        blocks += [(io["wqk"][c, a], [w[:, a].rearrange("p k n -> p (k n)") for w in wqk]) for c in range(KC) for a in range(2)]
        blocks += [(io["wp"][:, i * BLK:(i + 1) * BLK], [w[:, i * BLK:(i + 1) * BLK] for w in flat(wbig)]) for i in range(2)]
        blocks += [(io["ctxT"][:, k, :], [c[:, k, :] for c in cT]) for k in range(KC)]
        ring += [raw[(n - KC) % NRAW][:, 0:blocks[n][0].shape[1]] for n in range(KC, len(blocks))]
        banks_before = lambda c, i: NT + 4 * c + i

        def slot(n):
            return n // PER_CHUNK, n // 4 % QUADS, n % 4

        with nc.Block() as block:
            @block.sync
            def _(sp):
                for n, (src, dst) in enumerate(blocks):
                    if n >= KC + NRAW:
                        sp.wait_ge(w_low, n - NRAW + 1)
                    sp.dma_start(ring[n], src).then_inc(v_raw[n] if n < KC else w_raw[n % NRAW], 16)
                    if n < KC:
                        sp.dma_start(rawx[:, n, :], io["xT"][:, n, :]).then_inc(in_xT[n], 16)
                    if n == KC:
                        for dst, name in ((pos, "pos"), (bqk, "bqk"), (parity, "parity"), (own, "own"), (alibi, "alibi"), (ident, "ident")):
                            sp.dma_start(dst[:], io[name]).then_inc(small, 16)
                        for dst, name in ((bv, "bv"), (bp, "bp")):
                            sp.dma_start(dst[:], io[name].to_broadcast([P, D])).then_inc(small, 16)
                        sp.dma_start(xtok[:], io["x_tok"]).then_inc(in_tok, 16)
                load_ahead(sp, w_low, len(blocks), raw_of["G"], group_sources(0))

            @block.gpsimd
            def _(pool):
                nc.gpsimd.memset(zero[:], 0.0).then_inc(zeroed, 1)
                nc.gpsimd.memset(epsilon[:], EPS).then_inc(zeroed, 1)
                pool.wait_ge(zeroed, 2)
                for n, (_, dst) in enumerate(blocks):
                    if n < KC:
                        pool.wait_ge(v_raw[n], 16)
                    else:
                        pool.wait_ge(w_raw[n % NRAW], 16 * ((n - KC) // NRAW + 1))
                    if KC + 2 <= n < 3 * KC:
                        c, a = (n - KC) // 2, (n - KC) % 2
                        pool.wait_ge(a_ready, banks_before(c - 1, 3 + a))
                    high_part(dst[0], ring[n]).then_inc(w_high, 1)
                    pool.wait_ge(w_high, n + 1)
                    nc.gpsimd.tensor_tensor(dst[1], ring[n], f32(dst[0]), ALU.subtract).then_inc(w_low, 1)
                    if n == KC - 1:
                        for k in kt:
                            nc.gpsimd.memset(k[:], 0.0).then_inc(zeroed, 1)
                    if n == KC + 3:
                        pool.wait_ge(small, 128)
                        pool.wait_ge(in_tok, 16)
                        for t in range(NT):
                            nc.gpsimd.tensor_tensor(xtok[:, t, :], xtok[:, t, :], bp[:], ALU.add).then_inc(pbias, 1)
                pool.wait_ge(clamped, 1)
                pool.wait_ge(a_ready, banks_before(KC, 0))
                for t in range(NT):
                    nc.gpsimd.indirect_dma_start(out=table_rows[:, t, :], out_offset=None, in_=io["rope"],
                                                 in_offset=bass.IndirectOffsetOnAxis(ap=row[:, t:t + 1], axis=0)).then_inc(gathered, 16)

            @block.tensor
            def _(pe):
                for k in range(KC):
                    pe.wait_ge(w_low, k + 1)
                    pe.wait_ge(in_low, k + 1)
                    for t in range(NT):
                        done = product(vbank[t], three([w[:, k, t * P:(t + 1) * P] for w in xT], [w[:, k, :] for w in wbig]), start=k == 0, stop=k == KC - 1)
                        if k == KC - 1:
                            done.then_inc(a_ready, 1)

                def project(c, i, chunks):
                    a, h = i % 2, i // 2
                    if 0 in chunks:
                        if h == 0:
                            pe.wait_ge(w_low, KC + 2 * c + a + 1)
                        if c == 0 and h == 0:
                            pe.wait_ge(v_done, a + 1)
                        else:
                            pe.wait_ge((k_done, q_done)[a], 2 * c + h)
                    cols = slice(h * HALF, (h + 1) * HALF)
                    done = product(bankY[a][:], [x for k in chunks for x in three([w[:, a, k, :] for w in wqk], [w[:, k, cols] for w in xT])],
                                   start=0 in chunks, stop=KC - 1 in chunks)
                    if KC - 1 in chunks:
                        done.then_inc(a_ready, 1)

                def scores(n):
                    c, quad, m = slot(n)
                    if n == 0:
                        pe.wait_ge(v_done, 4)
                    if n % PER_CHUNK == 0:
                        pe.wait_ge(k_done, 2 * (c + 1))
                    if m == 0:
                        pe.wait_ge(m_done, HEADS * (n // 4 + 1))
                    if n >= 2:
                        pe.wait_ge(st["masked"], n - 1)
                    for j in range(4):
                        done = nc.tensor.matmul(bankA[n % 2][:, j * P:(j + 1) * P], qm[quad % 2][:, j, 2 * m:2 * m + 2, :].rearrange("p e q -> p (e q)"),
                                                window(kt[c % 2], quad * 4 + j, slice(None)), start=True, stop=True)
                    done.then_inc(s_ready, 1)

                def output(t, half):
                    if t == 0 and half == 0:
                        pe.wait_ge(w_low, 3 * KC + 2)
                        pe.wait_ge(k_done, 2 * KC)
                        pe.wait_ge(q_done, 2 * KC)
                    if half == 0:
                        pe.wait_ge(o_low, 3 * QUADS + t // 2 + 1)
                        if t >= 2:
                            pe.wait_ge(y_done, t - 1)
                    done = product(bankY[t % 2][:], [x for k in (2 * half, 2 * half + 1) for x in three([w[:, k, t * P:(t + 1) * P] for w in oT], [w[:, k, :] for w in wbig])],
                                   start=half == 0, stop=half == 1)
                    if half:
                        done.then_inc(y_ready, 1)

                for i in range(4):
                    project(0, i, range(KC))
                for n in range(AHEAD):
                    scores(n)
                pe.wait_ge(small, 128)
                pe.wait_ge(v_done, NT)
                for n in range(UNITS):
                    c, quad, m = slot(n)
                    pe.wait_ge(st["prob"], n + 1)
                    if n >= 2:
                        pe.wait_ge(pt_done, n - 1)
                    for j in range(2):
                        done = nc.tensor.transpose(bankT[n % 2][:, j * P:(j + 1) * P], sc[n % 3][:, j].rearrange("p b k -> p (b k)"), ident[:])
                    done.then_inc(t_ready, 1)
                    if n + AHEAD < UNITS:
                        scores(n + AHEAD)
                    if c + 1 < KC:
                        project(c + 1, n // 4 % 4, [n % 4])
                    if n >= OUTPUT_AT:
                        output((n - OUTPUT_AT) // 2, n % 2)
                    pe.wait_ge(pt_done, n + 1)
                    if m == 0 and n:
                        pe.wait_ge(o_even, n // 2)
                        pe.wait_ge(o_odd, n // 2)
                    for j in range(4):
                        b, par, bpair = quad * 4 + j, j % 2, j // 2
                        rows = slice(S * par, S * par + S)
                        done = nc.tensor.matmul(bankO[32 * m:32 * m + 32, par, bpair * P:(bpair + 1) * P],
                                                V[rows, b // 2, c * P + 32 * m:c * P + 32 * m + 32], pt[n % 2][rows, bpair, :], start=True, stop=True)
                    done.then_inc(o_ready, 1)
                for t in range((UNITS - OUTPUT_AT) // 2, NT):
                    output(t, 0)
                    output(t, 1)

            @block.scalar
            def _(act):
                for k in range(KC):
                    act.wait_ge(in_xT[k], 16)
                    nc.scalar.activation(xT[0][:, k, :], rawx[:, k, :], ACT.Copy).then_inc(in_high, 1)

                def drain(c, i):
                    h, half = i // 2, slice(i // 2 * HALF, (i // 2 + 1) * HALF)
                    act.wait_ge(a_ready, banks_before(c, i) + 1)
                    if i % 2 == 0:
                        if c >= 2:
                            act.wait_ge(s_ready, PER_CHUNK * (c - 1))
                        nc.scalar.activation(kt[c % 2][:, S + half.start:S + half.stop], bankY[0][:], ACT.Identity, bias=bqk[:, 1, c:c + 1]).then_inc(k_done, 1)
                    else:
                        if c:
                            act.wait_ge(m_done, HEADS * (4 * c - 2 + 2 * h))
                        nc.scalar.activation(q[:, half], bankY[1][:], ACT.Identity, bias=bqk[:, 0, c:c + 1]).then_inc(q_done, 1)

                def by_head(step):
                    g, part = step // 4, step % 4
                    if part == 0:
                        act.wait_ge(q_done, g // 2 + 1)
                        if g >= 2:
                            act.wait_ge(s_ready, 4 * (g - 1))
                    for e in (2 * part, 2 * part + 1):
                        nc.scalar.activation(qm[g % 2][:, :, e, :], q[:, g % QUADS * 256:(g % QUADS + 1) * 256].rearrange("p (b s) -> p b s", s=S),
                                             ACT.Copy, scale=own[:, e:e + 1]).then_inc(m_done, 1)

                def exp(n):
                    act.wait_ge(st["sub"], n + 1)
                    tile = sc[n % 3][:].rearrange("p a b k -> p (a b k)")
                    nc.scalar.activation(tile, tile, ACT.Exp).then_inc(st["exp"], 1)

                def split(g):
                    c, quad = g // QUADS, g % QUADS
                    act.wait_ge(o_odd, 2 * (g + 1))
                    nc.scalar.activation(oT[0][:, c, quad * 256:(quad + 1) * 256], od[:].rearrange("p a b k -> p (a b k)"), ACT.Copy).then_inc(o_high, 1)

                act.wait_ge(small, 128)
                act.wait_ge(zeroed, 4)
                for i in range(4):
                    drain(0, i)
                    if i == 1:
                        for step in range(4):
                            by_head(step)
                for step in range(4, 7):
                    by_head(step)
                exp(0)
                exp(1)
                for n in range(UNITS):
                    act.wait_ge(t_ready, n + 1)
                    if n >= 2:
                        act.wait_ge(o_ready, n - 1)
                    nc.scalar.activation(pt[n % 2][:].rearrange("p a b -> p (a b)"), bankT[n % 2][:, 0:256], ACT.Copy).then_inc(pt_done, 1)
                    if n % 4 == 0 and n:
                        if n <= UNITS - PER_CHUNK:
                            drain((n + 12) // PER_CHUNK, (n // 4 - 1) % 4)
                        split(n // 4 - 1)
                    if n + 2 < UNITS:
                        exp(n + 2)
                    if n + 7 < UNITS:
                        by_head(n + 7)
                split(UNITS // 4 - 1)
                ln_roots(act, 0, 0)
                ln_rest(act, 0)

            @block.vector
            def _(dve):
                for k in range(KC):
                    dve.wait_ge(in_high, k + 1)
                    nc.vector.tensor_tensor(xT[1][:, k, :], rawx[:, k, :], f32(xT[0][:, k, :]), ALU.subtract).then_inc(in_low, 1)

                def values(t):
                    dve.wait_ge(a_ready, t + 1)
                    nc.vector.tensor_tensor(V[:, t, :], vbank[t], bv[:], ALU.add).then_inc(v_done, 1)

                def front(n):
                    c, quad, m = slot(n)
                    s4 = sc[n % 3][:].rearrange("p a b k -> p (a b) k")
                    dve.wait_ge(s_ready, n + 1)
                    if n >= 3:
                        dve.wait_ge(t_ready, n - 2)
                    nc.vector.scalar_tensor_tensor(sc[n % 3][:].rearrange("p a b k -> p a (b k)"), bankA[n % 2][:].rearrange("p (a c) -> p a c", a=2)[:, :, S:S + P], 1.0 / A_HD,
                                                   alibi[:, c * 4 + m, :].unsqueeze(1).to_broadcast([P, 2, P]), ALU.mult, ALU.add).then_inc(st["masked"], 1)
                    yield
                    dve.wait_ge(st["masked"], n + 1)
                    nc.vector.tensor_reduce(mx[:, n % 2, :], s4, AXX, ALU.max).then_inc(st["max"], 1)
                    yield
                    dve.wait_ge(st["max"], n + 1)
                    nc.vector.tensor_tensor(s4, s4, mx[:, n % 2, :].unsqueeze(2).to_broadcast([P, 4, S]), ALU.subtract).then_inc(st["sub"], 1)

                def back(n):
                    s4 = sc[n % 3][:].rearrange("p a b k -> p (a b) k")
                    dve.wait_ge(st["exp"], n + 1)
                    nc.vector.tensor_reduce(sm[:, n % 2, :], s4, AXX, ALU.add).then_inc(st["sum"], 1)
                    yield
                    dve.wait_ge(st["sum"], n + 1)
                    nc.vector.reciprocal(ri[:, n % 2, :], sm[:, n % 2, :]).then_inc(st["inv"], 1)
                    yield
                    dve.wait_ge(st["inv"], n + 1)
                    nc.vector.tensor_tensor(s4, s4, ri[:, n % 2, :].unsqueeze(2).to_broadcast([P, 4, S]), ALU.mult).then_inc(st["prob"], 1)

                def gather(g):
                    dve.wait_ge(o_ready, 4 * g + 4)
                    for par in range(2):
                        nc.vector.tensor_scalar(oc[:, :, par, :], bankO[:, par, 0:256].rearrange("p (a c) -> p a c", a=2)[:, :, 0:S],
                                                parity[:, 0:1], None, ALU.mult).then_inc(o_even, 1)
                    yield
                    dve.wait_ge(o_even, 2 * g + 2)
                    if g:
                        dve.wait_ge(o_low, g)
                    for par in range(2):
                        nc.vector.scalar_tensor_tensor(od[:, :, par, :], bankO[:, par, 0:256].rearrange("p (a c) -> p a c", a=2)[:, :, S:P],
                                                       parity[:, 1:2], oc[:, :, par, :], ALU.mult, ALU.add).then_inc(o_odd, 1)

                def low(g):
                    c, cols = g // QUADS, slice(g % QUADS * 256, (g % QUADS + 1) * 256)
                    dve.wait_ge(o_high, g + 1)
                    nc.vector.tensor_tensor(oT[1][:, c, cols], od[:].rearrange("p a b k -> p (a b k)"), f32(oT[0][:, c, cols]), ALU.subtract).then_inc(o_low, 1)

                def residual(t):
                    dve.wait_ge(y_ready, t + 1)
                    dve.wait_ge(pbias, t + 1)
                    nc.vector.tensor_tensor(xtok[:, t, :], xtok[:, t, :], bankY[t % 2][:], ALU.add).then_inc(y_done, 1)
                    dve.wait_ge(y_done, t + 1)
                    ln_follow(dve, 0, t)

                dve.wait_ge(small, 128)
                nc.vector.tensor_scalar(row[:], pos[:], 0, ROPE_ROWS - 1, ALU.max, ALU.min).then_inc(clamped, 1)
                for t in range(NT):
                    values(t)
                dve.wait_ge(v_done, NT)
                in_turns(front(0))
                in_turns(front(1), back(0))
                for n in range(UNITS):
                    in_turns(gather(n // 4 - 1) if n % 4 == 0 and n else None, front(n + 2) if n + 2 < UNITS else None, back(n + 1) if n + 1 < UNITS else None)
                    if n % 4 == 1 and n > 4:
                        low(n // 4 - 1)
                    if n > OUTPUT_AT and n % 2:
                        residual((n - OUTPUT_AT) // 2)
                in_turns(gather(UNITS // 4 - 1))
                low(UNITS // 4 - 1)
                for t in range((UNITS - OUTPUT_AT) // 2, NT):
                    residual(t)
    SLOTS = 2 * NT
    KEYS_AT = SLOTS - 3
    VALUES_AT = {10: 4, 12: 5, 14: 6, 15: 7}

    def slot_banks(u, final):
        banks = []
        if u + 2 < SLOTS or not final:
            banks.append(("S", u + 2))
        if u in VALUES_AT and not final:
            banks.append(("V", VALUES_AT[u]))
        if u + 6 < SLOTS or not final:
            banks.append(("Q", u + 6))
        if u == KEYS_AT and not final:
            banks += [("K", n) for n in range(4, 8)]
        return banks

    def late(u):
        return u % 4 == 2

    START = [("V", n) for n in range(4)] + [("K", n) for n in range(4)] + [("Q", n) for n in range(4)] + [("Q", 4), ("S", 0), ("S", 1), ("Q", 5)]
    TURN = [x for u in range(SLOTS) for x in slot_banks(u, False)]
    LAST = [x for u in range(SLOTS) for x in slot_banks(u, True)]
    only_qk = lambda order: [x for x in order if x[0] in "QK"]
    TURN_BANKS, TURN_QK = len(TURN), len(only_qk(TURN))
    START_BLOCKS = ["v", "k", "q0", "q1"]
    TURN_BLOCKS = ["o0", "o1", "q0", "q1", "k", "v", "o2", "o3", "q2", "q3"]
    LAST_BLOCKS = ["o0", "o1", "q0", "q1", "o2", "o3"]

    class Part:
        def __init__(self, it, order, blocks):
            started = order is not START
            self.it, self.order, self.blocks, self.final = it, order, blocks, order is LAST
            self.banks, self.qks, self.weights = it * TURN_BANKS, it * TURN_QK, it * len(TURN_BLOCKS)
            if started:
                self.banks, self.qks, self.weights = self.banks + len(START), self.qks + len(only_qk(START)), self.weights + len(START_BLOCKS)

        def bank(self, x):
            return self.banks + (self.order.index(x) if x in self.order else -1)

        def qk(self, x):
            return self.qks + (only_qk(self.order).index(x) if x in self.order else -1)

        def buffer(self, x):
            return (self.order.index(x) if x in self.order else -1) % 2

        def swap(self, x):
            return (only_qk(self.order).index(x) if x in self.order else -1) % 2

        def block(self, name):
            return self.weights + self.blocks.index(name) + 1

        def unit(self, u):
            return self.it * SLOTS + u

    assert not any(len(x) % 2 for x in (START, TURN, LAST, START_BLOCKS, TURN_BLOCKS, LAST_BLOCKS))
    group_names = ("w_high", "w_low", "padded", "a_ready", "swapped", "roped", "turned", "qk_done", "v_done",
                   "t_ready", "pt_done", "o_ready", "o_high", "o_low", "wo_used", "y_ready", "y_done")
    group_sems = [raw_of["G"], softmax_stages("G")] + [sem("G_" + name) for name in group_names]
    tabled = sem("G_tabled"); flipped = sem("G_flipped"); bounded = sem("G_bounded"); in_bound = sem("G_inbound")

    def grouped_attention(tag, norm, first, source, rope, following):
        w_raw, st, w_high, w_low, padded, a_ready, swapped, roped, turned, qk_done, v_done, \
            t_ready, pt_done, o_ready, o_high, o_low, wo_used, y_ready, y_done = group_sems
        final = first + NPAIR - 1
        with ExitStack() as mem:
            with ExitStack() as early:
                sb(early, f"{tag}rows", [P, NT, 2 * P])
                mask = sb(early, f"{tag}mask", [P, NT, P], I32); hidden = sb(early, f"{tag}hidden", [P, NT, P])
            qT = sb(mem, f"{tag}qT", [P, B, GROUP, S])
            wk = [sb(mem, f"{tag}wk{i}", [P, 2, KC, HD], F32R) for i in range(2)]
            wv = [sb(mem, f"{tag}wv{i}", [P, KC, 2 * HD], F32R) for i in range(2)]
            wq = [sb(mem, f"{tag}wq{i}", [P, GROUP, KC, HD], F32R) for i in range(2)]
            wo = [sb(mem, f"{tag}wo{i}", [P, GROUP, D], F32R) for i in range(2)]
            kt = sb(mem, f"{tag}kt", [P, 2, WINDOW])
            V = sb(mem, f"{tag}V", [P, NT, 2 * HD])
            sc = [sb(mem, f"{tag}sc{i}", [P, 2, 2, S]) for i in range(4)]
            pt = [sb(mem, f"{tag}pt{i}", [P, GROUP * S]) for i in range(2)]
            oT = [[sb(mem, f"{tag}oT{i}{p}", [P, GROUP, 2, S], F32R) for p in range(2)] for i in range(2)]
            mx = sb(mem, f"{tag}mx", [P, 2, 4]); sm = sb(mem, f"{tag}sm", [P, 2, 4]); ri = sb(mem, f"{tag}ri", [P, 2, 4])
            if rope:
                sw = [sb(mem, f"{tag}sw{i}", [P, HALF]) for i in range(2)]
                table = sb(mem, f"{tag}table", [P, 2, TOK]); bound = sb(mem, f"{tag}bound", [P, NT, P])
            else:
                bound = sb(mem, f"{tag}bound", [P, P])
            bound_of = lambda u: bound[:, u % NT, :] if rope else bound[:]

            def halves(pair, pattern):
                flat = [w[:].rearrange(pattern) for w in pair]
                return [[f[:, i * BLK:(i + 1) * BLK] for f in flat] for i in range(2)]

            dst = {"k": [w[:].rearrange("p h k n -> p (h k n)") for w in wk], "v": [w[:].rearrange("p k n -> p (k n)") for w in wv]}
            for i, (q, o) in enumerate(zip(halves(wq, "p h k n -> p (h k n)"), halves(wo, "p h n -> p (h n)"))):
                dst[f"q{i}"] = dst[f"q{i + 2}"] = q
                dst[f"o{i}"] = dst[f"o{i + 2}"] = o

            def run(engine, start, turn):
                start(Part(first, START, START_BLOCKS))
                with engine.Fori(first, final) as it:
                    turn(Part(it, TURN, TURN_BLOCKS))
                turn(Part(final, LAST, LAST_BLOCKS))

            with nc.Block() as block:
                @block.sync
                def _(sp):
                    if rope:
                        sp.dma_start(mask[:], io["mask"]).then_inc(in_bound, 16)
                    else:
                        sp.dma_start(bound[:], io["causal"]).then_inc(in_bound, 16)

                    def load(part):
                        for n in range(len(part.blocks)):
                            at = part.weights + n
                            if part.order is START and n < NRAW:
                                continue
                            sp.wait_ge(w_low, at - 1)
                            src = io["w_attn"][at] if part.order is not TURN else io["w_attn"][bass.ds(at, 1)].rearrange("a p c -> p (a c)")
                            sp.dma_start(raw[n % 2][:], src).then_inc(w_raw[n % 2], 16)
                    run(sp, load, load)
                    load_ahead(sp, w_low, (first + NPAIR) * len(TURN_BLOCKS), *following)

                @block.gpsimd
                def _(pool):
                    def split(part):
                        for n, name in enumerate(part.blocks):
                            if part.order is not START:
                                if name == "o0":
                                    pool.wait_ge(wo_used, part.it * 2 + 1)
                                elif name == "o1":
                                    pool.wait_ge(y_done, part.it * SLOTS + 2)
                                elif name == "o2":
                                    pool.wait_ge(wo_used, part.it * 2 + 2)
                                elif name == "o3":
                                    pool.wait_ge(y_done, part.it * SLOTS + NT + 2)
                                else:
                                    used = {"q0": ("Q", 5), "q1": ("Q", 7), "k": ("Q", 5), "v": ("Q", 5), "q2": ("Q", 13), "q3": ("Q", 15)}[name]
                                    pool.wait_ge(a_ready, part.bank(used) + 1)
                            pool.wait_ge(w_raw[n % 2], (part.weights + n - n % 2) * 8 + 16)
                            high_part(dst[name][0], raw[n % 2][:]).then_inc(w_high, 1)
                            pool.wait_ge(w_high, part.weights + n + 1)
                            nc.gpsimd.tensor_tensor(dst[name][1], raw[n % 2][:], f32(dst[name][0]), ALU.subtract).then_inc(w_low, 1)
                            if part.order is START and name == "k":
                                nc.gpsimd.memset(kt[:], 0.0).then_inc(padded, 1)
                    run(pool, split, split)

                @block.tensor
                def _(pe):
                    if first == 0:
                        pe.sem_inc(wo_used, 1)
                    ln_tensor(pe, norm)
                    if rope:
                        pe.wait_ge(gathered, 16 * NT)
                        for t in range(NT):
                            if t >= 2:
                                pe.wait_ge(tabled, t - 1)
                            for i in range(2):
                                done = nc.tensor.transpose(bankO[:, t % 2, i * P:(i + 1) * P], table_rows[:, t, i * P:(i + 1) * P], ident[:])
                            done.then_inc(flipped, 1)

                    def wait_drained(part, x):
                        kind, n = x
                        if kind == "S":
                            pe.wait_ge(st["masked"], part.unit(n) + 1)
                        elif kind == "V":
                            pe.wait_ge(v_done, part.it * 4 + n + 1)
                        else:
                            pe.wait_ge(roped if rope else qk_done, part.qk(x) + 1)

                    def take(part, x):
                        at = part.order.index(x)
                        if at >= 2:
                            wait_drained(part, part.order[at - 2])
                        elif part.order is not START:
                            wait_drained(part, ("Q", 5) if at else ("S", 1))
                            if at == 0:
                                wait_drained(part, ("V", 3))
                        return bankA[part.buffer(x)]

                    def project(part, x):
                        bank, (kind, n) = take(part, x), x
                        if part.order is START and not (rope and kind in "KV"):
                            tiles = {"V": 2 * n + 2, "K": NT // 2 * (n % 2 + 1), "Q": NT // 2 * (n // 4 + 1), "S": NT // 2}[kind]
                            pe.wait_ge(ln_low, norm * NT + tiles)
                        if kind == "K":
                            if part.order is START and n == 0:
                                pe.wait_ge(padded, first // NPAIR + 1)
                            if n % 4 == 0:
                                pe.wait_ge(w_low, part.block("k"))
                            cols = slice(n % 2 * HALF, (n % 2 + 1) * HALF)
                            done = product(bank[:], [x for k in range(KC) for x in three([w[:, n // 2 % 2, k, :] for w in wk], [s[:, k, cols] for s in source])])
                        elif kind == "Q":
                            if n % 8 in (0, 2):
                                pe.wait_ge(w_low, part.block({0: "q0", 2: "q1", 8: "q0", 10: "q1", 16: "q2", 18: "q3"}[n]))
                            cols = slice(n // 4 % 2 * HALF, (n // 4 % 2 + 1) * HALF)
                            done = product(bank[:], [x for k in range(KC) for x in three([w[:, n % 4, k, :] for w in wq], [s[:, k, cols] for s in xT])])
                        elif kind == "V":
                            if n % 4 == 0:
                                pe.wait_ge(w_low, part.block("v"))
                            for t in (n % 4 * 2, n % 4 * 2 + 1):
                                done = product(bank[:, t % 2 * 256:t % 2 * 256 + 256],
                                               [x for k in range(KC) for x in three([s[:, k, t * P:(t + 1) * P] for s in source], [w[:, k, :] for w in wv])])
                        else:
                            t, j = n % NT, n // NT % 2
                            if n % 4 == 0:
                                needed = ("K", 7) if n == SLOTS else ("Q", n // NT * 8 + (3 if t == 0 else 7))
                                pe.wait_ge(qk_done, part.qk(needed) + 1)
                            for hp in range(2):
                                for b in range(2):
                                    at = (hp * 2 + b) * P
                                    done = nc.tensor.matmul(bank[:, at:at + P], qT[:, 2 * t + b, 2 * hp:2 * hp + 2, :].rearrange("p h q -> p (h q)"),
                                                            window(kt, 2 * t + b, slice(None), j), start=True, stop=True)
                        done.then_inc(a_ready, 1)

                    def output(part, u):
                        if u % NT == 0:
                            pe.wait_ge(w_low, part.block("o3" if u else "o1"))
                        pe.wait_ge(o_low, part.unit(u) + 2)
                        pe.wait_ge(y_done, part.unit(u) + 1)
                        pairs = [x for h in range(GROUP) for x in three([o[:, h].rearrange("p b q -> p (b q)") for o in oT[u % 2]], [w[:, h, :] for w in wo])]
                        if u % NT == NT - 1:
                            product(bankY[u % 2][:], pairs[:len(pairs) // 2], stop=False).then_inc(wo_used, 1)
                            product(bankY[u % 2][:], pairs[len(pairs) // 2:], start=False).then_inc(y_ready, 1)
                        else:
                            product(bankY[u % 2][:], pairs).then_inc(y_ready, 1)

                    def start(part):
                        for x in START:
                            project(part, x)

                    def turn(part):
                        for u in range(SLOTS):
                            banks = slot_banks(u, part.final)
                            pe.wait_ge(st["prob"], part.unit(u) + 1)
                            pe.wait_ge(pt_done, part.unit(u) + 1)
                            for hp in range(2):
                                done = nc.tensor.transpose(bankT[u % 2][:, hp * P:(hp + 1) * P], sc[u % 4][:, hp].rearrange("p b k -> p (b k)"), ident[:])
                            done.then_inc(t_ready, 1)
                            if banks and banks[0][0] == "S" and not late(u):
                                project(part, banks[0])
                            if late(u):
                                output(part, u - 1)
                            if u < NT and u % 2 == 0:
                                pe.wait_ge(v_done, part.it * 4 + u // 2 + 1)
                            pe.wait_ge(pt_done, part.unit(u) + 3)
                            pe.wait_ge(o_low, part.unit(u) + 1)
                            for b in range(2):
                                rows = slice(S * b, S * b + S)
                                done = nc.tensor.matmul(bankO[:, b, 0:GROUP * S], V[rows, u % NT, u // NT * HD:(u // NT + 1) * HD], pt[u % 2][rows, :], start=True, stop=True)
                            done.then_inc(o_ready, 1)
                            if u % NT and not late(u):
                                output(part, u - 1)
                            for x in banks:
                                if x[0] != "S" or late(u):
                                    project(part, x)
                            if u % NT == NT - 1:
                                output(part, u)
                    run(pe, start, turn)

                def projected(u, final):
                    return [("Q", u + 5)] * (u % NT > 0 and (u + 5 < SLOTS or not final)) + [("K", n) for n in range(4, 8) if u == KEYS_AT + 1 and not final]

                def projected_last(u, final):
                    return [("Q", u + 6)] * (u % NT == NT - 1 and (u + 6 < SLOTS or not final))

                def half_of(x):
                    kind, n = x
                    h = n % 2 if kind == "K" else n // 4 % 2
                    if kind == "K":
                        return kt[:, n // 2 % 2, S + h * HALF:S + h * HALF + HALF].rearrange("p (b s) -> p b s", s=S), h
                    return qT[:, h * B // 2:(h + 1) * B // 2, n % 4, :], h

                @block.scalar
                def _(act):
                    ln_high_parts(act, norm)
                    if first == 0:
                        act.sem_inc(pt_done, 2)

                    def queries_or_keys(part, x):
                        act.wait_ge(a_ready, part.bank(x) + 1)
                        if rope:
                            if part.order is not START or only_qk(START).index(x) >= 2:
                                act.wait_ge(qk_done, part.qk(x) - 1)
                            for i in range(2):
                                nc.scalar.activation(sw[part.swap(x)][64 * i:64 * i + 64, :], bankA[part.buffer(x)][64 - 64 * i:P - 64 * i, :], ACT.Copy).then_inc(swapped, 1)
                        else:
                            nc.scalar.activation(half_of(x)[0], bankA[part.buffer(x)][:].rearrange("p (b s) -> p b s", s=S), ACT.Copy).then_inc(qk_done, 1)

                    def values(part, n):
                        act.wait_ge(a_ready, part.bank(("V", n)) + 1)
                        i = n % 4 * 2
                        nc.scalar.activation(V[:, i:i + 2, :].rearrange("p t n -> p (t n)"), bankA[part.buffer(("V", n))][:], ACT.Copy).then_inc(v_done, 1)

                    def exp(part, u):
                        act.wait_ge(st["sub"], part.unit(u) + 1)
                        flat = sc[u % 4][:].rearrange("p a b k -> p (a b k)")
                        nc.scalar.activation(flat, flat, ACT.Exp, scale=HD ** -0.5).then_inc(st["exp"], 1)

                    def start(part):
                        for x in START:
                            if x[0] == "V":
                                values(part, x[1])
                            elif x[0] == "S":
                                if x[1]:
                                    exp(part, 0)
                                    exp(part, 1)
                            else:
                                queries_or_keys(part, x)

                    def turn(part):
                        for u in range(SLOTS):
                            banks = projected(u, part.final)
                            if len(banks) > 1:
                                for x in banks:
                                    queries_or_keys(part, x)
                            act.wait_ge(t_ready, part.unit(u) + 1)
                            nc.scalar.activation(pt[u % 2][:], bankT[u % 2][:, 0:GROUP * S], ACT.Copy).then_inc(pt_done, 1)
                            if late(u - 1) and (u + 1 < SLOTS or not part.final):
                                exp(part, u + 1)
                            if len(banks) == 1:
                                queries_or_keys(part, banks[0])
                            act.wait_ge(o_ready, part.unit(u) + 1)
                            nc.scalar.activation(oT[u % 2][0][:].rearrange("p h b q -> p b h q"),
                                                 bankO[:, :, 0:GROUP * S].rearrange("p b (h q) -> p b h q", h=GROUP), ACT.Copy).then_inc(o_high, 1)
                            if not late(u) and (u + 2 < SLOTS or not part.final):
                                exp(part, u + 2)
                            if u in VALUES_AT and not part.final:
                                values(part, VALUES_AT[u])
                            for x in projected_last(u, part.final):
                                queries_or_keys(part, x)
                            if part.final and u == SLOTS - 2:
                                ln_roots(act, norm + 1, 0)
                            if part.final and u == SLOTS - 1:
                                ln_rest(act, norm + 1)
                    run(act, start, turn)

                @block.vector
                def _(dve):
                    ln_low_parts(dve, norm)
                    if first == 0:
                        dve.sem_inc(o_low, 1)
                        dve.sem_inc(y_done, 2)
                    dve.wait_ge(in_bound, 16 * (first // NPAIR + 1))
                    if rope:
                        nc.vector.tensor_scalar(hidden[:], mask[:], 0, -1.0e9 * HD ** 0.5, ALU.is_equal, ALU.mult).then_inc(bounded, 1)
                        nc.vector.tensor_scalar(bound[:], mask[:], 0, -OFF, ALU.not_equal, ALU.mult).then_inc(bounded, 1)
                        for t in range(NT):
                            dve.wait_ge(flipped, t + 1)
                            nc.vector.tensor_copy(table[:, :, t * P:(t + 1) * P], bankO[:, t % 2, 0:2 * P].rearrange("p (a c) -> p a c", a=2)).then_inc(tabled, 1)
                        dve.wait_ge(bounded, 2)
                        nc.vector.tensor_tensor(bound[:], bound[:], hidden[:], ALU.add).then_inc(bounded, 1)
                        dve.wait_ge(bounded, 3)
                        dve.wait_ge(tabled, NT)

                    def rotate(part, *banks):
                        for x in banks:
                            to, h = half_of(x)
                            half, b = slice(h * HALF, (h + 1) * HALF), sw[part.swap(x)]
                            dve.wait_ge(swapped, part.qk(x) * 2 + 2)
                            nc.vector.tensor_tensor(to, bankA[part.buffer(x)][:].rearrange("p (b s) -> p b s", s=S),
                                                    table[:, 0, half].rearrange("p (b s) -> p b s", s=S), ALU.mult).then_inc(roped, 1)
                            nc.vector.tensor_tensor(b[:], b[:], table[:, 1, half], ALU.mult).then_inc(turned, 1)
                            yield
                            dve.wait_ge(roped, part.qk(x) + 1)
                            dve.wait_ge(turned, part.qk(x) + 1)
                            nc.vector.tensor_tensor(to, to, b[:].rearrange("p (b s) -> p b s", s=S), ALU.add).then_inc(qk_done, 1)
                            yield

                    def front(part, u):
                        s3 = sc[u % 4][:].rearrange("p a b k -> p a (b k)")
                        s4 = sc[u % 4][:].rearrange("p a b k -> p (a b) k")
                        dve.wait_ge(a_ready, part.bank(("S", u)) + 1)
                        nc.vector.tensor_tensor(s3, bankA[part.buffer(("S", u))][:].rearrange("p (a c) -> p a c", a=2)[:, :, S:S + P],
                                                bound_of(u).unsqueeze(1).to_broadcast([P, 2, P]), ALU.min).then_inc(st["masked"], 1)
                        yield
                        dve.wait_ge(st["masked"], part.unit(u) + 1)
                        nc.vector.tensor_reduce(mx[:, u % 2, :], s4, AXX, ALU.max).then_inc(st["max"], 1)
                        yield
                        dve.wait_ge(st["max"], part.unit(u) + 1)
                        nc.vector.tensor_tensor(s4, s4, mx[:, u % 2, :].unsqueeze(2).to_broadcast([P, 4, S]), ALU.subtract).then_inc(st["sub"], 1)

                    def back(part, u):
                        s4 = sc[u % 4][:].rearrange("p a b k -> p (a b) k")
                        dve.wait_ge(st["exp"], part.unit(u) + 1)
                        nc.vector.tensor_reduce(sm[:, u % 2, :], s4, AXX, ALU.add).then_inc(st["sum"], 1)
                        yield
                        dve.wait_ge(st["sum"], part.unit(u) + 1)
                        nc.vector.reciprocal(ri[:, u % 2, :], sm[:, u % 2, :]).then_inc(st["inv"], 1)
                        yield
                        dve.wait_ge(st["inv"], part.unit(u) + 1)
                        nc.vector.tensor_tensor(s4, s4, ri[:, u % 2, :].unsqueeze(2).to_broadcast([P, 4, S]), ALU.mult).then_inc(st["prob"], 1)

                    def residual(part, u):
                        t = u % NT
                        dve.wait_ge(y_ready, part.unit(u) + 1)
                        nc.vector.tensor_tensor(xtok[:, t, :], xtok[:, t, :], bankY[u % 2][:], ALU.add).then_inc(y_done, 1)
                        if part.final and u >= NT:
                            dve.wait_ge(y_done, part.unit(u) + 3)
                            ln_follow(dve, norm + 1, t)

                    def start(part):
                        if rope:
                            in_turns(rotate(part, *only_qk(START)[:8]))
                        in_turns(rotate(part, ("Q", 4)) if rope else None, front(part, 0))
                        in_turns(front(part, 1), back(part, 0))
                        if rope:
                            in_turns(rotate(part, ("Q", 5)))

                    def turn(part):
                        for u in range(SLOTS):
                            banks = projected(u, part.final)
                            scores = front(part, u + 2) if u + 2 < SLOTS or not part.final else None
                            in_turns(rotate(part, *banks) if rope and banks else None,
                                     None if late(u) else scores,
                                     back(part, u + 1) if u + 1 < SLOTS or not part.final else None)
                            if u % NT >= 2:
                                residual(part, u - 2)
                            dve.wait_ge(o_high, part.unit(u) + 1)
                            nc.vector.tensor_tensor(oT[u % 2][1][:].rearrange("p h b q -> p b h q"), bankO[:, :, 0:GROUP * S].rearrange("p b (h q) -> p b h q", h=GROUP),
                                                    f32(oT[u % 2][0][:]).rearrange("p h b q -> p b h q"), ALU.subtract).then_inc(o_low, 1)
                            if late(u):
                                in_turns(scores)
                            if u % NT == NT - 1:
                                residual(part, u - 1)
                                if rope:
                                    in_turns(rotate(part, *projected_last(u, part.final)))
                                residual(part, u)
                    run(dve, start, turn)

    grouped_attention("B", 0, 0, cT, True, (raw_of["C"], [(raw[0][:], io["war"]), (raw[1][:], io["wb"][:, 0:BLK])]))

    def block_loader(sp, blocks, raw, w_raw, w_low):
        for n, (src, rows, cols, *_) in enumerate(blocks):
            if n >= NRAW:
                sp.wait_ge(w_low, n - NRAW + 1)
                sp.dma_start(raw[n % NRAW][0:rows, 0:cols], src).then_inc(w_raw[n % NRAW], 16)

    def split_block(pool, n, rows, cols, dst, raw, w_raw, w_high, w_low):
        src = raw[n % NRAW][0:rows, 0:cols]
        pool.wait_ge(w_raw[n % NRAW], 16 * (n // NRAW + 1))
        high_part(dst[0], src).then_inc(w_high, 1)
        pool.wait_ge(w_high, n + 1)
        nc.gpsimd.tensor_tensor(dst[1], src, f32(dst[0]), ALU.subtract).then_inc(w_low, 1)

    w_raw = raw_of["C"]; w_high = sem("C_whigh"); w_low = sem("C_wlow")
    small = sem("C_small"); a_ready = sem("C_aready"); a_done = sem("C_adone"); route = sem("C_route"); route_exp = sem("C_rexp")
    t_ready = sem("C_tready"); m_high = sem("C_mhigh"); m_low = sem("C_mlow"); y_ready = sem("C_yready"); y_done = sem("C_ydone")
    ER = EXPERTS * RANK
    with ExitStack() as mem:
        war = [sb(mem, f"Cwar{i}", [P, KC, 256], F32R) for i in range(2)]
        wb = [sb(mem, f"Cwb{i}", [P, KC, D], F32R) for i in range(2)]
        wup = [sb(mem, f"Cwup{i}", [P, D], F32R) for i in range(2)]
        mid = sb(mem, "Cmid", [P, NT, ER]); lg = sb(mem, "Clg", [P, NT, EXPERTS])
        earlier = sb(mem, "Cearlier", [P, EXPERTS, EXPERTS])
        top = sb(mem, "Ctop", [P, NT]); pr = sb(mem, "Cpr", [P, NT, EXPERTS]); gate = sb(mem, "Cgate", [P, NT, EXPERTS])
        above = sb(mem, "Cabove", [P, NT, EXPERTS, EXPERTS]); ties = sb(mem, "Cties", [P, NT, EXPERTS, EXPERTS])
        mT = [sb(mem, f"CmT{i}", [P, TOK], F32R) for i in range(2)]
        ybank = [bankY[0][:], bankY[1][:], bankO[:, 0, :], bankO[:, 1, :]]
        flat = lambda pair: [w[:].rearrange("p k n -> p (k n)") for w in pair]
        blocks = [(io["war"], P, BLK, flat(war))]
        blocks += [(io["wb"][:, i * BLK:(i + 1) * BLK], P, BLK, [w[:, i * BLK:(i + 1) * BLK] for w in flat(wb)]) for i in range(2)]
        blocks += [(io["wup"], P, D, [w[:] for w in wup])]
        with nc.Block() as block:
            @block.sync
            def _(sp):
                sp.dma_start(earlier[:], io["earlier"]).then_inc(small, 16)
                block_loader(sp, blocks, raw, w_raw, w_low)
                load_ahead(sp, w_low, len(blocks), raw_of["G"], group_sources(NPAIR))

            @block.gpsimd
            def _(pool):
                for n, (_, rows, cols, dst) in enumerate(blocks):
                    split_block(pool, n, rows, cols, dst, raw, w_raw, w_high, w_low)

            @block.tensor
            def _(pe):
                tok = lambda t: slice(t * P, (t + 1) * P)
                ln_tensor(pe, 1)
                pe.wait_ge(w_low, 1)
                for t in range(NT):
                    pe.wait_ge(ln_low, NT + t + 1)
                    if t >= 2:
                        pe.wait_ge(a_done, 2 * (t - 1))
                    product(bankA[t % 2][:, 0:256], [x for k in range(KC) for x in three([s[:, k, tok(t)] for s in xT], [w[:, k, :] for w in war])]).then_inc(a_ready, 1)

                def dense(t):
                    if t >= 4:
                        pe.wait_ge(y_done, t - 3)
                    product(ybank[t % 4], [x for k in range(KC) for x in three([s[:, k, tok(t)] for s in xT], [w[:, k, :] for w in wb])], stop=False)

                def experts(t):
                    product(ybank[t % 4], three([m[:, tok(t)] for m in mT], [w[:] for w in wup]), start=False).then_inc(y_ready, 1)

                pe.wait_ge(w_low, 3)
                for t in range(4):
                    dense(t)
                pe.wait_ge(w_low, 4)
                pe.wait_ge(route, 15)
                for t in range(NT):
                    done = nc.tensor.transpose(bankT[t // 4][:, t % 4 * P:(t % 4 + 1) * P], mid[:, t, :], ident[:])
                    if t % 4 == 3:
                        done.then_inc(t_ready, 1)
                pe.wait_ge(m_low, 1)
                experts(0)
                experts(1)
                for t in range(4, NT):
                    dense(t)
                    if t == 6:
                        pe.wait_ge(m_low, 2)
                    experts(t - 2)
                experts(NT - 2)
                experts(NT - 1)

            @block.scalar
            def _(act):
                ln_high_parts(act, 1)
                for t in range(NT):
                    act.wait_ge(a_ready, t + 1)
                    nc.scalar.activation(mid[:, t, :], bankA[t % 2][:, 0:ER], ACT.Copy).then_inc(a_done, 1)
                    nc.scalar.activation(lg[:, t, :], bankA[t % 2][:, ER:ER + EXPERTS], ACT.Copy).then_inc(a_done, 1)
                act.wait_ge(route, 2)
                nc.scalar.activation(pr[:].rearrange("p t e -> p (t e)"), pr[:].rearrange("p t e -> p (t e)"), ACT.Exp).then_inc(route_exp, 1)
                for h in range(2):
                    act.wait_ge(t_ready, h + 1)
                    nc.scalar.activation(mT[0][:, h * HALF:(h + 1) * HALF], bankT[h][:], ACT.Copy).then_inc(m_high, 1)
                ln_roots(act, 2, 0)
                ln_rest(act, 2)

            def add(dve, t):
                dve.wait_ge(y_ready, t + 1)
                nc.vector.tensor_tensor(xtok[:, t, :], xtok[:, t, :], ybank[t % 4], ALU.add).then_inc(y_done, 1)
                dve.wait_ge(y_done, t + 1)
                ln_follow(dve, 2, t, early=1)

            @block.vector
            def _(dve):
                ln_low_parts(dve, 1)
                wide = lambda v: v[:].unsqueeze(2).to_broadcast([P, NT, EXPERTS])
                pairs = [P, NT, EXPERTS, EXPERTS]
                steps = [0]

                def step(ins):
                    ins.then_inc(route, 1)
                    steps[0] += 1
                    dve.wait_ge(route, steps[0])

                dve.wait_ge(a_done, 2 * NT)
                dve.wait_ge(small, 16)
                step(nc.vector.tensor_reduce(top[:], lg[:], AXX, ALU.max))
                nc.vector.tensor_tensor(pr[:], lg[:], wide(top), ALU.subtract).then_inc(route, 1)
                steps[0] += 1
                dve.wait_ge(route_exp, 1)
                step(nc.vector.tensor_reduce(top[:], pr[:], AXX, ALU.add))
                step(nc.vector.reciprocal(top[:], top[:]))
                step(nc.vector.tensor_tensor(pr[:], pr[:], wide(top), ALU.mult))
                other, own = pr[:].unsqueeze(2).to_broadcast(pairs), pr[:].unsqueeze(3).to_broadcast(pairs)
                step(nc.vector.tensor_tensor(above[:], other, own, ALU.is_gt))
                step(nc.vector.tensor_tensor(ties[:], other, own, ALU.is_equal))
                step(nc.vector.tensor_tensor(ties[:].rearrange("p t a b -> p t (a b)"), ties[:].rearrange("p t a b -> p t (a b)"),
                                             earlier[:].rearrange("p a b -> p (a b)").unsqueeze(1).to_broadcast([P, NT, EXPERTS * EXPERTS]), ALU.mult))
                step(nc.vector.tensor_tensor(above[:], above[:], ties[:], ALU.add))
                step(nc.vector.tensor_reduce(gate[:].rearrange("p t e -> p (t e)"), above[:].rearrange("p t a b -> p (t a) b"), AXX, ALU.add))
                step(nc.vector.scalar_tensor_tensor(gate[:], gate[:], 2.0, pr[:], ALU.is_lt, ALU.mult))
                step(nc.vector.tensor_reduce(top[:], gate[:], AXX, ALU.add))
                step(nc.vector.reciprocal(top[:], top[:]))
                step(nc.vector.scalar_tensor_tensor(gate[:], gate[:], 2.0, wide(top), ALU.mult, ALU.mult))
                nc.vector.tensor_tensor(mid[:].rearrange("p t (e r) -> p t e r", e=EXPERTS), mid[:].rearrange("p t (e r) -> p t e r", e=EXPERTS),
                                        gate[:].unsqueeze(3).to_broadcast([P, NT, EXPERTS, RANK]), ALU.mult).then_inc(route, 1)
                for h in range(2):
                    dve.wait_ge(m_high, h + 1)
                    nc.vector.tensor_tensor(mT[1][:, h * HALF:(h + 1) * HALF], bankT[h][:], f32(mT[0][:, h * HALF:(h + 1) * HALF]), ALU.subtract).then_inc(m_low, 1)
                for t in range(NT):
                    add(dve, t)

    grouped_attention("D", 2, NPAIR, xT, False, (raw_of["E"], [(raw[i][:], io["wq2"][:, i * BLK:(i + 1) * BLK]) for i in range(NRAW)]))

    w_raw = raw_of["E"]; w_high = sem("E_whigh"); w_low = sem("E_wlow")
    small = sem("E_small"); a_ready = sem("E_aready"); q_done = sem("E_qdone"); s_ready = sem("E_sready"); st = softmax_stages("E")
    t_ready = sem("E_tready"); p_high = sem("E_phigh"); p_low = sem("E_plow"); y_ready = sem("E_yready"); y_done = sem("E_ydone")
    with ExitStack() as mem:
        w2 = [[sb(mem, f"Ew{a}{i}", [P, KC, KC, P], F32R) for i in range(2)] for a in range(2)]
        ft = [sb(mem, f"Eft{i}", [P, NT, D], F32R) for i in range(2)]
        qk = [sb(mem, f"Eqk{a}", [P, KC, TOK]) for a in range(2)]
        bias = sb(mem, "Ebias", [P, 2, KC]); same = sb(mem, "Esame", [P, P])
        sc = [sb(mem, f"Esc{i}", [P, 4, P]) for i in range(2)]
        pT = [sb(mem, f"EpT{i}", [P, NT, P], F32R) for i in range(2)]
        mx = sb(mem, "Emx", [P, 2, 4])
        blocks = []
        for a, name in enumerate(("wq2", "wk2")):
            fl = [w[:].rearrange("p m k n -> p (m k n)") for w in w2[a]]
            blocks += [(io[name][:, i * BLK:(i + 1) * BLK], P, BLK, [f[:, i * BLK:(i + 1) * BLK] for f in fl]) for i in range(2)]
        blocks += [(io["ctx_tok"][:, i * BLK:(i + 1) * BLK], P, BLK, [f[:].rearrange("p t n -> p (t n)")[:, i * BLK:(i + 1) * BLK] for f in ft]) for i in range(4)]
        with nc.Block() as block:
            @block.sync
            def _(sp):
                sp.dma_start(bias[:], io["bias2"]).then_inc(small, 16)
                sp.dma_start(same[:], io["same"]).then_inc(small, 16)
                block_loader(sp, blocks, raw, w_raw, w_low)
                load_ahead(sp, w_low, len(blocks), raw_of["F"], [(raw_small[0][:, 0:KC * 2 * LR_RANK], io["a_gu"]), (raw_small[1], io["q_gu"][0, 0].bitcast(F32))])

            @block.gpsimd
            def _(pool):
                for n, (_, rows, cols, dst) in enumerate(blocks):
                    split_block(pool, n, rows, cols, dst, raw, w_raw, w_high, w_low)

            @block.tensor
            def _(pe):
                ln_tensor(pe, 3)
                for n in range(16):
                    a, m, h = n // 8, n // 2 % 4, n % 2
                    if n % 4 == 0:
                        pe.wait_ge(w_low, n // 4 + 1)
                    if n < 2:
                        pe.wait_ge(ln_low, 3 * NT + NT // 2 * (h + 1))
                    if n >= 2:
                        pe.wait_ge(q_done, n - 1)
                    cols = slice(h * HALF, (h + 1) * HALF)
                    product(bankA[n % 2][:], [x for k in range(KC) for x in three([w[:, m, k, :] for w in w2[a]], [s[:, k, cols] for s in (xT, cT)[a]])]).then_inc(a_ready, 1)
                pe.wait_ge(q_done, 16)
                for t in range(NT):
                    tok = slice(t * P, (t + 1) * P)
                    done = product(bankA[t // 4][:, t % 4 * P:t % 4 * P + P], [(qk[0][:, m, tok], qk[1][:, m, tok]) for m in range(KC)])
                    if t % 4 == 3:
                        done.then_inc(s_ready, 1)
                for u in range(2):
                    pe.wait_ge(st["prob"], u + 1)
                    for j in range(4):
                        done = nc.tensor.transpose(bankT[u][:, j * P:(j + 1) * P], sc[u][:, j, :], ident[:])
                    done.then_inc(t_ready, 1)
                pe.wait_ge(w_low, 8)
                for t in range(NT):
                    pe.wait_ge(p_low, t // 4 + 1)
                    if t >= 2:
                        pe.wait_ge(y_done, t - 1)
                    product(bankY[t % 2][:], three([p[:, t, :] for p in pT], [f[:, t, :] for f in ft])).then_inc(y_ready, 1)

            @block.scalar
            def _(act):
                ln_high_parts(act, 3)
                act.wait_ge(small, 32)
                for n in range(16):
                    a, m, h = n // 8, n // 2 % 4, n % 2
                    act.wait_ge(a_ready, n + 1)
                    nc.scalar.activation(qk[a][:, m, h * HALF:(h + 1) * HALF], bankA[n % 2][:], ACT.Identity, bias=bias[:, a, m:m + 1]).then_inc(q_done, 1)
                for u in range(2):
                    act.wait_ge(st["sub"], u + 1)
                    fl = sc[u][:].rearrange("p t k -> p (t k)")
                    nc.scalar.activation(fl, fl, ACT.Exp, scale=D ** -0.5).then_inc(st["exp"], 1)
                for u in range(2):
                    act.wait_ge(t_ready, u + 1)
                    nc.scalar.activation(pT[0][:, 4 * u:4 * u + 4, :].rearrange("p t k -> p (t k)"), bankT[u][:], ACT.Copy).then_inc(p_high, 1)
                ln_roots(act, 4, 0)
                ln_rest(act, 4)

            @block.vector
            def _(dve):
                ln_low_parts(dve, 3)
                dve.wait_ge(small, 32)
                wide = lambda u: mx[:, u, :].unsqueeze(2).to_broadcast([P, 4, P])
                for u in range(2):
                    dve.wait_ge(s_ready, u + 1)
                    nc.vector.tensor_tensor(sc[u][:], bankA[u][:].rearrange("p (t k) -> p t k", t=4), same[:].unsqueeze(1).to_broadcast([P, 4, P]), ALU.min).then_inc(st["masked"], 1)
                    dve.wait_ge(st["masked"], u + 1)
                    nc.vector.tensor_reduce(mx[:, u, :], sc[u][:], AXX, ALU.max).then_inc(st["max"], 1)
                    dve.wait_ge(st["max"], u + 1)
                    nc.vector.tensor_tensor(sc[u][:], sc[u][:], wide(u), ALU.subtract).then_inc(st["sub"], 1)
                for u in range(2):
                    dve.wait_ge(st["exp"], u + 1)
                    nc.vector.tensor_reduce(mx[:, u, :], sc[u][:], AXX, ALU.add).then_inc(st["sum"], 1)
                    dve.wait_ge(st["sum"], u + 1)
                    nc.vector.reciprocal(mx[:, u, :], mx[:, u, :]).then_inc(st["inv"], 1)
                    dve.wait_ge(st["inv"], u + 1)
                    nc.vector.tensor_tensor(sc[u][:], sc[u][:], wide(u), ALU.mult).then_inc(st["prob"], 1)
                for u in range(2):
                    dve.wait_ge(p_high, u + 1)
                    part = [p[:, 4 * u:4 * u + 4, :].rearrange("p t k -> p (t k)") for p in pT]
                    nc.vector.tensor_tensor(part[1], bankT[u][:], f32(part[0]), ALU.subtract).then_inc(p_low, 1)
                for t in range(NT):
                    dve.wait_ge(y_ready, t + 1)
                    nc.vector.tensor_tensor(xtok[:, t, :], xtok[:, t, :], bankY[t % 2][:], ALU.add).then_inc(y_done, 1)
                    dve.wait_ge(y_done, t + 1)
                    ln_follow(dve, 4, t, early=1)
    cmem.close()

    ZERO, STEP, LR = 7.5, 0.005, 0.02
    w_raw = raw_of["F"]; w_high = sem("F_whigh"); w_low = sem("F_wlow")
    small = sem("F_small"); lr_ready = sem("F_lrready"); lr_high = sem("F_lrhigh"); lr_low = sem("F_lrlow")
    gu_ready = sem("F_guready"); scaled = sem("F_scaled"); g_sum = sem("F_gsum"); u_sum = sem("F_usum"); act_done = sem("F_act")
    h_done = sem("F_h"); h_high = sem("F_hhigh"); h_low = sem("F_hlow"); d_ready = sem("F_dready")
    y_ready = sem("F_yready"); y_scaled = sem("F_yscaled"); y_sum = sem("F_ysum"); y_done = sem("F_ydone")
    NU = NI * 2
    with ExitStack() as mem:
        wgu = [[sb(mem, f"Fwgu{i}{a}", [P, KC, P], F32R) for a in range(2)] for i in range(2)]
        wd = sb(mem, "Fwd", [P, NI, D], F32R)
        a_gu = [sb(mem, f"Fagu{i}", [P, KC, 2 * LR_RANK], F32R) for i in range(2)]
        b_gu = sb(mem, "Fbgu", [3 * LR_RANK, NI, 2, P], F32R)
        a_d = [sb(mem, f"Fad{i}", [P, NI, LR_RANK], F32R) for i in range(2)]
        b_d = sb(mem, "Fbd", [3 * LR_RANK, D], F32R)
        stack = [sb(mem, f"Fstack{i}", [3 * LR_RANK, TOK], F32R) for i in range(2)]
        hT = [sb(mem, f"FhT{i}", [P, NI, TOK], F32R) for i in range(2)]
        gs = [raw[1][:, i * HALF:(i + 1) * HALF] for i in range(2)]
        us = [sb(mem, f"Fus{i}", [P, HALF]) for i in range(2)]
        scale = sb(mem, "Fscale", [P, 2, NI]); dscale = sb(mem, "Fdscale", [P, D])
        bgu_flat = b_gu[:].rearrange("p i a n -> p (i a n)")
        blocks = [(io["a_gu"], P, KC * 2 * LR_RANK, "split", [w[:].rearrange("p k n -> p (k n)") for w in a_gu], None)]
        chunk_at = []
        for i in range(NI):
            for a in range(2):
                blocks.append((io["q_gu"][i, a].bitcast(F32), P, FB, "levels", wgu[i % 2][a][:].rearrange("p k n -> p (k n)"), i))
            if i % 2 == 0:
                cols = slice(i * 2 * P, min(i + 2, NI) * 2 * P)
                blocks.append((io["b_gu"][:, cols], 3 * LR_RANK, cols.stop - cols.start, "stack", bgu_flat[:, cols], None))
            chunk_at.append(len(blocks))
        first_d = len(blocks)
        blocks.append((io["a_d"], P, NI * LR_RANK, "split", [w[:].rearrange("p k n -> p (k n)") for w in a_d], None))
        blocks.append((io["b_d"], 3 * LR_RANK, D, "stack", b_d[:], None))
        blocks += [(io["q_d"][i].bitcast(F32), P, FB, "levels", wd[:, i, :], None) for i in range(NI)]
        sets = [(bankA[0][:], bankA[1][:], bankY[0][:], bankY[1][:]), (bankT[0][:], bankT[1][:], bankO[:, 0, :], bankO[:, 1, :])]
        with nc.Block() as block:
            @block.sync
            def _(sp):
                sp.dma_start(scale[:], io["gu_scale"]).then_inc(small, 16)
                sp.dma_start(dscale[:], io["d_scale"].to_broadcast([P, D])).then_inc(small, 16)
                block_loader(sp, blocks, raw_small, w_raw, w_low)
                store(sp, 5)

            @block.gpsimd
            def _(pool):
                for n, (_, rows, cols, kind, dst, i) in enumerate(blocks):
                    src = raw_small[n % 2][0:rows, 0:cols]
                    if kind == "split":
                        split_block(pool, n, rows, cols, dst, raw_small, w_raw, w_high, w_low)
                    elif kind == "stack":
                        low = slice(2 * LR_RANK, 3 * LR_RANK)
                        pool.wait_ge(w_raw[n % 2], 16 * (n // 2 + 1))
                        high_part(dst, src).then_inc(w_high, 1)
                        pool.wait_ge(w_high, n + 1)
                        nc.gpsimd.tensor_tensor(dst[low], src[low], f32(dst[low]), ALU.subtract).then_inc(w_low, 1)
                        pool.wait_ge(w_low, n + 1)
                    else:
                        if i is not None and i >= 2:
                            pool.wait_ge(gu_ready, 4 * (i - 1))
                        pool.wait_ge(w_raw[n % 2], 16 * (n // 2 + 1))
                        nc.gpsimd.tensor_scalar(dst, src.bitcast(I32), -ZERO, 1.0, ALU.add, ALU.mult).then_inc(w_low, 1)
                        pool.sem_inc(w_high, 1)

            @block.tensor
            def _(pe):
                ln_tensor(pe, 4)
                pe.wait_ge(w_low, 1)
                for h in range(2):
                    cols = slice(h * HALF, (h + 1) * HALF)
                    pe.wait_ge(ln_low, 4 * NT + NT // 2 * (h + 1))
                    product(bankO[0:2 * LR_RANK, h, :], [x for k in range(KC) for x in three([w[:, k, :] for w in a_gu], [s[:, k, cols] for s in xT])]).then_inc(lr_ready, 1)
                for n in range(NU):
                    i, h = n // 2, n % 2
                    cols = slice(h * HALF, (h + 1) * HALF)
                    if h == 0:
                        pe.wait_ge(w_low, chunk_at[i])
                    if n >= 2:
                        pe.wait_ge(g_sum, n - 1)
                        pe.wait_ge(u_sum, n - 1)
                    for a in range(2):
                        product(sets[h][a], [(wgu[i % 2][a][:, k, :], s[:, k, cols]) for k in range(KC) for s in xT])
                    if n < 2:
                        pe.wait_ge(lr_low, 2 * n + 2)
                    for a in range(2):
                        nc.tensor.matmul(sets[h][2 + a], b_gu[:, i, a, :], stack[a][:, cols], start=True, stop=True).then_inc(gu_ready, 1)
                pe.wait_ge(w_low, first_d + 1)
                for last in (False, True):
                    pe.wait_ge(h_low, NU if last else NU - 2)
                    if not last:
                        pe.wait_ge(g_sum, NU - 1)
                        pe.wait_ge(u_sum, NU - 1)
                    for h in range(2):
                        cols = slice(h * HALF, (h + 1) * HALF)
                        done = product(bankA[h][0:LR_RANK, :], [x for i in ([NI - 1] if last else range(NI - 1)) for x in three([w[:, i, :] for w in a_d], [s[:, i, cols] for s in hT])],
                                       start=not last, stop=last)
                        if last:
                            done.then_inc(d_ready, 1)
                pe.wait_ge(w_low, len(blocks))
                for t in range(NT):
                    tok = slice(t * P, (t + 1) * P)
                    if t >= 2:
                        pe.wait_ge(y_sum, t - 1)
                    product(bankY[t % 2][:], [(s[:, i, tok], wd[:, i, :]) for i in range(NI) for s in hT])
                    if t == 0:
                        pe.wait_ge(lr_low, 6)
                    nc.tensor.matmul(bankT[t % 2][:], stack[0][:, tok], b_d[:], start=True, stop=True).then_inc(y_ready, 1)

            R0, R1, R2 = (slice(LR_RANK * i, LR_RANK * (i + 1)) for i in range(3))

            @block.scalar
            def _(act):
                ln_high_parts(act, 4)
                act.wait_ge(small, 34)
                for h in range(2):
                    cols = slice(h * HALF, (h + 1) * HALF)
                    act.wait_ge(lr_ready, h + 1)
                    for dst, src in ((stack[0][R0, cols], R0), (stack[0][R2, cols], R0), (stack[1][R1, cols], R1), (stack[1][R2, cols], R1)):
                        nc.scalar.activation(dst, bankO[src, h, :], ACT.Copy, scale=LR).then_inc(lr_high, 1)
                for n in range(NU):
                    i, h = n // 2, n % 2
                    act.wait_ge(gu_ready, 2 * n + 1)
                    if n >= 2:
                        act.wait_ge(h_done, n - 1)
                    nc.scalar.activation(gs[h], sets[h][0], ACT.Copy, scale=scale[:, 0, i:i + 1]).then_inc(scaled, 1)
                    act.wait_ge(gu_ready, 2 * n + 2)
                    if n >= 2:
                        act.wait_ge(h_low, n - 1)
                    nc.scalar.activation(us[h][:], sets[h][3], ACT.Copy).then_inc(scaled, 1)
                    act.wait_ge(g_sum, n + 1)
                    nc.scalar.activation(gs[h], gs[h], ACT.Silu).then_inc(act_done, 1)
                    act.wait_ge(h_done, n + 1)
                    nc.scalar.activation(hT[0][:, i, h * HALF:(h + 1) * HALF], us[h][:], ACT.Copy).then_inc(h_high, 1)
                for h in range(2):
                    cols = slice(h * HALF, (h + 1) * HALF)
                    act.wait_ge(d_ready, h + 1)
                    for dst in (R0, R2):
                        nc.scalar.activation(stack[0][dst, cols], bankA[h][R0, :], ACT.Copy, scale=LR).then_inc(lr_high, 1)
                ln_roots(act, 5, 0)
                ln_rest(act, 5)

            @block.vector
            def _(dve):
                ln_low_parts(dve, 4)
                dve.wait_ge(small, 32)
                nc.vector.tensor_scalar(scale[:], scale[:], STEP, None, ALU.mult).then_inc(small, 1)
                nc.vector.tensor_scalar(dscale[:], dscale[:], STEP, None, ALU.mult).then_inc(small, 1)
                dve.wait_ge(small, 34)
                for h in range(2):
                    cols = slice(h * HALF, (h + 1) * HALF)
                    dve.wait_ge(lr_high, 4 * h + 4)
                    nc.vector.scalar_tensor_tensor(stack[0][R1, cols], bankO[R0, h, :], LR, f32(stack[0][R0, cols]), ALU.mult, ALU.subtract).then_inc(lr_low, 1)
                    nc.vector.scalar_tensor_tensor(stack[1][R0, cols], bankO[R1, h, :], LR, f32(stack[1][R1, cols]), ALU.mult, ALU.subtract).then_inc(lr_low, 1)
                for n in range(NU):
                    i, h = n // 2, n % 2
                    dve.wait_ge(scaled, 2 * n + 1)
                    nc.vector.tensor_tensor(gs[h], gs[h], sets[h][2], ALU.add).then_inc(g_sum, 1)
                    dve.wait_ge(scaled, 2 * n + 2)
                    nc.vector.scalar_tensor_tensor(us[h][:], sets[h][1], scale[:, 1, i:i + 1], us[h][:], ALU.mult, ALU.add).then_inc(u_sum, 1)
                    dve.wait_ge(u_sum, n + 1)
                    dve.wait_ge(act_done, n + 1)
                    nc.vector.tensor_tensor(us[h][:], us[h][:], gs[h], ALU.mult).then_inc(h_done, 1)
                    dve.wait_ge(h_high, n + 1)
                    cols = slice(h * HALF, (h + 1) * HALF)
                    nc.vector.tensor_tensor(hT[1][:, i, cols], us[h][:], f32(hT[0][:, i, cols]), ALU.subtract).then_inc(h_low, 1)
                for h in range(2):
                    cols = slice(h * HALF, (h + 1) * HALF)
                    dve.wait_ge(lr_high, 8 + 2 * h + 2)
                    nc.vector.scalar_tensor_tensor(stack[0][R1, cols], bankA[h][R0, :], LR, f32(stack[0][R0, cols]), ALU.mult, ALU.subtract).then_inc(lr_low, 1)
                for t in range(NT):
                    dve.wait_ge(y_ready, t + 1)
                    nc.vector.tensor_tensor(gs[t % 2], bankY[t % 2][:], dscale[:], ALU.mult).then_inc(y_scaled, 1)
                    dve.wait_ge(y_scaled, t + 1)
                    nc.vector.tensor_tensor(gs[t % 2], gs[t % 2], bankT[t % 2][:], ALU.add).then_inc(y_sum, 1)
                    dve.wait_ge(y_sum, t + 1)
                    nc.vector.tensor_tensor(xtok[:, t, :], xtok[:, t, :], gs[t % 2], ALU.add).then_inc(y_done, 1)
                    dve.wait_ge(y_done, t + 1)
                    ln_follow(dve, 5, t)
    ctx.close()


def layouts(i):
    def feat(w):
        return w.reshape(-1, P, w.shape[1]).transpose(1, 0, 2)

    a = {}
    a["x_tok"] = i["x"].reshape(NT, P, D).transpose(1, 0, 2)
    a["xT"] = feat(i["x"].reshape(TOK, D).T)
    a["ctxT"] = feat(i["ctx_4096"].reshape(TOK, D).T)
    a["ident"] = np.eye(P, dtype=np.float32)
    w, b = i["L0_attn_w_attn"], i["L0_attn_b_attn"]
    kq = np.stack([feat(w[:, D:2 * D]), feat(w[:, 0:D])], 1).reshape(P, 2, KC, KC, P)
    a["wqk"] = kq.transpose(3, 1, 0, 2, 4).reshape(KC, 2, P, D)
    a["wv"] = feat(w[:, 2 * D:]).reshape(P, KC * D)
    a["wp"] = feat(i["L0_attn_w_proj"]).reshape(P, KC * D)
    a["bqk"] = b[:2 * D].reshape(2, KC, P).transpose(2, 0, 1)
    a["bv"] = b[2 * D:].reshape(1, D)
    a["bp"] = i["L0_attn_b_proj"].reshape(1, D)
    base = 2 ** (-2 ** (-(math.log2(NH) - 3)))
    slopes = (base ** np.arange(1, NH + 1, dtype=np.float32)).astype(np.float32)
    rel = (np.arange(S)[None, :] - np.arange(S)[:, None])
    bias = np.where(rel[None] <= 0, slopes[:, None, None] * rel[None].astype(np.float32), np.float32(OFF)).astype(np.float32)
    a["alibi"] = np.concatenate([bias, bias], 2).reshape(NH // 2, 2 * S, 2 * S).transpose(1, 0, 2)
    even = (np.arange(P) % 32 < 16).astype(np.float32)
    a["parity"] = np.stack([even, 1 - even], 1)
    a["own"] = np.repeat(np.eye(P // A_HD, dtype=np.float32), A_HD, 0)

    def attention_blocks(wq, wk, wv, wo):
        heads = lambda w: w.reshape(KC, P, -1, HD).transpose(1, 2, 0, 3)
        q, k, o = heads(wq), heads(wk), wo.reshape(NH, HD, D).transpose(1, 0, 2)
        v = wv.reshape(KC, P, NPAIR, 2 * HD).transpose(1, 2, 0, 3)
        pair = lambda w, n: [w[:, n:n + 2], w[:, n + 2:n + 4]]
        blocks = [v[:, 0], k[:, 0:2]] + pair(q, 0)
        for it in range(NPAIR):
            h = 2 * it * GROUP
            blocks += pair(o, h) + pair(q, h + GROUP)
            if it + 1 < NPAIR:
                blocks += [k[:, 2 * it + 2:2 * it + 4], v[:, it + 1]]
            blocks += pair(o, h + GROUP)
            if it + 1 < NPAIR:
                blocks += pair(q, h + 2 * GROUP)
        return np.stack([x.reshape(P, BLK) for x in blocks])

    a["w_attn"] = np.concatenate([attention_blocks(*(i["L0_xattn_W" + c] for c in "qkvo")),
                                  attention_blocks(*(i["L1_attn_w" + c].T for c in "qkvo"))])
    a["pos"] = i["pos_BxS2"].reshape(NT, P).T
    m = i["mask_BxSxS2_ik0"].transpose(1, 0, 2)
    a["mask"] = np.concatenate([m, m]).reshape(P, NT, P)
    inv = (1.0 / np.float32(10000.0) ** (np.arange(0, HD, 2, dtype=np.float32) / HD)).astype(np.float32)
    angle = np.arange(ROPE_ROWS, dtype=np.float32)[:, None] * inv[None]
    cos, sin = np.cos(angle).astype(np.float32), np.sin(angle).astype(np.float32)
    a["rope"] = np.concatenate([cos, cos, -sin, sin], 1)

    far = np.float32(-OFF)
    a["earlier"] = np.broadcast_to(np.tril(np.ones((EXPERTS, EXPERTS), np.float32), -1), (P, EXPERTS, EXPERTS))
    a["causal"] = np.tile(np.where(np.tril(np.ones((S, S))) > 0, far, -far).astype(np.float32), (2, 2))
    a["same"] = np.where(np.kron(np.eye(2), np.ones((S, S))) > 0, far, -far).astype(np.float32)
    down = i["L0_ffn_lora_A"].transpose(1, 0, 2).reshape(D, EXPERTS * RANK)
    war = np.concatenate([down, i["L0_ffn_router_W"].T, np.zeros((D, 256 - EXPERTS * RANK - EXPERTS), np.float32)], 1)
    a["war"] = feat(war).reshape(P, BLK)
    a["wb"] = feat(i["L0_ffn_base_W"].T).reshape(P, KC * D)
    a["wup"] = i["L0_ffn_lora_B"].reshape(EXPERTS * RANK, D)
    for name in "qk":
        a["w" + name + "2"] = feat(i["L1_xattn_W" + name].T).reshape(P, KC, KC, P).transpose(0, 2, 1, 3).reshape(P, KC * D)
    a["ctx_tok"] = i["ctx_4096"].reshape(NT, P, D).transpose(1, 0, 2).reshape(P, NT * D)
    a["bias2"] = np.stack([i["L1_xattn_bq"], i["L1_xattn_bk"]]).reshape(2, KC, P).transpose(2, 0, 1)
    pad = NI * P - INNER
    grow = lambda w, axis: np.pad(w, [(0, pad if x == axis else 0) for x in range(w.ndim)])
    a["a_gu"] = feat(np.concatenate([i["L1_ffn_gate_A"], i["L1_ffn_up_A"]], 1)).reshape(P, KC * 2 * LR_RANK)
    bgu = np.stack([grow(i["L1_ffn_gate_B"], 1), grow(i["L1_ffn_up_B"], 1)], 1).reshape(LR_RANK, 2, NI, P).transpose(0, 2, 1, 3).reshape(LR_RANK, -1)
    a["b_gu"] = np.concatenate([bgu, bgu, bgu])
    q = np.stack([grow(i["L1_ffn_gate_q"], 0), grow(i["L1_ffn_up_q"], 0)])
    a["q_gu"] = q.reshape(2, NI, P, KC, P).transpose(1, 0, 4, 3, 2).reshape(NI, 2, P, KC * P)
    a["gu_scale"] = np.stack([grow(i["L1_ffn_gate_scale"], 0), grow(i["L1_ffn_up_scale"], 0)]).reshape(2, NI, P).transpose(2, 0, 1)
    a["a_d"] = grow(i["L1_ffn_down_A"], 0).reshape(NI, P, LR_RANK).transpose(1, 0, 2).reshape(P, NI * LR_RANK)
    a["b_d"] = np.concatenate([i["L1_ffn_down_B"]] * 3)
    a["q_d"] = grow(i["L1_ffn_down_q"], 1).T.reshape(NI, P, D)
    a["d_scale"] = i["L1_ffn_down_scale"].reshape(1, D)
    return {k: np.ascontiguousarray(v) for k, v in a.items()}


def kernel(**inputs):
    import concourse.bacc as _bacc
    from concourse.bass_utils import run_bass_kernel_spmd as _run

    nc = _bacc.Bacc("TRN2", target_bir_lowering=False, num_devices=1)
    arrays = layouts({k: np.asarray(v) for k, v in inputs.items()})
    io = {k: nc.dram_tensor("in_" + k, v.shape, mybir.dt.from_np(v.dtype), kind="ExternalInput").ap() for k, v in arrays.items()}
    io["out"] = nc.dram_tensor("out_dram", (P, NT, D), F32, kind="ExternalOutput").ap()
    build_program(nc, io)
    r = _run(nc, [{"in_" + k: v for k, v in arrays.items()}], core_ids=[0])
    return np.asarray(r.results[0]["out_dram"]).transpose(1, 0, 2).reshape(B, S, D)
```
